# Optimizing a Trainium2 kernel written in Bass

```python
import numpy as np
import jax
import jax.numpy as jnp

def _softmax(x, axis=-1):
    return jax.nn.softmax(x, axis=axis)

def _gelu(x):
    return jax.nn.gelu(x, approximate=True)

def _silu(x):
    return jax.nn.silu(x)

def _sigmoid(x):
    return jax.nn.sigmoid(x)

def _layernorm(x, axis=-1, eps=1e-05):
    m = jnp.mean(x, axis=axis, keepdims=True)
    v = jnp.var(x, axis=axis, keepdims=True)
    return (x - m) / jnp.sqrt(v + eps)

def _scatter_add(tgt, idx, src, axis=0):
    return tgt.at[idx].add(src)

def _segment_sum(src, seg, n):
    return jax.ops.segment_sum(src, seg, n)
kernel_name = 'mk_decoder_preln_d2_seqx_r4_d5b6ad'

def setup_inputs(seed: int=0):
    np.random.seed(seed)
    _w = jnp.asarray

    def _rec_inputs():
        import jax
        import jax.numpy as jnp
        _rk = jax.random.key(seed)
        x = -0.0002928 + 1 * jax.random.normal(jax.random.fold_in(_rk, 1), (4, 512, 256), jnp.float32)
        _lenS = 512 - jax.random.randint(jax.random.fold_in(_rk, 7), (4,), 0, max(1, 512 // 4) + 1, jnp.int32)
        _lenS2 = 1024 - jax.random.randint(jax.random.fold_in(_rk, 8), (4,), 0, max(1, 1024 // 4) + 1, jnp.int32)
        _ctx_512P = jax.random.normal(jax.random.fold_in(_rk, 11), (4, 16, 128), jnp.float32)
        _ctx_512c = jax.random.dirichlet(jax.random.fold_in(_rk, 511), 0.3 * jnp.ones((16,), jnp.float32), (4, 1024))
        _ctx_512t = jnp.einsum('bsk,bkd->bsd', _ctx_512c, _ctx_512P)
        _ctx_512t = _ctx_512t * jax.lax.rsqrt(jnp.mean(jnp.square(_ctx_512t)) + 1e-12) * 0.953939
        ctx_512 = 0.00222621 + 0.99962 * (_ctx_512t + 0.3 * jax.random.normal(jax.random.fold_in(_rk, 611), (4, 1024, 128), jnp.float32))
        return (x, ctx_512)
    x, ctx_512 = _rec_inputs()

    def _L0_attn_setup():
        import jax, jax.numpy as jnp
        import numpy as np
        NUM_LANDMARKS = 64
        key = jax.random.key(seed)
        ks = jax.random.split(key, 4)
        B, S, D = (4, 1024, 256)
        init = 0.02
        return {'hidden_states': jax.random.normal(ks[0], (B, S, D), dtype=jnp.float32), 'Wq': jax.random.normal(ks[1], (D, D), dtype=jnp.float32) * init, 'bq': jnp.zeros((D,), dtype=jnp.float32), 'Wk': jax.random.normal(ks[2], (D, D), dtype=jnp.float32) * init, 'bk': jnp.zeros((D,), dtype=jnp.float32), 'Wv': jax.random.normal(ks[3], (D, D), dtype=jnp.float32) * init, 'bv': jnp.zeros((D,), dtype=jnp.float32)}
    _L0_attn_all = _L0_attn_setup()
    _L0_attn_in = {k: v for k, v in _L0_attn_all.items() if k in ('Wq', 'bq', 'Wk', 'bk', 'Wv', 'bv')}
    del _L0_attn_all

    def _L0_xattn_setup():
        import jax, jax.numpy as jnp
        import numpy as np
        B, T, TC, C, CC, H = (2, 512, 128, 256, 128, 16)
        D = C // H

        def _heads(t):
            b, l, _ = t.shape
            return t.reshape(b, l, H, D).transpose(0, 2, 1, 3)
        key = jax.random.key(seed)
        ks = jax.random.split(key, 18)
        w = lambda k, i, o: jax.random.normal(k, (i, o), jnp.float32) / np.sqrt(i).astype(np.float32)
        return {'x': jax.random.normal(ks[0], (B, T, C), jnp.float32), 'cross_input': jax.random.normal(ks[1], (B, TC, CC), jnp.float32), 'Wk': w(ks[2], C, C), 'bk': jnp.zeros((C,), jnp.float32), 'Wq': w(ks[3], C, C), 'bq': jnp.zeros((C,), jnp.float32), 'Wv': w(ks[4], C, C), 'bv': jnp.zeros((C,), jnp.float32), 'Wck': w(ks[5], CC, C), 'bck': jnp.zeros((C,), jnp.float32), 'Wcq': w(ks[6], C, C), 'bcq': jnp.zeros((C,), jnp.float32), 'Wcv': w(ks[7], CC, C), 'bcv': jnp.zeros((C,), jnp.float32), 'Wp': w(ks[8], C, C), 'bp': jnp.zeros((C,), jnp.float32)}
    _L0_xattn_all = _L0_xattn_setup()
    _L0_xattn_in = {k: v for k, v in _L0_xattn_all.items() if k in ('Wk', 'bk', 'Wq', 'bq', 'Wv', 'bv', 'Wck', 'bck', 'Wcq', 'bcq', 'Wcv', 'bcv', 'Wp', 'bp')}
    del _L0_xattn_all

    def _L0_ffn_setup():
        import jax, jax.numpy as jnp
        import numpy as np
        BLOCK_SIZE = 32
        FP6_E2M3_MAX = 7.5

        def _build_fp6_e2m3_grid():
            vals = set()
            for bits in range(64):
                s = bits >> 5 & 1
                e = bits >> 3 & 3
                m = bits & 7
                v = m / 8.0 if e == 0 else (1.0 + m / 8.0) * 2.0 ** (e - 1)
                vals.add(-v if s else v)
            return np.array(sorted(vals), dtype=np.float32)
        _GRID = jnp.asarray(_build_fp6_e2m3_grid())

        def _nearest_on_grid(x, grid):
            idx = jnp.clip(jnp.searchsorted(grid, x), 0, grid.shape[0] - 1)
            idx_lo = jnp.maximum(idx - 1, 0)
            v_hi = grid[idx]
            v_lo = grid[idx_lo]
            return jnp.where(jnp.abs(x - v_lo) <= jnp.abs(x - v_hi), v_lo, v_hi)

        def _mx_quantize(t, eps=1e-30):
            rows, K = t.shape
            blocks = t.reshape(rows, K // BLOCK_SIZE, BLOCK_SIZE)
            scales = jnp.maximum(jnp.max(jnp.abs(blocks), axis=-1) / FP6_E2M3_MAX, eps)
            q = _nearest_on_grid(blocks / scales[..., None], _GRID)
            return (q, scales)
        key = jax.random.key(seed)
        k1, k2, k3 = jax.random.split(key, 3)
        x = jax.random.normal(k1, (8, 2048, 256), dtype=jnp.float32)
        weight = jax.random.normal(k2, (256, 256), dtype=jnp.float32) * 0.02
        bias = jax.random.normal(k3, (256,), dtype=jnp.float32) * 0.02
        return {'x': x, 'weight': weight, 'bias': bias}
    _L0_ffn_all = _L0_ffn_setup()
    _L0_ffn_in = {k: v for k, v in _L0_ffn_all.items() if k in ('weight', 'bias')}
    del _L0_ffn_all

    def _L1_attn_setup():
        import jax, jax.numpy as jnp
        import numpy as np
        B, T, C, H = (4, 256, 256, 16)
        D = C // H

        def _expmap0_split(u):
            mink = -u[..., :1] ** 2 + jnp.sum(u[..., 1:] ** 2, axis=-1, keepdims=True)
            nomin = jnp.sqrt(jnp.maximum(mink, 1e-08))
            time = jnp.cosh(nomin)
            space = jnp.sinh(nomin) * u[..., 1:] / nomin
            return (time, space)
        key = jax.random.key(seed)
        ks = jax.random.split(key, 6)
        s = 1.0 / np.sqrt(C)
        return {'x': jax.random.normal(ks[0], (B, T, C), jnp.float32), 'W_qkv': jax.random.normal(ks[1], (C, 3 * C), jnp.float32) * s, 'b_qkv': jnp.zeros((3 * C,), jnp.float32), 'W_out': jax.random.normal(ks[2], (C, C), jnp.float32) * s, 'b_out': jnp.zeros((C,), jnp.float32), 'w_sur': jax.random.normal(ks[3], (C,), jnp.float32) * s, 'b_sur': jnp.zeros((), jnp.float32), 'threshold': jnp.float32(0.5)}
    _L1_attn_all = _L1_attn_setup()
    _L1_attn_in = {k: v for k, v in _L1_attn_all.items() if k in ('W_qkv', 'b_qkv', 'W_out', 'b_out', 'w_sur', 'b_sur', 'threshold')}
    del _L1_attn_all

    def _L1_xattn_setup():
        import jax, jax.numpy as jnp
        import numpy as np
        H, D, C1, C2, S, M, B, W = (16, 32, 256, 128, 512, 128, 2, 4)

        def _ln(x, g, b):
            m = jnp.mean(x, -1, keepdims=True)
            v = jnp.var(x, -1, keepdims=True)
            return (x - m) * jax.lax.rsqrt(v + 1e-05) * g + b

        def _mha(x, y, wq, wk, wv, li1_w, li1_b, lnx_g, lnx_b, lny_g, lny_b, ln3_g, ln3_b, li2_w, li2_b, li3_w, li3_b, causal):
            xn = _ln(x, lnx_g, lnx_b)
            yn = _ln(y, lny_g, lny_b)
            q = jnp.einsum('bsc,hcd->bhsd', xn, wq)
            k = jnp.einsum('btc,hcd->bhtd', yn, wk)
            v = jnp.einsum('btc,hcd->bhtd', yn, wv)
            a = jax.nn.softmax(jnp.einsum('bhsd,bhtd->bhst', q, k) * D ** (-0.5), axis=-1)
            if causal:
                s, t = (a.shape[-2], a.shape[-1])
                mask = (jnp.arange(t)[None, :] > jnp.arange(s)[:, None]).astype(a.dtype)
                a = a * mask
            o = jnp.einsum('bhst,bhtd->bhsd', a, v)
            o = o.transpose(0, 2, 1, 3).reshape(x.shape[0], x.shape[1], H * D)
            x_out = x + o @ li1_w + li1_b
            h = jax.nn.gelu(_ln(x_out, ln3_g, ln3_b) @ li2_w + li2_b, approximate=False)
            return x_out + h @ li3_w + li3_b
        key = jax.random.key(seed)
        ks = iter(jax.random.split(key, 64))

        def w(shape, scale=0.02):
            return jax.random.normal(next(ks), shape, jnp.float32) * scale
        inp = {'xx': jax.random.normal(next(ks), (B, S, C1), jnp.float32), 'ee': jax.random.normal(next(ks), (B, M, C2), jnp.float32), 'ln1_g': jnp.ones(C1, jnp.float32), 'ln1_b': jnp.zeros(C1, jnp.float32), 'ln2_g': jnp.ones(C1, jnp.float32), 'ln2_b': jnp.zeros(C1, jnp.float32)}
        for pfx, cy in (('a1', C1), ('a2', C2)):
            inp[pfx + '_wq'] = w((H, C1, D))
            inp[pfx + '_wk'] = w((H, cy, D))
            inp[pfx + '_wv'] = w((H, cy, D))
            inp[pfx + '_li1_w'] = w((H * D, C1))
            inp[pfx + '_li1_b'] = jnp.zeros(C1, jnp.float32)
            inp[pfx + '_lnx_g'] = jnp.ones(C1, jnp.float32)
            inp[pfx + '_lnx_b'] = jnp.zeros(C1, jnp.float32)
            inp[pfx + '_lny_g'] = jnp.ones(cy, jnp.float32)
            inp[pfx + '_lny_b'] = jnp.zeros(cy, jnp.float32)
            inp[pfx + '_ln3_g'] = jnp.ones(C1, jnp.float32)
            inp[pfx + '_ln3_b'] = jnp.zeros(C1, jnp.float32)
            inp[pfx + '_li2_w'] = w((C1, C1 * W))
            inp[pfx + '_li2_b'] = jnp.zeros(C1 * W, jnp.float32)
            inp[pfx + '_li3_w'] = w((C1 * W, C1))
            inp[pfx + '_li3_b'] = jnp.zeros(C1, jnp.float32)
        inp['training'] = 0
        return inp
    _L1_xattn_all = _L1_xattn_setup()
    _L1_xattn_in = {k: v for k, v in _L1_xattn_all.items() if k in ('ln1_g', 'ln1_b', 'ln2_g', 'ln2_b', 'a1_wq', 'a1_wk', 'a1_wv', 'a1_li1_w', 'a1_li1_b', 'a1_lnx_g', 'a1_lnx_b', 'a1_lny_g', 'a1_lny_b', 'a1_ln3_g', 'a1_ln3_b', 'a1_li2_w', 'a1_li2_b', 'a1_li3_w', 'a1_li3_b', 'a2_wq', 'a2_wk', 'a2_wv', 'a2_li1_w', 'a2_li1_b', 'a2_lnx_g', 'a2_lnx_b', 'a2_lny_g', 'a2_lny_b', 'a2_ln3_g', 'a2_ln3_b', 'a2_li2_w', 'a2_li2_b', 'a2_li3_w', 'a2_li3_b')}
    del _L1_xattn_all

    def _L1_ffn_setup():
        import jax, jax.numpy as jnp
        import numpy as np
        N_EMBED = 256
        FFN_HIDDEN = 1024
        NUM_EXPERTS = 8
        TOP_K = 2
        key = jax.random.key(seed)
        ks = jax.random.split(key, 8)
        d, f, E = (N_EMBED, FFN_HIDDEN, NUM_EXPERTS)
        s_d = 1.0 / np.sqrt(d)
        s_f = 1.0 / np.sqrt(f)
        return {'x': jax.random.normal(ks[0], (2, 512, d), dtype=jnp.float32), 'Wg': jax.random.uniform(ks[1], (d, E), jnp.float32, -s_d, s_d), 'bg': jax.random.uniform(ks[2], (E,), jnp.float32, -s_d, s_d), 'W1': jax.random.uniform(ks[3], (E, d, f), jnp.float32, -s_d, s_d), 'b1': jax.random.uniform(ks[4], (E, f), jnp.float32, -s_d, s_d), 'W2': jax.random.uniform(ks[5], (E, f, d), jnp.float32, -s_f, s_f), 'b2': jax.random.uniform(ks[6], (E, d), jnp.float32, -s_f, s_f)}
    _L1_ffn_all = _L1_ffn_setup()
    _L1_ffn_in = {k: v for k, v in _L1_ffn_all.items() if k in ('Wg', 'bg', 'W1', 'b1', 'W2', 'b2')}
    del _L1_ffn_all
    return {'x': x, 'ctx_512': ctx_512, 'L0_attn_Wq': _L0_attn_in['Wq'], 'L0_attn_bq': _L0_attn_in['bq'], 'L0_attn_Wk': _L0_attn_in['Wk'], 'L0_attn_bk': _L0_attn_in['bk'], 'L0_attn_Wv': _L0_attn_in['Wv'], 'L0_attn_bv': _L0_attn_in['bv'], 'L0_xattn_Wk': _L0_xattn_in['Wk'], 'L0_xattn_bk': _L0_xattn_in['bk'], 'L0_xattn_Wq': _L0_xattn_in['Wq'], 'L0_xattn_bq': _L0_xattn_in['bq'], 'L0_xattn_Wv': _L0_xattn_in['Wv'], 'L0_xattn_bv': _L0_xattn_in['bv'], 'L0_xattn_Wck': _L0_xattn_in['Wck'], 'L0_xattn_bck': _L0_xattn_in['bck'], 'L0_xattn_Wcq': _L0_xattn_in['Wcq'], 'L0_xattn_bcq': _L0_xattn_in['bcq'], 'L0_xattn_Wcv': _L0_xattn_in['Wcv'], 'L0_xattn_bcv': _L0_xattn_in['bcv'], 'L0_xattn_Wp': _L0_xattn_in['Wp'], 'L0_xattn_bp': _L0_xattn_in['bp'], 'L0_ffn_weight': _L0_ffn_in['weight'], 'L0_ffn_bias': _L0_ffn_in['bias'], 'L1_attn_W_qkv': _L1_attn_in['W_qkv'], 'L1_attn_b_qkv': _L1_attn_in['b_qkv'], 'L1_attn_W_out': _L1_attn_in['W_out'], 'L1_attn_b_out': _L1_attn_in['b_out'], 'L1_attn_w_sur': _L1_attn_in['w_sur'], 'L1_attn_b_sur': _L1_attn_in['b_sur'], 'L1_attn_threshold': _L1_attn_in['threshold'], 'L1_xattn_ln1_g': _L1_xattn_in['ln1_g'], 'L1_xattn_ln1_b': _L1_xattn_in['ln1_b'], 'L1_xattn_ln2_g': _L1_xattn_in['ln2_g'], 'L1_xattn_ln2_b': _L1_xattn_in['ln2_b'], 'L1_xattn_a1_wq': _L1_xattn_in['a1_wq'], 'L1_xattn_a1_wk': _L1_xattn_in['a1_wk'], 'L1_xattn_a1_wv': _L1_xattn_in['a1_wv'], 'L1_xattn_a1_li1_w': _L1_xattn_in['a1_li1_w'], 'L1_xattn_a1_li1_b': _L1_xattn_in['a1_li1_b'], 'L1_xattn_a1_lnx_g': _L1_xattn_in['a1_lnx_g'], 'L1_xattn_a1_lnx_b': _L1_xattn_in['a1_lnx_b'], 'L1_xattn_a1_lny_g': _L1_xattn_in['a1_lny_g'], 'L1_xattn_a1_lny_b': _L1_xattn_in['a1_lny_b'], 'L1_xattn_a1_ln3_g': _L1_xattn_in['a1_ln3_g'], 'L1_xattn_a1_ln3_b': _L1_xattn_in['a1_ln3_b'], 'L1_xattn_a1_li2_w': _L1_xattn_in['a1_li2_w'], 'L1_xattn_a1_li2_b': _L1_xattn_in['a1_li2_b'], 'L1_xattn_a1_li3_w': _L1_xattn_in['a1_li3_w'], 'L1_xattn_a1_li3_b': _L1_xattn_in['a1_li3_b'], 'L1_xattn_a2_wq': _L1_xattn_in['a2_wq'], 'L1_xattn_a2_wk': _L1_xattn_in['a2_wk'], 'L1_xattn_a2_wv': _L1_xattn_in['a2_wv'], 'L1_xattn_a2_li1_w': _L1_xattn_in['a2_li1_w'], 'L1_xattn_a2_li1_b': _L1_xattn_in['a2_li1_b'], 'L1_xattn_a2_lnx_g': _L1_xattn_in['a2_lnx_g'], 'L1_xattn_a2_lnx_b': _L1_xattn_in['a2_lnx_b'], 'L1_xattn_a2_lny_g': _L1_xattn_in['a2_lny_g'], 'L1_xattn_a2_lny_b': _L1_xattn_in['a2_lny_b'], 'L1_xattn_a2_ln3_g': _L1_xattn_in['a2_ln3_g'], 'L1_xattn_a2_ln3_b': _L1_xattn_in['a2_ln3_b'], 'L1_xattn_a2_li2_w': _L1_xattn_in['a2_li2_w'], 'L1_xattn_a2_li2_b': _L1_xattn_in['a2_li2_b'], 'L1_xattn_a2_li3_w': _L1_xattn_in['a2_li3_w'], 'L1_xattn_a2_li3_b': _L1_xattn_in['a2_li3_b'], 'L1_ffn_Wg': _L1_ffn_in['Wg'], 'L1_ffn_bg': _L1_ffn_in['bg'], 'L1_ffn_W1': _L1_ffn_in['W1'], 'L1_ffn_b1': _L1_ffn_in['b1'], 'L1_ffn_W2': _L1_ffn_in['W2'], 'L1_ffn_b2': _L1_ffn_in['b2']}

def reference(x, ctx_512, L0_attn_Wq, L0_attn_bq, L0_attn_Wk, L0_attn_bk, L0_attn_Wv, L0_attn_bv, L0_xattn_Wk, L0_xattn_bk, L0_xattn_Wq, L0_xattn_bq, L0_xattn_Wv, L0_xattn_bv, L0_xattn_Wck, L0_xattn_bck, L0_xattn_Wcq, L0_xattn_bcq, L0_xattn_Wcv, L0_xattn_bcv, L0_xattn_Wp, L0_xattn_bp, L0_ffn_weight, L0_ffn_bias, L1_attn_W_qkv, L1_attn_b_qkv, L1_attn_W_out, L1_attn_b_out, L1_attn_w_sur, L1_attn_b_sur, L1_attn_threshold, L1_xattn_ln1_g, L1_xattn_ln1_b, L1_xattn_ln2_g, L1_xattn_ln2_b, L1_xattn_a1_wq, L1_xattn_a1_wk, L1_xattn_a1_wv, L1_xattn_a1_li1_w, L1_xattn_a1_li1_b, L1_xattn_a1_lnx_g, L1_xattn_a1_lnx_b, L1_xattn_a1_lny_g, L1_xattn_a1_lny_b, L1_xattn_a1_ln3_g, L1_xattn_a1_ln3_b, L1_xattn_a1_li2_w, L1_xattn_a1_li2_b, L1_xattn_a1_li3_w, L1_xattn_a1_li3_b, L1_xattn_a2_wq, L1_xattn_a2_wk, L1_xattn_a2_wv, L1_xattn_a2_li1_w, L1_xattn_a2_li1_b, L1_xattn_a2_lnx_g, L1_xattn_a2_lnx_b, L1_xattn_a2_lny_g, L1_xattn_a2_lny_b, L1_xattn_a2_ln3_g, L1_xattn_a2_ln3_b, L1_xattn_a2_li2_w, L1_xattn_a2_li2_b, L1_xattn_a2_li3_w, L1_xattn_a2_li3_b, L1_ffn_Wg, L1_ffn_bg, L1_ffn_W1, L1_ffn_b1, L1_ffn_W2, L1_ffn_b2):
    import jax
    import jax.numpy as jnp

    def _L0_attn_ref(hidden_states, Wq, bq, Wk, bk, Wv, bv):
        import jax, jax.numpy as jnp
        import numpy as np
        NUM_LANDMARKS = 64
        B, S, D = hidden_states.shape
        L = NUM_LANDMARKS
        q = hidden_states @ Wq + bq
        k = hidden_states @ Wk + bk
        v = hidden_states @ Wv + bv
        q = jax.nn.softmax(q, axis=-1)
        k = jax.nn.softmax(k, axis=-1)
        k_landmarks = k.reshape(B, L, S // L, D).mean(axis=2)
        kernel_1 = jnp.einsum('bqd,bkd->bqk', q, k_landmarks)
        kernel_2 = jnp.einsum('bkd,bld->bkl', k_landmarks, k)
        kernel_3 = k * v
        mid = jnp.einsum('bkl,bld->bkd', kernel_2, kernel_3)
        output = jnp.einsum('bqk,bkd->bqd', kernel_1, mid)
        return output

    def _L0_xattn_ref(x, cross_input, Wk, bk, Wq, bq, Wv, bv, Wck, bck, Wcq, bcq, Wcv, bcv, Wp, bp):
        import jax, jax.numpy as jnp
        import numpy as np
        B, T, TC, C, CC, H = (2, 512, 128, 256, 128, 16)
        D = C // H

        def _heads(t):
            b, l, _ = t.shape
            return t.reshape(b, l, H, D).transpose(0, 2, 1, 3)
        scale = np.float32(1.0 / np.sqrt(D))
        q = _heads(x @ Wq + bq)
        k = _heads(x @ Wk + bk)
        v = _heads(x @ Wv + bv)
        att = jnp.einsum('bhqd,bhkd->bhqk', q, k) * scale
        causal = jnp.tril(jnp.ones((T, T), bool))
        att = jnp.where(causal[None, None], att, -jnp.inf)
        y = jnp.einsum('bhqk,bhkd->bhqd', jax.nn.softmax(att, axis=-1), v)
        qc = _heads(x @ Wcq + bcq)
        kc = _heads(cross_input @ Wck + bck)
        vc = _heads(cross_input @ Wcv + bcv)
        attc = jnp.einsum('bhqd,bhkd->bhqk', qc, kc) * scale
        y = y + jnp.einsum('bhqk,bhkd->bhqd', jax.nn.softmax(attc, axis=-1), vc)
        y = y.transpose(0, 2, 1, 3).reshape(x.shape[0], T, C)
        return y @ Wp + bp

    def _L0_ffn_ref(x, weight, bias):
        import jax, jax.numpy as jnp
        import numpy as np
        BLOCK_SIZE = 32
        FP6_E2M3_MAX = 7.5

        def _build_fp6_e2m3_grid():
            vals = set()
            for bits in range(64):
                s = bits >> 5 & 1
                e = bits >> 3 & 3
                m = bits & 7
                v = m / 8.0 if e == 0 else (1.0 + m / 8.0) * 2.0 ** (e - 1)
                vals.add(-v if s else v)
            return np.array(sorted(vals), dtype=np.float32)
        _GRID = jnp.asarray(_build_fp6_e2m3_grid())

        def _nearest_on_grid(x, grid):
            idx = jnp.clip(jnp.searchsorted(grid, x), 0, grid.shape[0] - 1)
            idx_lo = jnp.maximum(idx - 1, 0)
            v_hi = grid[idx]
            v_lo = grid[idx_lo]
            return jnp.where(jnp.abs(x - v_lo) <= jnp.abs(x - v_hi), v_lo, v_hi)

        def _mx_quantize(t, eps=1e-30):
            rows, K = t.shape
            blocks = t.reshape(rows, K // BLOCK_SIZE, BLOCK_SIZE)
            scales = jnp.maximum(jnp.max(jnp.abs(blocks), axis=-1) / FP6_E2M3_MAX, eps)
            q = _nearest_on_grid(blocks / scales[..., None], _GRID)
            return (q, scales)
        batch_shape = x.shape[:-1]
        in_features = x.shape[-1]
        x2 = x.astype(jnp.float32).reshape(-1, in_features)
        w2 = weight.astype(jnp.float32)
        xq, xs = _mx_quantize(x2)
        wq, ws = _mx_quantize(w2)
        xd = (xq * xs[..., None]).reshape(x2.shape)
        wd = (wq * ws[..., None]).reshape(w2.shape)
        out = xd @ wd.T + bias
        return out.reshape(*batch_shape, -1)

    def _L1_attn_ref(x, W_qkv, b_qkv, W_out, b_out, w_sur, b_sur, threshold):
        import jax, jax.numpy as jnp
        import numpy as np
        B, T, C, H = (4, 256, 256, 16)
        D = C // H

        def _expmap0_split(u):
            mink = -u[..., :1] ** 2 + jnp.sum(u[..., 1:] ** 2, axis=-1, keepdims=True)
            nomin = jnp.sqrt(jnp.maximum(mink, 1e-08))
            time = jnp.cosh(nomin)
            space = jnp.sinh(nomin) * u[..., 1:] / nomin
            return (time, space)
        Bx, Tx, Cx = x.shape
        importance = jax.nn.sigmoid(jnp.einsum('btc,c->bt', x, w_sur) + b_sur)
        spikes = (importance > threshold).astype(x.dtype)
        spike_mask = spikes[:, None, :, None]
        qkv = x @ W_qkv + b_qkv
        qkv = qkv.reshape(Bx, Tx, 3, H, D).transpose(2, 0, 3, 1, 4)
        q, k, v = (qkv[0], qkv[1], qkv[2])
        tq, sq = _expmap0_split(q)
        tk, sk = _expmap0_split(k)
        neg_inner = jnp.einsum('bhie,bhje->bhij', tq, tk) - jnp.einsum('bhid,bhjd->bhij', sq, sk)
        dist = jnp.arccosh(jnp.maximum(neg_inner, 1.0 + 1e-07))
        scores = -dist ** 2 / np.sqrt(D)
        causal = jnp.tril(jnp.ones((Tx, Tx), dtype=bool))
        scores = jnp.where(causal[None, None], scores, -jnp.inf)
        attn = jax.nn.softmax(scores, axis=-1) * spike_mask
        y = jnp.einsum('bhij,bhjd->bhid', attn, v)
        y = y.transpose(0, 2, 1, 3).reshape(Bx, Tx, Cx)
        return y @ W_out + b_out

    def _L1_xattn_ref(xx, ee, ln1_g, ln1_b, ln2_g, ln2_b, a1_wq, a1_wk, a1_wv, a1_li1_w, a1_li1_b, a1_lnx_g, a1_lnx_b, a1_lny_g, a1_lny_b, a1_ln3_g, a1_ln3_b, a1_li2_w, a1_li2_b, a1_li3_w, a1_li3_b, a2_wq, a2_wk, a2_wv, a2_li1_w, a2_li1_b, a2_lnx_g, a2_lnx_b, a2_lny_g, a2_lny_b, a2_ln3_g, a2_ln3_b, a2_li2_w, a2_li2_b, a2_li3_w, a2_li3_b, training):
        import jax, jax.numpy as jnp
        import numpy as np
        H, D, C1, C2, S, M, B, W = (16, 32, 256, 128, 512, 128, 2, 4)

        def _ln(x, g, b):
            m = jnp.mean(x, -1, keepdims=True)
            v = jnp.var(x, -1, keepdims=True)
            return (x - m) * jax.lax.rsqrt(v + 1e-05) * g + b

        def _mha(x, y, wq, wk, wv, li1_w, li1_b, lnx_g, lnx_b, lny_g, lny_b, ln3_g, ln3_b, li2_w, li2_b, li3_w, li3_b, causal):
            xn = _ln(x, lnx_g, lnx_b)
            yn = _ln(y, lny_g, lny_b)
            q = jnp.einsum('bsc,hcd->bhsd', xn, wq)
            k = jnp.einsum('btc,hcd->bhtd', yn, wk)
            v = jnp.einsum('btc,hcd->bhtd', yn, wv)
            a = jax.nn.softmax(jnp.einsum('bhsd,bhtd->bhst', q, k) * D ** (-0.5), axis=-1)
            if causal:
                s, t = (a.shape[-2], a.shape[-1])
                mask = (jnp.arange(t)[None, :] > jnp.arange(s)[:, None]).astype(a.dtype)
                a = a * mask
            o = jnp.einsum('bhst,bhtd->bhsd', a, v)
            o = o.transpose(0, 2, 1, 3).reshape(x.shape[0], x.shape[1], H * D)
            x_out = x + o @ li1_w + li1_b
            h = jax.nn.gelu(_ln(x_out, ln3_g, ln3_b) @ li2_w + li2_b, approximate=False)
            return x_out + h @ li3_w + li3_b
        x = _ln(xx, ln1_g, ln1_b)
        x = x + _mha(x, x, a1_wq, a1_wk, a1_wv, a1_li1_w, a1_li1_b, a1_lnx_g, a1_lnx_b, a1_lny_g, a1_lny_b, a1_ln3_g, a1_ln3_b, a1_li2_w, a1_li2_b, a1_li3_w, a1_li3_b, causal=True)
        x = _ln(x, ln2_g, ln2_b)
        return x + _mha(x, ee, a2_wq, a2_wk, a2_wv, a2_li1_w, a2_li1_b, a2_lnx_g, a2_lnx_b, a2_lny_g, a2_lny_b, a2_ln3_g, a2_ln3_b, a2_li2_w, a2_li2_b, a2_li3_w, a2_li3_b, causal=False)

    def _L1_ffn_ref(x, Wg, bg, W1, b1, W2, b2):
        import jax, jax.numpy as jnp
        import numpy as np
        N_EMBED = 256
        FFN_HIDDEN = 1024
        NUM_EXPERTS = 8
        TOP_K = 2
        gate_scores = jax.nn.softmax(x @ Wg + bg, axis=-1)
        topk_scores, topk_idx = jax.lax.top_k(gate_scores, TOP_K)
        topk_scores = topk_scores / (jnp.sum(topk_scores, axis=-1, keepdims=True) + 1e-08)
        onehot = jax.nn.one_hot(topk_idx, NUM_EXPERTS, dtype=x.dtype)
        combine_w = jnp.einsum('bsk,bske->bse', topk_scores, onehot)
        output = jnp.zeros_like(x)
        for e in range(NUM_EXPERTS):
            h = jax.nn.gelu(x @ W1[e] + b1[e])
            y = h @ W2[e] + b2[e]
            output = output + y * combine_w[..., e:e + 1]
        return output
    x = x + _L0_attn_ref(_layernorm(x, axis=-1), L0_attn_Wq, L0_attn_bq, L0_attn_Wk, L0_attn_bk, L0_attn_Wv, L0_attn_bv)
    x = x + _L0_xattn_ref(_layernorm(x, axis=-1), ctx_512, L0_xattn_Wk, L0_xattn_bk, L0_xattn_Wq, L0_xattn_bq, L0_xattn_Wv, L0_xattn_bv, L0_xattn_Wck, L0_xattn_bck, L0_xattn_Wcq, L0_xattn_bcq, L0_xattn_Wcv, L0_xattn_bcv, L0_xattn_Wp, L0_xattn_bp)
    x = x + _L0_ffn_ref(_layernorm(x, axis=-1), L0_ffn_weight, L0_ffn_bias)
    x = x + _L1_attn_ref(_layernorm(x, axis=-1), L1_attn_W_qkv, L1_attn_b_qkv, L1_attn_W_out, L1_attn_b_out, L1_attn_w_sur, L1_attn_b_sur, L1_attn_threshold)
    x = x + _L1_xattn_ref(_layernorm(x, axis=-1), ctx_512, L1_xattn_ln1_g, L1_xattn_ln1_b, L1_xattn_ln2_g, L1_xattn_ln2_b, L1_xattn_a1_wq, L1_xattn_a1_wk, L1_xattn_a1_wv, L1_xattn_a1_li1_w, L1_xattn_a1_li1_b, L1_xattn_a1_lnx_g, L1_xattn_a1_lnx_b, L1_xattn_a1_lny_g, L1_xattn_a1_lny_b, L1_xattn_a1_ln3_g, L1_xattn_a1_ln3_b, L1_xattn_a1_li2_w, L1_xattn_a1_li2_b, L1_xattn_a1_li3_w, L1_xattn_a1_li3_b, L1_xattn_a2_wq, L1_xattn_a2_wk, L1_xattn_a2_wv, L1_xattn_a2_li1_w, L1_xattn_a2_li1_b, L1_xattn_a2_lnx_g, L1_xattn_a2_lnx_b, L1_xattn_a2_lny_g, L1_xattn_a2_lny_b, L1_xattn_a2_ln3_g, L1_xattn_a2_ln3_b, L1_xattn_a2_li2_w, L1_xattn_a2_li2_b, L1_xattn_a2_li3_w, L1_xattn_a2_li3_b, 0)
    x = x + _L1_ffn_ref(_layernorm(x, axis=-1), L1_ffn_Wg, L1_ffn_bg, L1_ffn_W1, L1_ffn_b1, L1_ffn_W2, L1_ffn_b2)
    return x

_drawn_inputs = setup_inputs


def setup_inputs(seed=0):
    import zlib

    import numpy as np

    out = dict(_drawn_inputs(seed))
    spreads = {'L0_attn_bq': (0.0, 2.0),
     'L0_attn_bk': (0.0, 0.8),
     'L0_attn_bv': (0.0, 2.0),
     'L0_xattn_bk': (0.0, 2.0),
     'L0_xattn_bq': (0.0, 0.1),
     'L0_xattn_bv': (0.0, 0.1),
     'L0_xattn_bck': (0.0, 2.0),
     'L0_xattn_bcq': (0.0, 0.1),
     'L0_xattn_bcv': (0.0, 0.1),
     'L0_xattn_bp': (0.0, 0.1),
     'L1_attn_b_qkv': (0.0, 0.1),
     'L1_attn_b_out': (0.0, 0.1),
     'L1_xattn_ln1_g': (1.0, 0.2),
     'L1_xattn_ln1_b': (0.0, 0.1),
     'L1_xattn_ln2_g': (1.0, 0.2),
     'L1_xattn_ln2_b': (0.0, 0.1),
     'L1_xattn_a1_li1_b': (0.0, 0.289),
     'L1_xattn_a1_lnx_g': (1.0, 0.6),
     'L1_xattn_a1_lnx_b': (0.0, 0.8),
     'L1_xattn_a1_lny_g': (1.0, 0.6),
     'L1_xattn_a1_lny_b': (0.0, 0.8),
     'L1_xattn_a1_ln3_g': (1.0, 0.6),
     'L1_xattn_a1_ln3_b': (0.0, 2.0),
     'L1_xattn_a1_li2_b': (0.0, 0.72),
     'L1_xattn_a1_li3_b': (0.0, 0.297),
     'L1_xattn_a2_li1_b': (0.0, 0.267),
     'L1_xattn_a2_lnx_g': (1.0, 0.6),
     'L1_xattn_a2_lnx_b': (0.0, 0.8),
     'L1_xattn_a2_lny_g': (1.0, 0.6),
     'L1_xattn_a2_lny_b': (0.0, 0.8),
     'L1_xattn_a2_ln3_g': (1.0, 0.6),
     'L1_xattn_a2_ln3_b': (0.0, 2.0),
     'L1_xattn_a2_li2_b': (0.0, 0.724),
     'L1_xattn_a2_li3_b': (0.0, 0.272)}
    factors = {'L0_attn_Wq': 47.654,
     'L0_attn_Wk': 8.0,
     'L0_attn_Wv': 8.0,
     'L1_xattn_a1_wq': 8.0,
     'L1_xattn_a1_wk': 8.0,
     'L1_xattn_a1_wv': 4.264,
     'L1_xattn_a1_li1_w': 4.083,
     'L1_xattn_a2_wq': 8.0,
     'L1_xattn_a2_wk': 8.0,
     'L1_xattn_a2_wv': 3.54,
     'L1_xattn_a2_li1_w': 3.398,
     'L1_ffn_bg': 7.128,
     'L1_ffn_b1': 21.779,
     'L1_ffn_b2': 8.0}
    for name, (base, spread) in spreads.items():
        noise = np.random.default_rng([zlib.crc32(name.encode()), seed]).standard_normal(out[name].shape)
        drawn = base * np.exp(spread * noise) if base else spread * noise
        out[name] = jnp.asarray(drawn.astype(out[name].dtype))
    for name, factor in factors.items():
        out[name] = (out[name] * factor).astype(out[name].dtype)
    return out
```

```python
from contextlib import ExitStack, contextmanager

import concourse.bass as bass
from concourse import mybir

F32 = mybir.dt.float32
BF16 = mybir.dt.bfloat16
U32 = mybir.dt.uint32
ALU = mybir.AluOpType
ACT = mybir.ActivationFunctionType
AX = mybir.AxisListType

P = 128
B, T, C = 4, 512, 256
TC, CC = 1024, 128
QT, KT, CT = T // P, C // P, TC // P
H, J = 16, 4
HG, W = H // J, 32
D16 = C // H
BANK = 512
EPS = 1e-5
BIG = 1e30
F = 4 * C
FT = F // P
NE = 8
GRID_MAX = 7.5
MAGIC = 12582912.0


def build(nc, dram, out):
    ctx = ExitStack()
    with ctx:
        ctx.enter_context(nc.allow_non_contiguous_dma(reason="bias vectors to columns, once"))
        psum = ctx.enter_context(nc.psum_tensor("psum", [P, 8, BANK], F32))
        x5 = nc.dram_tensor("x_after_layers", [B, P, QT, C], F32, kind="Internal").ap()
        ident = ctx.enter_context(nc.sbuf_tensor("ident", [P, P], F32))
        nhalf = ctx.enter_context(nc.sbuf_tensor("nhalf", [P, QT * QT], F32))
        with ExitStack() as layers:
            decoder_layers(nc, layers, dram, x5, psum, ident, nhalf)
        with ExitStack() as experts:
            mixture(nc, experts, dram, x5, out, psum, ident, nhalf)


class Shared:
    pass


@contextmanager
def stage(nc, tag, *names):
    with ExitStack() as s:
        sems = [s.enter_context(nc.semaphore(f"{tag}_{n}")) for n in names]
        with nc.Block() as block:
            yield (block, *sems)
        nums = sorted(x.num for x in sems)
        while nums:
            n = next((i for i, v in enumerate(nums) if v != nums[0] + i), len(nums))
            nc.all_engine_barrier(sems_to_clear=range(nums[0], nums[0] + n))
            nums = nums[n:]


def chained(eng, sem):
    count = [0]

    def then(ins):
        count[0] += 1
        ins.then_inc(sem, 1)
        eng.wait_ge(sem, count[0])
    return then


def norm_stats(nc, tag, src, stats, mv, rstd, eps_var, nhalf, n, sems):
    chain, var_ready, rstd_ready = sems

    def on_vector(dve, then):
        for t in range(n):
            last = dve.bn_stats(stats[:, t, :], src[:, t, :])
        then(last)
        for t in range(n):
            last = dve.bn_aggr(mv[:, t, :], stats[:, t, :])
        then(last)
        dve.tensor_scalar(eps_var[:, 0:n], mv[:, 0:n, 1], EPS, None, ALU.add).then_inc(var_ready, 1)
        dve.wait_ge(rstd_ready, 1)

    def on_pool(pool):
        pool.wait_ge(var_ready, 1)
        pool.tensor_tensor(rstd[:, 0:n], eps_var[:, 0:n], nhalf[:, 0:n], ALU.pow).then_inc(rstd_ready, 1)
    return on_vector, on_pool


def decoder_layers(nc, es, dram, x5, psum, ident, nhalf):
    def sb(name, shape, dt=F32):
        return es.enter_context(nc.sbuf_tensor(name, shape, dt))

    w_slot = sb("w_slot", [P, 6 * BANK])
    wA = w_slot[:, 0:KT * 3 * C].rearrange("p (k n) -> p k n", k=KT)
    w1q, w1k, w1v = (w_slot[:, i * 1024:(i + 1) * 1024].rearrange("p (k n) -> p k n", k=KT) for i in range(3))
    w2q = w1q
    w2k = w_slot[:, 1024:1536].rearrange("p (k n) -> p k n", k=1)
    w2v = w_slot[:, 1536:2048].rearrange("p (k n) -> p k n", k=1)
    bA = sb("bA", [P, 3 * C])
    wBq, wBk, wBcq = (sb(n, [P, KT, C]) for n in ("wBq", "wBk", "wBcq"))
    wBck = sb("wBck", [P, 1, C])
    wBv, wBcv = sb("wBv", [P, KT, H * W]), sb("wBcv", [P, 1, H * W])
    wBp = sb("wBp", [P, HG, C])
    colB = sb("colB", [P, 2, HG])
    wC = sb("wC", [P, KT, C])
    wD, bD, wDo = sb("wD", [P, KT, 3 * C]), sb("bD", [P, 3 * C]), sb("wDo", [P, HG, C])
    w_sur, scal = sb("w_sur", [P, C]), sb("scal", [P, 2])
    w_li1 = [sb(f"w_li1_{i}", [P, HG, C]) for i in (1, 2)]
    w_li2, w_li3 = sb("w_li2", [P, KT, F]), sb("w_li3", [P, FT, C])
    rows = sb("rows", [P, 15, C])
    R = {n: rows[:, i, :] for i, n in enumerate(
        ("L0_xattn_bp", "L0_ffn_bias", "L1_attn_b_out", "L1_xattn_ln1_g", "L1_xattn_ln1_b",
         "L1_xattn_ln2_g", "L1_xattn_ln2_b", "L1_xattn_a1_li1_b", "L1_xattn_a1_li3_b",
         "L1_xattn_a2_li1_b", "L1_xattn_a2_li3_b",
         "L0_xattn_bq", "L0_xattn_bk", "L0_xattn_bcq", "L0_xattn_bck"))}
    cols = sb("cols", [P, 40])
    Ccol, at = {}, 0
    for a in ("a1", "a2"):
        for n, k in (("lnx_g", 2), ("lnx_b", 2), ("lny_g", 2 if a == "a1" else 1),
                     ("lny_b", 2 if a == "a1" else 1), ("ln3_g", 2), ("ln3_b", 2), ("li2_b", 8)):
            Ccol[f"L1_xattn_{a}_{n}"] = cols[:, at:at + k]
            at += k
    identb = sb("identb", [P, P], BF16)
    ones_f = sb("ones_f", [P, W])
    avg = sb("avg", [P, 16])
    hide_above, hide_below = sb("hide_above", [P, P], BF16), sb("hide_below", [P, P], BF16)

    x, xh, xa, xo = (sb(n, [P, QT, C]) for n in ("x", "xh", "xa", "xo"))
    xT = sb("xT", [P, KT, T])
    cT, cnT = sb("cT", [P, 1, TC]), sb("cnT", [P, 1, TC])
    yT = sb("yT", [P, HG, T])
    stack = sb("stack", [P, 16384], BF16)
    vbig = sb("vbig", [P, CT * H * W])
    prob = sb("prob", [P, 4, 2, T])
    parts2 = sb("parts2", [P, 6144], BF16)
    ob, scr = sb("ob", [P, T]), sb("scr", [P, 2 * T])
    sm, rs = scr[:, 0:T], scr[:, T:2 * T]
    stats, mv = sb("stats", [P, CT, 6]), sb("mv", [P, CT, 2])
    eps_var, rstd = sb("eps_var", [P, CT]), sb("rstd", [P, CT])
    small = sb("small", [P, 32])

    NM = HG * QT * J
    mx = ob[:, 0:2 * NM].rearrange("p (h g t j) -> p h g t j", h=2, g=HG, t=QT)
    mm, m1, m2 = (ob[:, (2 + i) * NM:(3 + i) * NM] for i in range(3))
    mb = ob[:, 5 * NM:5 * NM + 3 * NM // 2].bitcast(BF16).rearrange("p (i m) -> p i m", i=3)
    yT2 = yT[:, KT:2 * KT, :]
    work = stack[:, :].bitcast(F32)
    hT = work[:, 0:FT * T].rearrange("p (f n) -> p f n", f=FT)
    V = vbig[:, 0:QT * H * W].rearrange("p (k n) -> p k n", k=QT)
    Vc = vbig[:, :].rearrange("p (k n) -> p k n", k=CT)
    probb = prob[:, :, :, :].rearrange("p a b n -> p (a b n)").bitcast(BF16)
    parts = [probb[:, 0:6144], parts2[:, :]]
    mpad = probb[:, 0:HG * QT * J * W].rearrange("p (m w) -> p m w", w=W)
    pm = xh[:, :, :].rearrange("p a (b n) -> p a b n", b=2)

    loads = es.enter_context(nc.semaphore("params_loaded"))
    slot_loaded = es.enter_context(nc.semaphore("slot_loaded"))
    mlp_loaded = es.enter_context(nc.semaphore("mlp_loaded"))

    def load_qkv(eng, i):
        if i == 0:
            for m, n in enumerate("qkv"):
                eng.dma_start(wA[:, :, m * C:(m + 1) * C],
                              dram[f"L0_attn_W{n}"].rearrange("(k p) n -> p k n", p=P)).then_inc(slot_loaded, 16)
            return
        for w, n in ((w1q, "wq"), (w1k, "wk"), (w1v, "wv")) if i == 1 else ((w2q, "wq"), (w2k, "wk"), (w2v, "wv")):
            s = dram[f"L1_xattn_a{i}_{n}"].rearrange("h (k p) d -> k p h d", p=P)
            for k in range(w.shape[1]):
                eng.dma_start(w[:, k, :].rearrange("p (h d) -> p h d", d=W), s[k]).then_inc(slot_loaded, 16)

    def spread(v):
        return v.partition_broadcast(P)

    with stage(nc, "clear", "cleared", "shaped", "dc") as (block, cleared, shaped, dc):
        padded = [wBv, wBcv, wBp, wDo]

        @block.vector
        def _(dve):
            for w in padded:
                dve.memset(w[:, :, :], 0.0)
            dve.memset(colB[:, :, :], 0.0)
            dve.memset(ones_f[:, :], 1.0)
            dve.memset(nhalf[:, :], -0.5)
            dve.memset(ident[:, :], 1.0).then_inc(cleared, 1)
            dve.memset(avg[:, :], float(H) / 128.0).then_inc(cleared, 1)
            dve.memset(prob[:, 0, 0, 0:P], BIG).then_inc(cleared, 1)
            dve.memset(prob[:, 0, 1, 0:P], -BIG).then_inc(cleared, 1)
            dve.wait_ge(shaped, 5)
            dve.tensor_copy(identb[:, :], ident[:, :])
            dve.tensor_copy(hide_below[:, :], prob[:, 0, 0, 0:P])
            dve.tensor_copy(hide_above[:, :], prob[:, 0, 1, 0:P])

        @block.gpsimd
        def _(pool):
            pool.wait_ge(cleared, 4)
            pool.affine_select(ident[:, :], ident[:, :], [[1, P]], ALU.is_equal, 0.0, base=0,
                               channel_multiplier=-1).then_inc(shaped, 1)
            pool.affine_select(avg[:, :], avg[:, :], [[-8, 16]], ALU.is_ge, 0.0, base=0,
                               channel_multiplier=1).then_inc(shaped, 1)
            pool.wait_ge(shaped, 2)
            pool.affine_select(avg[:, :], avg[:, :], [[8, 16]], ALU.is_ge, 0.0, base=7,
                               channel_multiplier=-1).then_inc(shaped, 1)
            for i in range(2):
                pool.affine_select(prob[:, 0, i, 0:P], prob[:, 0, i, 0:P], [[1, P]], ALU.is_gt, 0.0,
                                   base=0, channel_multiplier=-1).then_inc(shaped, 1)

    with stage(nc, "load", "unused") as (block, _u):
        n_loads = [0]

        def put(eng, dst, src):
            eng.dma_start(dst, src).then_inc(loads, 16)
            n_loads[0] += 1

        def load_first(eng):
            load_qkv(eng, 0)

        def pad_heads(eng, dst, src, kts):
            s = src.rearrange("(k p) (h d) -> k p h d", p=P, d=D16)
            d = dst.rearrange("p k (h w) -> p k h w", w=W)
            for k in range(kts):
                put(eng, d[:, k, :, 0:D16], s[k])

        def pad_rows(eng, dst, src):
            s = src.rearrange("(g j d) n -> j d g n", j=J, d=D16)
            for j in range(J):
                put(eng, dst[W * j:W * j + D16, :, :], s[j])

        @block.sync
        def _(sp):
            for i, n in enumerate("qkv"):
                put(sp, bA[:, i * C:(i + 1) * C], spread(dram[f"L0_attn_b{n}"]))
            for w, n in ((wBq, "Wq"), (wBk, "Wk"), (wBcq, "Wcq"), (wBck, "Wck")):
                put(sp, w[:, :, :], dram[f"L0_xattn_{n}"].rearrange("(k p) n -> p k n", p=P))
            pad_heads(sp, wBv, dram["L0_xattn_Wv"], KT)
            pad_rows(sp, wBp, dram["L0_xattn_Wp"])
            put(sp, bD[:, :], spread(dram["L1_attn_b_qkv"]))
            put(sp, wD[:, :, :], dram["L1_attn_W_qkv"].rearrange("(k p) n -> p k n", p=P))
            put(sp, w_sur[:, :], spread(dram["L1_attn_w_sur"]))
            put(sp, scal[:, 0:1], spread(dram["L1_attn_b_sur"]))
            put(sp, scal[:, 1:2], spread(dram["L1_attn_threshold"]))
            for n, dst in R.items():
                put(sp, dst, spread(dram[n]))

        @block.scalar
        def _(act):
            load_first(act)
            pad_heads(act, wBcv, dram["L0_xattn_Wcv"], 1)
            pad_rows(act, wDo, dram["L1_attn_W_out"])
            for i in (1, 2):
                put(act, w_li1[i - 1][:, :, :],
                    dram[f"L1_xattn_a{i}_li1_w"].rearrange("(g p) n -> p g n", p=P))

            for i, n in enumerate(("bv", "bcv")):
                s = dram[f"L0_xattn_{n}"].rearrange("(g j d) -> j d g", j=J, d=D16)
                for j in range(J):
                    put(act, colB[W * j:W * j + D16, i, :], s[j])
            for n, dst in Ccol.items():
                put(act, dst, dram[n].rearrange("(k p) -> p k", p=P))
            put(act, xa[:, 0:KT, :], dram["L0_ffn_weight"].rearrange("(k p) n -> p k n", p=P))
            act.wait_ge(loads, 16 * n_loads[0])

    def quantise(dve, then, src, n, a, b_, c_, amax, scale, rscale):
        nb = n * C // 32
        s3 = src.rearrange("p t (b e) -> p (t b) e", e=32)
        a3 = a.rearrange("p t (b e) -> p (t b) e", e=32)
        wide3 = [P, nb, 32]
        then(dve.tensor_reduce(amax, s3, AX.X, ALU.max, apply_absolute_value=True))
        then(dve.tensor_scalar(scale, amax, 1.0 / GRID_MAX, 1e-30, ALU.mult, ALU.max))
        then(dve.reciprocal(rscale, scale))
        then(dve.tensor_tensor(a3, s3, rscale.unsqueeze(2).to_broadcast(wide3), ALU.mult))
        then(dve.tensor_tensor(b_, a, a, ALU.mult))
        dve.tensor_scalar(c_, b_, 4.0, -4.0, ALU.is_ge, ALU.mult)
        then(dve.tensor_scalar(src, b_, 16.0, -2.0, ALU.is_ge, ALU.mult))
        then(dve.scalar_tensor_tensor(b_, c_, 8.0, src, ALU.add, ALU.add))
        then(dve.tensor_scalar(c_, c_, -1.0 / 32.0, 0.125, ALU.mult, ALU.add))
        then(dve.scalar_tensor_tensor(c_, src, -0.125, c_, ALU.mult, ALU.add))
        then(dve.tensor_tensor(a, a, b_, ALU.mult))
        then(dve.tensor_scalar(src, a, MAGIC, None, ALU.add))
        then(dve.tensor_scalar(src, src, MAGIC, None, ALU.subtract))
        then(dve.tensor_tensor(b_, src, a, ALU.subtract))
        then(dve.tensor_scalar(b_, b_, 0.5, None, ALU.is_ge))
        then(dve.tensor_tensor(src, src, b_, ALU.subtract))
        then(dve.tensor_tensor(src, src, c_, ALU.mult))
        then(dve.tensor_tensor(s3, s3, scale.unsqueeze(2).to_broadcast(wide3), ALU.mult))

    amax, scale, rscale = m1[:, 0:32], m2[:, 0:32], mm[:, 0:32]

    with stage(nc, "qw", "dc", "quant", "turned") as (block, dc, quant, turned):
        @block.vector
        def _(dve):
            then = chained(dve, dc)
            quantise(dve, then, xa[:, 0:KT, :], KT, xo[:, 0:KT, :], xh[:, 0:KT, :], x[:, 0:KT, :],
                     amax[:, 0:16], scale[:, 0:16], rscale[:, 0:16])
            dve.sem_inc(quant, 1)

        @block.tensor
        def _(pe):
            pe.wait_ge(quant, 1)
            for n in range(KT):
                for k in range(KT):
                    last = pe.transpose(psum[:, k, n * P:(n + 1) * P], xa[:, n, k * P:(k + 1) * P], ident[:, :])
            last.then_inc(turned, 1)

        @block.scalar
        def _(act):
            act.wait_ge(turned, 1)
            act.copy(wC[:, :, :], psum[:, 0:KT, 0:C])

    def norm(tag, src, dst=None, turns=(), gain=None, n=QT, width=C, also=None):
        kts = width // P
        names = ("dc", "ac", "var_ready", "rstd_ready", "normed", "turned", "raw_turned")
        with stage(nc, tag, *names) as (block, dc, ac, var_ready, rstd_ready, normed, turned, raw_turned):
            on_vector, on_pool = norm_stats(nc, tag, src, stats, mv, rstd, eps_var, nhalf, n,
                                            (dc, var_ready, rstd_ready))

            @block.gpsimd
            def _(pool):
                on_pool(pool)

            @block.vector
            def _(dve):
                then = chained(dve, dc)
                on_vector(dve, then)
                if also is not None:
                    dve.wait_ge(raw_turned, 1)
                for t in range(n):
                    ins = dve.tensor_scalar(dst[:, t, :], src[:, t, :], mv[:, t, 0:1], rstd[:, t:t + 1],
                                            ALU.subtract, ALU.mult)
                    if gain is None:
                        ins.then_inc(normed, 1)
                    else:
                        then(ins)
                        then(dve.tensor_tensor(dst[:, t, :], dst[:, t, :], gain[0], ALU.mult))
                        dve.tensor_tensor(dst[:, t, :], dst[:, t, :], gain[1], ALU.add).then_inc(normed, 1)

            def bank(t, k):
                i = t * kts + k if kts == 1 else k * n + t
                return psum[:, i // 4, (i % 4) * P:(i % 4 + 1) * P]

            def raw_bank(t):
                return psum[:, 4 + t // 4, (t % 4) * P:(t % 4 + 1) * P]

            if turns or also is not None:
                @block.tensor
                def _(pe):
                    if also is not None:
                        for t in range(n):
                            last = pe.transpose(raw_bank(t), src[:, t, :], ident[:, :])
                        last.then_inc(raw_turned, 1)
                    for t in range(n):
                        pe.wait_ge(normed, t + 1)
                        for k in range(kts):
                            last = pe.transpose(bank(t, k), dst[:, t, k * P:(k + 1) * P], ident[:, :])
                    last.then_inc(turned, 1)

                @block.scalar
                def _(act):
                    banks = n * kts // 4
                    if also is not None:
                        act.wait_ge(raw_turned, 1)
                        act.copy(also.rearrange("p k (a n) -> p (k a) n", n=BANK), psum[:, 4:4 + banks, :])
                    act.wait_ge(turned, 1)
                    per = banks // kts
                    for target, g, b_ in turns:
                        tv = target.rearrange("p k (a n) -> p k a n", n=BANK)
                        for k in range(kts):
                            src_ = psum[:, k * per:(k + 1) * per, :]
                            if g is None:
                                act.copy(tv[:, k], src_)
                            else:
                                act.activation(tv[:, k], src_, ACT.Identity, bias=b_[:, k:k + 1],
                                               scale=g[:, k:k + 1])

    def products(tag, jobs, before=None, start_wait=None, after_pe=None):
        on = {"act": [j for j in jobs if j[0] == "act"], "dve": [j for j in jobs if j[0] == "dve"]}
        place = {}
        for i, j in enumerate(jobs):
            place[i] = (j[0], sum(1 for k in jobs[:i + 1] if k[0] == j[0]))
        with stage(nc, tag, "summed", "act_free", "dve_free", "prepared", "pc") as (
                block, summed, act_free, dve_free, prepared, pc):
            free = {"act": act_free, "dve": dve_free}

            @block.tensor
            def _(pe):
                if start_wait is not None:
                    pe.wait_ge(*start_wait)
                for i, (_e, pairs, n, _f) in enumerate(jobs):
                    if i >= 8:
                        e, count = place[i - 8]
                        pe.wait_ge(free[e], count)
                    for k, (lhsT, rhs) in enumerate(pairs):
                        last = pe.matmul(psum[:, i % 8, 0:n], lhsT, rhs, start=(k == 0),
                                         stop=(k == len(pairs) - 1))
                    last.then_inc(summed, 1)

            def evacuate(eng, name):
                for i, (e, _p, n, f) in enumerate(jobs):
                    if e == name:
                        eng.wait_ge(summed, i + 1)
                        f(eng, psum[:, i % 8, 0:n]).then_inc(free[name], 1)

            @block.scalar
            def _(act):
                evacuate(act, "act")

            @block.vector
            def _(dve):
                if before is not None:
                    dve.wait_ge(prepared, 1)
                evacuate(dve, "dve")

            @block.gpsimd
            def _(pool):
                if before is not None:
                    before(pool, chained(pool, pc))
                    pool.sem_inc(prepared, 1)
            if after_pe is not None:
                @block.sync
                def _(sp):
                    sp.wait_ge(summed, len(jobs))
                    after_pe(sp)

    ORDER = {("q", 16): "hmlhmh", ("k", 16): "hhhmml",
             ("q", 32): "hmhlmh", ("k", 32): "hhmhml"}
    ROWS = 96

    def view(first, heads, tiles, n):
        return stack[:, first:first + heads * tiles * n].rearrange("p (h a n) -> p h a n", h=heads, a=tiles)

    def operands(tag, ops, jobs, wait=None, then_load=None):
        names = ("pad_ones", "pc", "projected", "biased", "high", "rest", "mid", "low", "parted",
                 "turned", "act_free", "dve_free", "summed", "act_out", "dve_out")
        n_ops = len(ops)
        fills = []
        last_fill = []
        for u, o in enumerate(ops):
            nh, nt, d = o["heads"], o["tiles"], o["d"]
            stg = parts[u % 2].rearrange("p (t h c) -> p t h c", t=nt, c=6 * d)[:, :, 0:nh, :] \
                if nt * nh * 6 * d == 6144 else \
                parts[u % 2][:, 0:nt * nh * 6 * d].rearrange("p (t h c) -> p t h c", t=nt, c=6 * d)
            o["stg"] = stg
            per = 8 // nt
            tiles = [(h, a) for h in range(nh) for a in range(d // 16)]
            for i in range(0, len(tiles), per):
                fills.append((u, stg, tiles[i:i + per], o))
            last_fill.append(len(fills))
        with stage(nc, tag, *names) as (block, pad_ones, pc, projected, biased, high, rest, mid, low, parted,
                                        turned, act_free, dve_free, summed, act_out, dve_out):
            def cols(o):
                return o["heads"] * o["d"]

            def bank(u):
                return psum[:, 2 * (u % 2):2 * (u % 2) + 2, :].rearrange("p a n -> p (a n)")

            def value(u):
                o = ops[u]
                if "value" in o:
                    return o["value"]
                return left(u) if o.get("bias") is not None else bank(u)[:, 0:o["tiles"] * cols(o)]

            def left(u):
                o = ops[u]
                if "value" in o:
                    return o["value"]
                buf = scr[:, :] if u % 2 == 0 else xo[:, :, :].rearrange("p t n -> p (t n)")
                return buf[:, 0:o["tiles"] * cols(o)]

            def slots(u, i, n=1):
                o = ops[u]
                d = o["d"]
                v = o["stg"].rearrange("p t h c -> p (t h) c")
                return v[:, :, i * d:(i + n) * d]

            def by_head(u, v):
                return v.rearrange("p (m d) -> p m d", d=ops[u]["d"])

            def at(u, part):
                o = ops[u]
                return [i for i, c in enumerate(ORDER[o["side"], o["d"]]) if c == part]

            def fill_target(f):
                u, stg, tiles, o = fills[f]
                nt, t0 = o["tiles"], o["first"]
                h, a = tiles[0]
                if o["d"] == 16:
                    return o["stack"][0:ROWS, h:h + len(tiles), 0, t0:t0 + nt * P]
                if len(tiles) == 1:
                    return o["stack"][0:ROWS, h, a, t0:t0 + nt * P]
                return o["stack"][0:ROWS, h, :, t0:t0 + nt * P]

            def fill_source(f):
                u, stg, tiles, o = fills[f]
                n = o["tiles"] * P
                v = psum[0:ROWS, 4 + f % 2, :].bitcast(BF16)[:, 0:len(tiles) * n]
                return v if len(tiles) == 1 else v.rearrange("p (a n) -> p a n", n=n)

            @block.tensor
            def _(pe):
                def project(u):
                    o = ops[u]
                    if "value" in o:
                        return
                    if u >= 2:
                        if ops[u - 2].get("bias") is None:
                            pe.wait_ge(rest, u - 1)
                        else:
                            pe.wait_ge(biased, u - 1)
                    w, c0, src = o["w"]
                    n = cols(o)
                    for t in range(o["tiles"]):
                        for k in range(w.shape[1]):
                            last = pe.matmul(bank(u)[:, t * n:(t + 1) * n],
                                             src[:, k, o["first"] + t * P:o["first"] + (t + 1) * P],
                                             w[:, k, c0:c0 + n], start=(k == 0), stop=(k == w.shape[1] - 1))
                    last.then_inc(projected, 1)

                if wait is not None:
                    pe.wait_ge(*wait)
                project(0)
                if n_ops > 1:
                    project(1)
                done = 0

                def some_jobs(upto):
                    nonlocal done
                    while done < min(upto, len(jobs)):
                        i = done
                        if i >= 2:
                            pe.wait_ge(act_out if i % 2 else dve_out, (i - 2) // 2 + 1)
                        _e, pairs, n, _f = jobs[i]
                        for k, (lhsT, rhs) in enumerate(pairs):
                            last = pe.matmul(psum[:, 6 + i % 2, 0:n], lhsT, rhs, start=(k == 0),
                                             stop=(k == len(pairs) - 1))
                        last.then_inc(summed, 1)
                        done += 1

                for u in range(n_ops):
                    some_jobs(-(-len(jobs) * (u + 1) // n_ops))
                    pe.wait_ge(parted, u + 1)
                    for f in range(last_fill[u - 1] if u else 0, last_fill[u]):
                        if f >= 2:
                            pe.wait_ge(act_free if f % 2 else dve_free, (f - 2) // 2 + 1)
                        _u, stg, tiles, o = fills[f]
                        nt, d = o["tiles"], o["d"]
                        out_ = psum[0:ROWS, 4 + f % 2, :].bitcast(BF16)
                        for i, (h, a) in enumerate(tiles):
                            for t in range(nt):
                                last = pe.transpose(out_[:, (i * nt + t) * P:(i * nt + t + 1) * P],
                                                    stg[:, t, h, a * ROWS:(a + 1) * ROWS], identb[:, :])
                        last.then_inc(turned, 1)
                    if u + 2 < n_ops:
                        project(u + 2)

            def evacuate_job(eng, i):
                eng.wait_ge(summed, i + 1)
                _e, _p, n, f = jobs[i]
                f(eng, psum[:, 6 + i % 2, 0:n]).then_inc(act_out if i % 2 else dve_out, 1)

            def evacuate_fill(eng, f):
                eng.wait_ge(turned, f + 1)
                if f % 2:
                    eng.copy(fill_target(f), fill_source(f)).then_inc(act_free, 1)
                else:
                    eng.tensor_copy(fill_target(f), fill_source(f)).then_inc(dve_free, 1)

            def share(u, odd):
                lo, hi = -(-len(jobs) * u // n_ops), -(-len(jobs) * (u + 1) // n_ops)
                return [i for i in range(lo, hi) if i % 2 == odd]

            def fills_of(u, odd):
                return [f for f in range(last_fill[u - 1] if u else 0, last_fill[u]) if f % 2 == odd]

            @block.scalar
            def _(act):
                def split(u):
                    o = ops[u]
                    if o.get("bias") is not None:
                        act.wait_ge(biased, u + 1)
                    elif "value" not in o:
                        act.wait_ge(projected, u + 1)
                    if u >= 2:
                        act.wait_ge(turned, last_fill[u - 2])
                    act.copy(slots(u, at(u, "h")[0]), by_head(u, value(u))).then_inc(high, 1)
                    act.wait_ge(rest, u + 1)
                    act.copy(slots(u, at(u, "m")[0]), by_head(u, left(u))).then_inc(mid, 1)

                split(0)
                for u in range(n_ops):
                    if u + 1 < n_ops:
                        split(u + 1)
                    for i in share(u, 1):
                        evacuate_job(act, i)
                    for f in fills_of(u, 1):
                        evacuate_fill(act, f)

            @block.vector
            def _(dve):
                def split(u):
                    o = ops[u]
                    if u >= 2:
                        dve.wait_ge(low, u - 1)
                    if o.get("bias") is not None:
                        dve.wait_ge(projected, u + 1)
                        n = cols(o)
                        v3 = bank(u)[:, 0:o["tiles"] * n].rearrange("p (t n) -> p t n", n=n)
                        dve.tensor_tensor(left(u).rearrange("p (t n) -> p t n", n=n), v3,
                                          o["bias"].unsqueeze(1).to_broadcast([P, o["tiles"], n]),
                                          ALU.add).then_inc(biased, 1)
                    else:
                        dve.sem_inc(biased, 1)
                    dve.wait_ge(high, u + 1)
                    dve.tensor_tensor(by_head(u, left(u)), by_head(u, value(u)), slots(u, at(u, "h")[0]),
                                      ALU.subtract).then_inc(rest, 1)
                    h = at(u, "h")
                    for i in h[1:]:
                        dve.tensor_copy(slots(u, i), slots(u, h[0]))
                    dve.wait_ge(mid, u + 1)
                    m = at(u, "m")
                    for i in m[1:]:
                        ins = dve.tensor_copy(slots(u, i), slots(u, m[0]))
                    ins.then_inc(pc, 1)
                    dve.wait_ge(pc, u + 1)
                    dve.wait_ge(low, u + 1)
                    dve.sem_inc(parted, 1)

                split(0)
                for u in range(n_ops):
                    if u + 1 < n_ops:
                        split(u + 1)
                    for i in share(u, 0):
                        evacuate_job(dve, i)
                    for f in fills_of(u, 0):
                        evacuate_fill(dve, f)

            @block.gpsimd
            def _(pool):
                for o in ops:
                    if o["side"] == "k":
                        t0, n = o["first"], o["tiles"] * P
                        a = o["d"] // 16 - 1
                        pool.memset(o["stack"][ROWS:P, :, a, t0:t0 + n], 1.0).then_inc(pad_ones, 1)
                pool.wait_ge(pad_ones, 1)
                for u in range(n_ops):
                    pool.wait_ge(mid, u + 1)
                    pool.tensor_tensor(slots(u, at(u, "l")[0]), by_head(u, left(u)), slots(u, at(u, "m")[0]),
                                       ALU.subtract).then_inc(low, 1)

    def values(dst, w, srcT, tiles):
        jobs = []
        kts = w.shape[1]
        for t in range(tiles):
            pairs = [(srcT[:, k, t * P:(t + 1) * P], w[:, k, :]) for k in range(kts)]

            def f(eng, bank, t=t):
                return eng.copy(dst[:, t, :], bank) if eng is nc.scalar else eng.tensor_copy(dst[:, t, :], bank)
            jobs.append(("act" if t % 2 else "dve", pairs, w.shape[2], f))
        return jobs

    def into_rows(dst, resid, lhs, w, n=C):
        jobs = []
        for t in range(QT):
            pairs = [(lhs[:, k, t * P:(t + 1) * P], w[:, k, :]) for k in range(w.shape[1])]

            def f(eng, bank, t=t):
                return eng.tensor_tensor(dst[:, t, :], bank, resid[:, t, :], ALU.add)
            jobs.append(("dve", pairs, n, f))
        return jobs

    def add_rows(dst, *parts):
        def before(pool, then):
            for part in parts:
                for t in range(QT):
                    p_ = part[:, t, :] if len(part.shape) == 3 else part
                    ins = pool.tensor_tensor(dst[:, t, :], dst[:, t, :], p_, ALU.add)
                then(ins)
        return before

    def row_maxima(tag, Q, K, n_keys, causal, op=ALU.max, dist=None):
        halves, hgs = n_keys // BANK, Q.shape[1] // J
        groups = [(g, t, h) for g in range(hgs) for t in range(QT) for h in range(halves)]
        hide = hide_above if op == ALU.max else hide_below
        nm, last_tile = hgs * QT * J, Q.shape[2] - 1
        with stage(nc, tag, "scored", "reduced", "dc", "padz", "split", "turned", "tiny", "tiny_back") as (
                block, scored, reduced, dc, padz, split, turned, tiny, tiny_back):
            @block.tensor
            def _(pe):
                for i, (g, t, h) in enumerate(groups):
                    n = (t + 1) * P if causal else BANK
                    base = (i % 2) * 4
                    if i >= 2:
                        pe.wait_ge(reduced, i - 1)
                    if causal:
                        for j in range(J):
                            pe.matmul(psum[:, base + j, t * P:(t + 1) * P], identb[:, :], hide[:, :],
                                      start=True, stop=False, skip_group_check=True)
                    for j in range(J):
                        hd = g * J + j
                        last = pe.matmul(psum[:, base + j, 0:n], Q[0:ROWS, hd, 0, t * P:(t + 1) * P],
                                         K[0:ROWS, hd, 0, h * BANK:h * BANK + n], start=not causal,
                                         stop=True, skip_group_check=True)
                    last.then_inc(scored, 1)
                pe.wait_ge(split, 1)
                for f in range(hgs * J // 2):
                    for i in range(2):
                        g, j = (2 * f + i) // J, (2 * f + i) % J
                        for t in range(QT):
                            last = pe.transpose(psum[ROWS:P, f, :].bitcast(BF16)[:, (i * QT + t) * P:(i * QT + t + 1) * P],
                                                mpad[:, (g * QT + t) * J + j, :], identb[:, :])
                    last.then_inc(turned, 1)

            @block.gpsimd
            def _(pool):
                pool.memset(mpad[:, 0:nm, :], 0.0).then_inc(padz, 1)

            def turn(eng, odd):
                for f in range(hgs * J // 2):
                    if f % 2 == odd:
                        eng.wait_ge(turned, f + 1)
                        src = psum[ROWS:P, f, :].bitcast(BF16).rearrange("p (a n) -> p a n", a=2)
                        dst = Q[ROWS:P, 2 * f:2 * f + 2, last_tile, :]
                        if odd:
                            eng.copy(dst, src)
                        else:
                            eng.tensor_copy(dst, src)

            @block.vector
            def _(dve):
                then = chained(dve, dc)
                for i, (g, t, h) in enumerate(groups):
                    n = (t + 1) * P if causal else BANK
                    base = (i % 2) * 4
                    dve.wait_ge(scored, i + 1)
                    dve.tensor_reduce(mx[:, h, g, t, :], psum[:, base:base + 4, 0:n], AX.X, op).then_inc(reduced, 1)
                dve.wait_ge(reduced, len(groups))
                m = mx[:, 0, 0:hgs, :, :].rearrange("p g t j -> p (g t j)")
                if halves == 2:
                    then(dve.tensor_tensor(mm[:, 0:nm], m, mx[:, 1, 0:hgs, :, :].rearrange("p g t j -> p (g t j)"), ALU.max))
                    m = mm[:, 0:nm]
                if dist is not None:
                    dist(dve, then, m, tiny, tiny_back)
                    m = mm[:, 0:nm]
                sign = -1.0 if dist is None else 1.0
                then(dve.tensor_copy(mb[:, 0, 0:nm], m))
                then(dve.tensor_tensor(m1[:, 0:nm], m, mb[:, 0, 0:nm], ALU.subtract))
                then(dve.tensor_copy(mb[:, 1, 0:nm], m1[:, 0:nm]))
                then(dve.tensor_tensor(m2[:, 0:nm], m1[:, 0:nm], mb[:, 1, 0:nm], ALU.subtract))
                then(dve.tensor_copy(mb[:, 2, 0:nm], m2[:, 0:nm]))
                dve.wait_ge(padz, 1)
                for i in range(3):
                    ins = dve.tensor_scalar(mpad[:, 0:nm, i], mb[:, i, 0:nm], sign, None, ALU.mult)
                ins.then_inc(split, 1)
                turn(dve, 0)

            @block.scalar
            def _(act):
                if dist is not None:
                    act.wait_ge(tiny, 1)
                    act.activation(m2[:, :], m2[:, :], ACT.Ln).then_inc(tiny_back, 1)
                    act.wait_ge(tiny_back, 1)
                    act.activation(m2[:, :], m2[:, :], ACT.Exp, scale=0.5).then_inc(tiny_back, 1)
                    act.wait_ge(tiny, 2)
                    act.activation(m1[:, :], m1[:, :], ACT.Ln, bias=1.0).then_inc(tiny_back, 1)
                turn(act, 1)

    def attend(tag, Q, K, vals, n_keys, scale, g0=0, causal=False, anti=False, add=None, loading=None):
        kts = n_keys // P
        hgs = Q.shape[1] // J
        order = list(range(kts))[::-1] if anti else list(range(kts))
        steps = [(g, k) for g in range(hgs) for k in order]
        tiles = Q.shape[2]
        with stage(nc, tag, "scored", "exped", "masked", "weighed", "bank_free", "dc") as (
                block, scored, exped, masked, weighed, bank_free, dc):
            def first_query(k):
                return k * P if causal else 0

            if loading is not None:
                @block.sync
                def _(sp):
                    loading(sp)

            @block.tensor
            def _(pe):
                def score(n):
                    g, k = steps[n]
                    q0 = first_query(k)
                    for p in range(2):
                        i = 2 * n + p
                        if i >= 3:
                            pe.wait_ge(exped, i - 2)
                        for jj in range(2):
                            hd = g * J + 2 * p + jj
                            for a in range(tiles):
                                r = P if a == tiles - 1 else ROWS
                                last = pe.matmul(psum[:, 2 * (i % 3) + jj, q0:T], K[0:r, hd, a, k * P:(k + 1) * P],
                                                 Q[0:r, hd, a, q0:T], start=(a == 0), stop=(a == tiles - 1))
                        last.then_inc(scored, 1)

                def weigh(n):
                    g, k = steps[n]
                    q0 = first_query(k)
                    first, final = k == order[0], k == order[-1]
                    pe.wait_ge(exped, 2 * n + 2)
                    if causal or anti:
                        pe.wait_ge(masked, 2 * n + 2)
                    if first and g:
                        pe.wait_ge(bank_free, g)
                    for j in range(J):
                        c = (g0 + g) * P + W * j
                        lhsT = vals[:, k, c:c + W]
                        slot = (2 * n + j // 2) % 4
                        o = psum[W * j:W * j + W, 6, :]
                        if anti:
                            if k:
                                pe.matmul(o[:, 0:k * P], lhsT, prob[:, slot, j % 2, 0:k * P],
                                          start=first, stop=False, skip_group_check=True)
                            pe.matmul(o[:, k * P:(k + 1) * P], lhsT, pm[:, slot, j % 2, :],
                                      start=False, stop=final, skip_group_check=True)
                        else:
                            pe.matmul(o[:, q0:T], lhsT, prob[:, slot, j % 2, q0:T],
                                      start=first, stop=final, skip_group_check=True)
                    for j in range(J):
                        last = pe.matmul(psum[W * j:W * j + W, 7, q0:T], ones_f[:, :],
                                         prob[:, (2 * n + j // 2) % 4, j % 2, q0:T],
                                         start=first, stop=final, skip_group_check=True)
                    last.then_inc(weighed, 1)

                score(0)
                for n in range(len(steps)):
                    if n + 1 < len(steps):
                        score(n + 1)
                    weigh(n)

            @block.scalar
            def _(act):
                for n, (g, k) in enumerate(steps):
                    q0 = first_query(k)
                    for p in range(2):
                        i = 2 * n + p
                        act.wait_ge(scored, i + 1)
                        if n >= 2:
                            act.wait_ge(weighed, n - 1)
                        b0 = 2 * (i % 3)
                        act.activation(prob[:, i % 4, :, q0:T], psum[:, b0:b0 + 2, q0:T], ACT.Exp,
                                       scale=scale).then_inc(exped, 1)

            @block.gpsimd
            def _(pool):
                if causal or anti:
                    for n, (g, k) in enumerate(steps):
                        for p in range(2):
                            i = 2 * n + p
                            pool.wait_ge(exped, i + 1)
                            if anti and n >= 2:
                                pool.wait_ge(weighed, n - 1)
                            d = prob[:, i % 4, :, k * P:(k + 1) * P]
                            if causal:
                                pool.affine_select(d, d, [[0, 2], [1, P]], ALU.is_ge, 0.0, base=0,
                                                   channel_multiplier=-1).then_inc(masked, 1)
                            else:
                                pool.affine_select(pm[:, i % 4, :, :], d, [[0, 2], [-1, P]], ALU.is_gt, 0.0,
                                                   base=0, channel_multiplier=1).then_inc(masked, 1)

            @block.vector
            def _(dve):
                normalise(dve, chained(dve, dc), weighed, bank_free, kts, add, hgs, g0)

    def normalise(dve, then, weighed, bank_free, per_group, add, hgs=HG, g0=0):
        for g in range(hgs):
            dve.wait_ge(weighed, per_group * (g + 1))
            dve.tensor_copy(ob[:, :], psum[:, 6, :])
            ins = dve.tensor_copy(sm[:, :], psum[:, 7, :])
            ins.then_inc(bank_free, 1)
            dve.wait_ge(bank_free, g + 1)
            then(dve.reciprocal(rs[:, :], sm[:, :]))
            if add is None:
                then(dve.tensor_tensor(yT[:, g0 + g, :], ob[:, :], rs[:, :], ALU.mult))
            else:
                then(dve.tensor_tensor(ob[:, :], ob[:, :], rs[:, :], ALU.mult))
                then(dve.scalar_tensor_tensor(yT[:, g0 + g, :], ob[:, :], add[:, g0 + g:g0 + g + 1],
                                              yT[:, g0 + g, :], ALU.add, ALU.add))

    e = Shared()
    e.Ccol, e.R, e.ROWS, e.V, e.Vc, e.add_rows, e.amax = \
        Ccol, R, ROWS, V, Vc, add_rows, amax
    e.attend, e.avg, e.bA, e.bD, e.cT, e.cnT, e.colB = \
        attend, avg, bA, bD, cT, cnT, colB
    e.dram, e.hT, e.ident, e.into_rows, e.load_qkv, e.m1, e.m2 = \
        dram, hT, ident, into_rows, load_qkv, m1, m2
    e.mlp_loaded, e.mm, e.nc, e.norm, e.ob, e.ones_f, e.operands = \
        mlp_loaded, mm, nc, norm, ob, ones_f, operands
    e.parts2, e.prob, e.products, e.psum,  e.quantise, e.row_maxima = \
        parts2, prob, products, psum, quantise, row_maxima
    e.rs, e.rscale, e.scal, e.scale, e.slot_loaded, e.sm, e.small = \
        rs, rscale, scal, scale, slot_loaded, sm, small
    e.values, e.vbig, e.view, e.w1k, e.w1q, e.w1v, e.w2k = \
        values, vbig, view, w1k, w1q, w1v, w2k
    e.w2q, e.w2v, e.wA, e.wBck, e.wBcq, e.wBcv, e.wBk = \
        w2q, w2v, wA, wBck, wBcq, wBcv, wBk
    e.wBp, e.wBq, e.wBv, e.wC, e.wD, e.wDo, e.w_li1 = \
        wBp, wBq, wBv, wC, wD, wDo, w_li1
    e.w_li2, e.w_li3, e.w_sur, e.work, e.x, e.x5, e.xT = \
        w_li2, w_li3, w_sur, work, x, x5, xT
    e.xa, e.xh, e.xo, e.yT, e.yT2 = \
        xa, xh, xo, yT, yT2
    with nc.Fori(0, B) as b:
        batch(e, b)
    with stage(nc, "after", "unused") as (block, _u):
        @block.sync
        def _(sp):
            sp.wait_ge(slot_loaded, 48)


def batch(e, b):
    nc, dram, psum, R, Ccol, ident = e.nc, e.dram, e.psum, e.R, e.Ccol, e.ident
    x, xh, xa, xo, xT, yT2, yT = e.x, e.xh, e.xa, e.xo, e.xT, e.yT2, e.yT
    one = bass.ds(b, 1)
    context = e.prob[:, 0, :, :].rearrange("p a (t n) -> p (a t) n", n=CC)
    cn = e.prob[:, 1, :, :].rearrange("p a (t n) -> p (a t) n", n=CC)

    with stage(nc, "in", "rows_in") as (block, rows_in):
        @block.sync
        def _(sp):
            sp.dma_start(x[:, :, :], dram["x"][one].rearrange("o (t p) c -> p (o t) c", p=P)).then_inc(rows_in, 16)
            sp.dma_start(context[:, :, :], dram["ctx_512"][one].rearrange("o (t p) c -> p (o t) c", p=P)).then_inc(rows_in, 16)
            sp.wait_ge(rows_in, 32)

        @block.scalar
        def _(act):
            load_mlp(e, act, 1)

    a2 = "L1_xattn_a2_"
    e.norm("nctx", context, cn, turns=[(e.cnT, Ccol[a2 + "lny_g"], Ccol[a2 + "lny_b"])], n=CT, width=CC,
           also=e.cT)

    landmark_attention(e)
    standard_attention(e)
    fp6_linear(e)
    hyperbolic_attention(e)

    e.norm("n5", x, xh)
    e.norm("n6", xh, xa, gain=(R["L1_xattn_ln1_g"], R["L1_xattn_ln1_b"]))
    a1 = "L1_xattn_a1_"
    e.norm("n7", xa, xh, turns=[(xT, Ccol[a1 + "lnx_g"], Ccol[a1 + "lnx_b"]),
                                (yT2, Ccol[a1 + "lny_g"], Ccol[a1 + "lny_b"])])
    for c in range(2):
        Q, K = e.view(0, 8, 2, T), e.view(8192, 8, 2, T)
        e.operands(f"e1p{c}", [
            {"side": "q", "d": W, "heads": 8, "tiles": QT, "w": (e.w1q, 256 * c, xT), "stack": Q, "first": 0},
            {"side": "k", "d": W, "heads": 8, "tiles": QT, "w": (e.w1k, 256 * c, yT2), "stack": K, "first": 0}],
            e.values(e.V, e.w1v, yT2, QT) if c == 0 else [], wait=(e.slot_loaded, 96) if c == 0 else None)
        if c == 0:
            clear(nc, e.slot_loaded)
        e.row_maxima(f"e1m{c}", Q, K, T, False)
        e.attend(f"e1a{c}", Q, K, e.V, T, W ** -0.5, g0=2 * c, anti=True,
                 loading=(lambda sp: e.load_qkv(sp, 2)) if c == 1 else None)
    mlp_unit(e, 1, xa)
    e.norm("n9", xa, xa, gain=(R["L1_xattn_ln2_g"], R["L1_xattn_ln2_b"]))
    e.norm("n10", xa, xh, turns=[(xT, Ccol[a2 + "lnx_g"], Ccol[a2 + "lnx_b"])])
    for c in range(4):
        Q, K = e.view(0, 4, 2, T), e.view(4096, 4, 2, TC)
        e.operands(f"e2p{c}", [
            {"side": "q", "d": W, "heads": 4, "tiles": QT, "w": (e.w2q, P * c, xT), "stack": Q, "first": 0},
            {"side": "k", "d": W, "heads": 4, "tiles": CT, "w": (e.w2k, P * c, e.cnT), "stack": K, "first": 0}],
            e.values(e.Vc, e.w2v, e.cnT, CT) if c == 0 else [], wait=(e.slot_loaded, 64) if c == 0 else None)
        if c == 0:
            clear(nc, e.slot_loaded)
        e.row_maxima(f"e2m{c}", Q, K, TC, False)
        e.attend(f"e2a{c}", Q, K, e.Vc, TC, W ** -0.5, g0=c,
                 loading=(lambda sp: e.load_qkv(sp, 0)) if c == 3 else None)
    mlp_unit(e, 2, x)

    with stage(nc, "out", "stored") as (block, stored):
        @block.sync
        def _(sp):
            sp.dma_start(e.x5[one].rearrange("o p t c -> p (o t) c"), x[:, :, :]).then_inc(stored, 16)
            sp.wait_ge(stored, 16)


def clear(nc, sem):
    nc.all_engine_barrier(sems_to_clear=range(sem.num, sem.num + 1))


def load_mlp(e, eng, i):
    eng.dma_start(e.w_li2[:, :, :], e.dram[f"L1_xattn_a{i}_li2_w"].rearrange("(k p) n -> p k n", p=P)).then_inc(e.mlp_loaded, 16)
    eng.dma_start(e.w_li3[:, :, :], e.dram[f"L1_xattn_a{i}_li3_w"].rearrange("(k p) n -> p k n", p=P)).then_inc(e.mlp_loaded, 16)


def mlp_unit(e, i, target):
    nc, Ccol, R = e.nc, e.Ccol, e.R
    a = f"L1_xattn_a{i}_"
    w_li1, xo, xa, xT = e.w_li1[i - 1], e.xo, e.xa, e.xT

    def copy_first(pool, then):
        for t in range(QT):
            ins = pool.tensor_tensor(xo[:, t, :], xa[:, t, :], R[a + "li1_b"], ALU.add)
        then(ins)
    e.products(f"u{i}o", e.into_rows(xo, xo, e.yT, w_li1), before=copy_first)
    e.norm(f"u{i}n", xo, e.xh, turns=[(xT, Ccol[a + "ln3_g"], Ccol[a + "ln3_b"])])
    jobs = []
    for f in range(FT):
        pairs = [(e.w_li2[:, k, f * P:(f + 1) * P], xT[:, k, :]) for k in range(KT)]

        def gelu(eng, bank, f=f):
            return eng.activation(e.hT[:, f, :], bank, ACT.Gelu, bias=Ccol[a + "li2_b"][:, f:f + 1])
        jobs.append(("act", pairs, T, gelu))
    e.products(f"u{i}h", jobs, start_wait=(e.mlp_loaded, 32))
    clear(nc, e.mlp_loaded)
    parts = [xa, R[a + "li3_b"]] + ([e.x] if target is e.x else [])
    e.products(f"u{i}y", e.into_rows(target, xo, e.hT, e.w_li3), before=e.add_rows(xo, *parts),
               after_pe=(lambda sp: load_mlp(e, sp, 2)) if i == 1 else None)


def landmark_attention(e):
    nc, psum, x, ident = e.nc, e.psum, e.x, e.ident
    L = 64
    qkv = e.vbig[:, 0:QT * 3 * C].rearrange("p (t n) -> p t n", t=QT)
    k3 = e.yT[:, 0:2, :].rearrange("p a (t n) -> p (a t) n", n=C)
    qkT = e.work[:, 0:4 * T].rearrange("p (a n) -> p a n", a=4)
    qAT, kAT = qkT[:, 0:KT, :], qkT[:, KT:2 * KT, :]
    klT = e.work[:, 2048:2048 + KT * L].rearrange("p (k n) -> p k n", k=KT)
    k2T = e.work[:, 2304:2304 + QT * L].rearrange("p (t n) -> p t n", t=QT)
    mid = e.work[0:L, 2560:2560 + C]
    k1T = e.work[0:L, 3072:3072 + T]
    mxq, sums = e.small[:, 0:8], e.small[:, 8:16]

    e.norm("n1", x, e.xh, turns=[(e.xT, None, None)])
    jobs = []
    for t in range(QT):
        for n0, n in ((0, 2 * C), (2 * C, C)):
            pairs = [(e.xT[:, k, t * P:(t + 1) * P], e.wA[:, k, n0:n0 + n]) for k in range(KT)]

            def f(eng, bank, t=t, n0=n0, n=n):
                return eng.tensor_tensor(qkv[:, t, n0:n0 + n], bank, e.bA[:, n0:n0 + n], ALU.add)
            jobs.append(("dve", pairs, n, f))

    e.products("Ap", jobs, start_wait=(e.slot_loaded, 48))
    clear(nc, e.slot_loaded)

    with stage(nc, "Asm", "maxed", "exped", "dc", "soft", "turned", "copied", "lm", "lm_in", "k2",
               "k2_in", "k1_in", "md", "md_in", "fin") as (
            block, maxed, exped, dc, soft, turned, copied, lm, lm_in, k2, k2_in, k1_in, md, md_in, fin):
        def half(t, i):
            return qkv[:, t, i * C:(i + 1) * C]

        @block.sync
        def _(sp):
            e.load_qkv(sp, 1)

        @block.vector
        def _(dve):
            then = chained(dve, dc)
            for t in range(QT):
                ins = dve.tensor_reduce(mxq[:, 2 * t:2 * t + 2],
                                        qkv[:, t, 0:2 * C].rearrange("p (i n) -> p i n", i=2), AX.X, ALU.max,
                                        negate=True)
            ins.then_inc(maxed, 1)
            dve.wait_ge(exped, 8)
            then(dve.reciprocal(sums, sums))
            for t in range(QT):
                for i in range(2):
                    ins = dve.tensor_scalar(half(t, i), half(t, i), sums[:, 2 * t + i:2 * t + i + 1], None, ALU.mult)
                ins.then_inc(soft, 1)
            dve.wait_ge(soft, QT)
            for t in range(QT):
                ins = dve.tensor_tensor(k3[:, t, :], half(t, 1), half(t, 2), ALU.mult)
            then(ins)
            dve.wait_ge(lm, 1)
            dve.tensor_copy(klT, psum[:, 4, 0:KT * L].rearrange("p (k n) -> p k n", k=KT)).then_inc(lm_in, 1)
            dve.wait_ge(k2, 1)
            dve.tensor_copy(k2T, psum[:, 5, 0:QT * L].rearrange("p (t n) -> p t n", t=QT)).then_inc(k2_in, 1)
            dve.wait_ge(md, 1)
            dve.tensor_copy(mid, psum[0:L, 7, 0:C]).then_inc(md_in, 1)
            for t in range(QT):
                dve.wait_ge(fin, t + 1)
                dve.tensor_tensor(x[:, t, :], psum[:, t, 0:C], x[:, t, :], ALU.add)

        @block.scalar
        def _(act):
            act.wait_ge(maxed, 1)
            for t in range(QT):
                for i in range(2):
                    c = 2 * t + i
                    act.activation(half(t, i), half(t, i), ACT.Exp, bias=mxq[:, c:c + 1],
                                   accum_out=sums[:, c:c + 1]).then_inc(exped, 1)
            act.wait_ge(turned, 1)
            act.copy(qkT, psum[:, 0:4, :]).then_inc(copied, 1)
            act.wait_ge(k2, 1)
            act.copy(k1T, psum[0:L, 6, 0:T]).then_inc(k1_in, 1)

        @block.tensor
        def _(pe):
            for t in range(QT):
                pe.wait_ge(soft, t + 1)
                for i in range(2):
                    for k in range(KT):
                        last = pe.transpose(psum[:, i * KT + k, t * P:(t + 1) * P],
                                            qkv[:, t, i * C + k * P:i * C + (k + 1) * P], ident[:, :])
            last.then_inc(turned, 1)
            for t in range(QT):
                for k in range(KT):
                    last = pe.matmul(psum[:, 4, k * L + 16 * t:k * L + 16 * t + 16],
                                     qkv[:, t, C + k * P:C + (k + 1) * P], e.avg[:, :],
                                     start=(t == 0 and k == 0), stop=True, skip_group_check=True)
            last.then_inc(lm, 1)
            pe.wait_ge(lm_in, 1)
            pe.wait_ge(copied, 1)
            for k in range(KT):
                pe.matmul(psum[0:L, 6, :], klT[:, k, :], qAT[:, k, :], start=(k == 0), stop=(k == KT - 1))
            for t in range(QT):
                for k in range(KT):
                    last = pe.matmul(psum[:, 5, t * L:(t + 1) * L], kAT[:, k, t * P:(t + 1) * P], klT[:, k, :],
                                     start=(t == 0 and k == 0), stop=(k == KT - 1), skip_group_check=True)
            last.then_inc(k2, 1)
            pe.wait_ge(k2_in, 1)
            for t in range(QT):
                last = pe.matmul(psum[0:L, 7, 0:C], k2T[:, t, :], k3[:, t, :], start=(t == 0), stop=(t == QT - 1))
            last.then_inc(md, 1)
            pe.wait_ge(md_in, 1)
            pe.wait_ge(k1_in, 1)
            for t in range(QT):
                pe.matmul(psum[:, t, 0:C], k1T[:, t * P:(t + 1) * P], mid, start=True, stop=True).then_inc(fin, 1)


def standard_attention(e):
    x, xT, V, Vc, colB, R = e.x, e.xT, e.V, e.Vc, e.colB, e.R
    e.norm("n2", x, e.xh, turns=[(xT, None, None)])
    Q, K = e.view(0, H, 1, T), e.view(8192, H, 1, T)
    e.operands("Bp", [
        {"side": "q", "d": D16, "heads": H, "tiles": QT, "w": (e.wBq, 0, xT), "bias": R["L0_xattn_bq"],
         "stack": Q, "first": 0},
        {"side": "k", "d": D16, "heads": H, "tiles": QT, "w": (e.wBk, 0, xT), "bias": R["L0_xattn_bk"],
         "stack": K, "first": 0}], e.values(V, e.wBv, xT, QT))
    e.row_maxima("Bm", Q, K, T, True)
    e.attend("Ba", Q, K, V, T, D16 ** -0.5, causal=True)
    with stage(e.nc, "Bb", "unused") as (block, _u):
        @block.vector
        def _(dve):
            dve.tensor_tensor(e.small[:, 0:HG], colB[:, 0, :], colB[:, 1, :], ALU.add)
    for c in range(2):
        Q, K = e.view(0, 8, 1, T), e.view(4096, 8, 1, TC)
        ops = [{"side": "q", "d": D16, "heads": 8, "tiles": QT, "w": (e.wBcq, P * c, xT),
                "bias": R["L0_xattn_bcq"][:, P * c:P * (c + 1)], "stack": Q, "first": 0},
               {"side": "k", "d": D16, "heads": 8, "tiles": CT, "w": (e.wBck, P * c, e.cT),
                "bias": R["L0_xattn_bck"][:, P * c:P * (c + 1)], "stack": K, "first": 0}]
        e.operands(f"Bc{c}", ops, e.values(Vc, e.wBcv, e.cT, CT) if c == 0 else [])
        e.row_maxima(f"Bcm{c}", Q, K, TC, False)
        e.attend(f"Bca{c}", Q, K, Vc, TC, D16 ** -0.5, g0=2 * c, add=e.small[:, 0:HG])
    e.products("Bo", e.into_rows(x, x, e.yT, e.wBp), before=e.add_rows(x, e.R["L0_xattn_bp"]))


def fp6_linear(e):
    nc, psum, x, xh = e.nc, e.psum, e.x, e.xh
    e.norm("n3", x, xh)
    sc = [e.vbig[:, i * QT * C:(i + 1) * QT * C].rearrange("p (t n) -> p t n", t=QT) for i in range(3)]
    with stage(nc, "Cq", "dc", "quant", "turned") as (block, dc, quant, turned):
        @block.vector
        def _(dve):
            then = chained(dve, dc)
            e.quantise(dve, then, xh[:, :, :], QT, *sc, e.amax, e.scale, e.rscale)
            dve.sem_inc(quant, 1)

        @block.tensor
        def _(pe):
            pe.wait_ge(quant, 1)
            for t in range(QT):
                for k in range(KT):
                    last = pe.transpose(psum[:, k, t * P:(t + 1) * P], xh[:, t, k * P:(k + 1) * P], e.ident[:, :])
            last.then_inc(turned, 1)

        @block.scalar
        def _(act):
            act.wait_ge(turned, 1)
            act.copy(e.xT[:, :, :], psum[:, 0:KT, :])
    e.products("Co", e.into_rows(x, x, e.xT, e.wC), before=e.add_rows(x, e.R["L0_ffn_bias"]))


def hyperbolic_attention(e):
    nc, psum, x, xh, ident = e.nc, e.psum, e.x, e.xh, e.ident
    V = e.V
    e.norm("n4", x, xh, turns=[(e.xT, None, None)])
    qkp = [e.cT[:, 0, :].rearrange("p (t n) -> p t n", t=QT), e.xo[:, :, :]]
    raw = e.prob[:, :, :, :].rearrange("p a b n -> p (a b n)")[:, 0:QT * 3 * C].rearrange("p (t n) -> p t n", t=QT)
    imp, spike = e.small[:, 0:4], e.small[:, 4:8]
    jobs = []
    for t in range(QT):
        for n0, n in ((0, 2 * C), (2 * C, C)):
            pairs = [(e.xT[:, k, t * P:(t + 1) * P], e.wD[:, k, n0:n0 + n]) for k in range(KT)]

            def f(eng, bank, t=t, n0=n0, n=n):
                return eng.tensor_tensor(raw[:, t, n0:n0 + n], bank, e.bD[:, n0:n0 + n], ALU.add)
            jobs.append(("dve", pairs, n, f))

    def zero_pads(pool, then):
        then(pool.memset(V[:, :, :], 0.0))
    e.products("Dp", jobs, before=zero_pads)

    rawv = raw.rearrange("p t (i h d) -> p t i h d", i=3, d=D16)
    NV = QT * 2 * H
    VW = QT * H * W
    nmin, root, small_c, small_s, big_c, big_s = (e.vbig[:, VW + i * NV:VW + (i + 1) * NV] for i in range(6))

    with stage(nc, "De", "dc", "ac", "wready", "rooted", "exped", "vals_in", "spiked", "spike_e") as (
            block, dc, ac, wready, rooted, exped, vals_in, spiked, spike_e):
        ones_tmp = e.rs[:, 0:NV]
        em = e.sm[:, 0:NV]
        ep = e.sm[:, NV:2 * NV]
        pick = e.sm[:, 2 * NV:3 * NV]

        @block.vector
        def _(dve):
            then = chained(dve, dc)
            for t in range(QT):
                then(dve.tensor_tensor_reduce(out=e.ob[:, 0:C], in0=xh[:, t, :], in1=e.w_sur[:, :], scale=1.0,
                                              scalar=0.0, op0=ALU.mult, op1=ALU.add, accum_out=imp[:, t:t + 1]))
            dve.tensor_scalar(imp, imp, e.scal[:, 0:1], None, ALU.add).then_inc(spiked, 1)
            for t in range(QT):
                dve.tensor_copy(V[:, t, :].rearrange("p (h w) -> p h w", w=W)[:, :, 0:D16], rawv[:, t, 2])
            sq = e.ob[:, 0:512]
            for t in range(QT):
                then(dve.tensor_tensor(sq, raw[:, t, 0:2 * C], raw[:, t, 0:2 * C], ALU.mult))
                sv = sq.rearrange("p (v d) -> p v d", d=D16)
                seg = nmin[:, t * 2 * H:(t + 1) * 2 * H]
                then(dve.tensor_reduce(seg, sv[:, :, 1:D16], AX.X, ALU.add))
                then(dve.tensor_tensor(seg, seg, sv[:, :, 0], ALU.subtract))
            then(dve.tensor_scalar(nmin, nmin, 1e-8, None, ALU.max))
            dve.sem_inc(wready, 1)
            then(dve.tensor_scalar(ones_tmp, nmin, 1.0, None, ALU.min))
            for dst, terms in ((small_c, (90.0, 56.0, 30.0, 12.0, 2.0)), (small_s, (110.0, 72.0, 42.0, 20.0, 6.0))):
                then(dve.tensor_scalar(dst, ones_tmp, 1.0 / terms[0], 1.0, ALU.mult, ALU.add))
                for c in terms[1:]:
                    then(dve.tensor_tensor(dst, dst, ones_tmp, ALU.mult))
                    then(dve.tensor_scalar(dst, dst, 1.0 / c, 1.0, ALU.mult, ALU.add))
            dve.wait_ge(exped, 2)
            then(dve.tensor_tensor(big_c, ep, em, ALU.add))
            then(dve.tensor_scalar(big_c, big_c, 0.5, None, ALU.mult))
            then(dve.tensor_tensor(big_s, ep, em, ALU.subtract))
            then(dve.reciprocal(em, root))
            then(dve.scalar_tensor_tensor(big_s, big_s, 0.5, em, ALU.mult, ALU.mult))
            then(dve.tensor_scalar(pick, nmin, 1.0, None, ALU.is_lt))
            for big, low in ((big_c, small_c), (big_s, small_s)):
                then(dve.copy_predicated(big, pick.bitcast(U32), low))
            for t in range(QT):
                for i in range(2):
                    seg = slice((2 * t + i) * H, (2 * t + i + 1) * H)
                    dst = qkp[i][:, t, :].rearrange("p (h w) -> p h w", w=D16)
                    dve.tensor_copy(dst[:, :, 0], big_c[:, seg])
                    sp_ = big_s[:, seg].unsqueeze(2).to_broadcast([P, H, D16 - 1])
                    if i == 0:
                        dve.tensor_tensor(dst[:, :, 1:D16], rawv[:, t, 0, :, 1:D16], sp_, ALU.mult)
                    else:
                        dve.scalar_tensor_tensor(dst[:, :, 1:D16], rawv[:, t, 1, :, 1:D16], -1.0, sp_,
                                                 ALU.mult, ALU.mult)
            dve.wait_ge(spike_e, 1)
            then(dve.tensor_scalar(spike, spike, 1.0, None, ALU.add))
            then(dve.reciprocal(spike, spike))
            dve.tensor_scalar(spike, spike, e.scal[:, 1:2], None, ALU.is_gt)

        @block.scalar
        def _(act):
            act.wait_ge(spiked, 1)
            act.activation(spike, imp, ACT.Exp, scale=-1.0).then_inc(spike_e, 1)
            act.wait_ge(wready, 1)
            act.activation(root, nmin, ACT.Sqrt).then_inc(rooted, 1)
            act.wait_ge(rooted, 1)
            act.activation(ep, root, ACT.Exp).then_inc(exped, 1)
            act.activation(em, root, ACT.Exp, scale=-1.0).then_inc(exped, 1)

    Q, K = e.view(0, H, 1, T), e.view(8192, H, 1, T)
    e.operands("Dt", [
        {"side": "q", "d": D16, "heads": H, "tiles": QT, "value": e.cT[:, 0, :], "stack": Q, "first": 0},
        {"side": "k", "d": D16, "heads": H, "tiles": QT, "value": e.xo[:, :, :].rearrange("p t n -> p (t n)"),
         "stack": K, "first": 0}], [])

    def least_distance(dve, then, m, tiny, tiny_back):
        mm, m1, m2 = e.mm[:, :], e.m1[:, :], e.m2[:, :]
        then(dve.tensor_scalar(m1, m, 1.0 + 1e-7, -1.0, ALU.max, ALU.add))
        dve.scalar_tensor_tensor(m2, m1, 2.0, m1, ALU.add, ALU.mult).then_inc(tiny, 1)
        dve.wait_ge(tiny_back, 2)
        dve.tensor_tensor(m1, m1, m2, ALU.add).then_inc(tiny, 1)
        dve.wait_ge(tiny_back, 3)
        then(dve.tensor_tensor(mm, m1, m1, ALU.mult))
    e.row_maxima("Dm", Q, K, T, True, op=ALU.min, dist=least_distance)

    steps = [(g, p, k) for g in range(HG) for p in range(2) for k in range(QT)]
    NS = len(steps)
    SCALE = -1.0 / D16 ** 0.5
    prob = e.prob
    tbuf = [r[:, i * 2 * T:(i + 1) * 2 * T].rearrange("p (a n) -> p a n", a=2)
            for r in (e.vbig[:, VW:2 * VW], e.parts2[:, :].bitcast(F32)) for i in range(2)]

    with stage(nc, "Da", "scored", "lows", "over", "wready", "rooted", "summed", "logged", "squared",
               "less", "exped", "masked", "weighed", "bank_free", "dc", "ac") as (
            block, scored, lows, over, wready, rooted, summed, logged, squared, less, exped, masked,
            weighed, bank_free, dc, ac):
        @block.tensor
        def _(pe):
            def score(n):
                g, p, k = steps[n]
                q0 = k * P
                if n >= 2:
                    pe.wait_ge(over, n - 1)
                for jj in range(2):
                    hd = g * J + 2 * p + jj
                    last = pe.matmul(psum[:, 2 * (n % 2) + jj, q0:T], K[0:e.ROWS, hd, 0, q0:q0 + P],
                                     Q[0:e.ROWS, hd, 0, q0:T], start=True, stop=True)
                last.then_inc(scored, 1)

            def spread_lows(n):
                g, p, k = steps[n]
                if n:
                    pe.wait_ge(less, n)
                for jj in range(2):
                    hd = g * J + 2 * p + jj
                    last = pe.matmul(psum[:, 4 + jj, :], K[e.ROWS:P, hd, 0, 0:P], Q[e.ROWS:P, hd, 0, :],
                                     start=True, stop=True)
                last.then_inc(lows, 1)

            def weigh(n):
                g, p, k = steps[n]
                q0 = k * P
                pe.wait_ge(masked, n + 1)
                if g and p == 0 and k == 0:
                    pe.wait_ge(bank_free, g)
                for bank, ones in ((6, False), (7, True)):
                    for jj in range(2):
                        j = 2 * p + jj
                        lhsT = e.ones_f[:, :] if ones else V[:, k, g * P + W * j:g * P + W * j + W]
                        last = pe.matmul(psum[W * j:W * j + W, bank, q0:T], lhsT, prob[:, n % 4, jj, q0:T],
                                         start=(k == 0), stop=(k == QT - 1), skip_group_check=True)
                last.then_inc(weighed, 1)

            for n in range(NS + 2):
                if n < NS:
                    score(n)
                if n >= 2:
                    m = n - 2
                    if steps[m][2] == 0:
                        spread_lows(m)
                    if m >= 1:
                        weigh(m - 1)
            weigh(NS - 1)

        @block.vector
        def _(dve):
            then = chained(dve, dc)

            def above_one(n):
                q0 = steps[n][2] * P
                dve.wait_ge(scored, n + 1)
                if n >= 4:
                    dve.wait_ge(exped, n - 3)
                    dve.wait_ge(weighed, n - 3)
                t_ = tbuf[n % 4][:, :, q0:T]
                dve.tensor_scalar(t_, psum[:, 2 * (n % 2):2 * (n % 2) + 2, q0:T], 1.0 + 1e-7, -1.0,
                                  ALU.max, ALU.add).then_inc(over, 1)
                dve.wait_ge(over, n + 1)
                dve.scalar_tensor_tensor(prob[:, n % 4, :, q0:T], t_, 2.0, t_, ALU.add, ALU.mult).then_inc(wready, 1)

            def add_root(n):
                q0 = steps[n][2] * P
                dve.wait_ge(rooted, 2 * (n + 1))
                t_ = tbuf[n % 4][:, :, q0:T]
                dve.tensor_tensor(t_, t_, prob[:, n % 4, :, q0:T], ALU.add).then_inc(summed, 1)

            def subtract_low(n):
                q0 = steps[n][2] * P
                dve.wait_ge(squared, n + 1)
                dve.wait_ge(lows, n // QT + 1)
                t_ = tbuf[n % 4][:, :, q0:T]
                dve.tensor_tensor(t_, t_, psum[:, 4:6, q0:T], ALU.subtract).then_inc(less, 1)

            done = 0
            for n in range(NS + 4):
                if n < NS:
                    above_one(n)
                if 1 <= n <= NS:
                    add_root(n - 1)
                if 2 <= n <= NS + 1:
                    subtract_low(n - 2)
                if n >= 4 + 2 * QT - 1 and (n - 4 - (2 * QT - 1)) % (2 * QT) == 0:
                    g = done
                    dve.wait_ge(weighed, 2 * QT * (g + 1))
                    dve.tensor_copy(e.ob[:, :], psum[:, 6, :])
                    dve.tensor_copy(e.sm[:, :], psum[:, 7, :]).then_inc(bank_free, 1)
                    dve.wait_ge(bank_free, g + 1)
                    then(dve.reciprocal(e.rs[:, :], e.sm[:, :]))
                    then(dve.tensor_tensor(e.yT[:, g, :], e.ob[:, :], e.rs[:, :], ALU.mult))
                    done += 1

        @block.scalar
        def _(act):
            def root(n):
                q0 = steps[n][2] * P
                w_ = prob[:, n % 4, :, q0:T]
                act.wait_ge(wready, n + 1)
                act.activation(w_, w_, ACT.Ln).then_inc(rooted, 1)
                act.wait_ge(rooted, 2 * n + 1)
                act.activation(w_, w_, ACT.Exp, scale=0.5).then_inc(rooted, 1)

            def log(n):
                q0 = steps[n][2] * P
                t_ = tbuf[n % 4][:, :, q0:T]
                act.wait_ge(summed, n + 1)
                act.activation(t_, t_, ACT.Ln, bias=1.0).then_inc(logged, 1)

            def exponentiate(n):
                q0 = steps[n][2] * P
                act.wait_ge(less, n + 1)
                act.activation(prob[:, n % 4, :, q0:T], tbuf[n % 4][:, :, q0:T], ACT.Exp,
                               scale=SCALE).then_inc(exped, 1)

            for n in range(NS + 2):
                if n < NS:
                    root(n)
                if 1 <= n <= NS:
                    log(n - 1)
                if n >= 2:
                    exponentiate(n - 2)

        @block.gpsimd
        def _(pool):
            def square(n):
                q0 = steps[n][2] * P
                t_ = tbuf[n % 4][:, :, q0:T]
                pool.wait_ge(logged, n + 1)
                pool.tensor_tensor(t_, t_, t_, ALU.mult).then_inc(squared, 1)

            def cut(n):
                q0 = steps[n][2] * P
                d = prob[:, n % 4, :, q0:q0 + P]
                pool.wait_ge(exped, n + 1)
                pool.affine_select(d, d, [[0, 2], [1, P]], ALU.is_ge, 0.0, base=0,
                                   channel_multiplier=-1).then_inc(masked, 1)

            for n in range(NS + 1):
                if n < NS:
                    square(n)
                if n >= 1:
                    cut(n - 1)

    jobs = []
    for t in range(QT):
        pairs = [(e.yT[:, g, t * P:(t + 1) * P], e.wDo[:, g, :]) for g in range(HG)]

        def f(eng, bank, t=t):
            return eng.scalar_tensor_tensor(x[:, t, :], bank, spike[:, t:t + 1], x[:, t, :], ALU.mult, ALU.add)
        jobs.append(("dve", pairs, C, f))
    e.products("Do", jobs, before=e.add_rows(x, e.R["L1_attn_b_out"]))


def mixture(nc, es, dram, x5, out, psum, ident, nhalf):
    def sb(name, shape, dt=F32):
        return es.enter_context(nc.sbuf_tensor(name, shape, dt))

    NT = B * QT
    xs, xn = sb("xs", [P, NT, C]), sb("xn", [P, NT, C])
    xTall = sb("xTall", [P, KT, NT * P])
    hid = sb("hid", [P, 2, FT, T])
    w1, w2 = sb("ew1", [P, 2, KT, F]), sb("ew2", [P, 2, FT, C])
    b1c = sb("b1c", [P, NE, FT])
    b2s = sb("b2s", [NE, C])
    wg, bg = sb("wg", [P, KT, NE]), sb("bg", [P, NE])
    comb = sb("comb", [P, NT, NE])
    combT = sb("combT", [NE, NT * P])
    lg, ex, top = sb("lg", [P, NT, NE]), sb("ex", [P, NT, NE]), sb("top", [P, NT, NE])
    idx, idf = sb("idx", [P, NT, NE], U32), sb("idf", [P, NT, NE])
    iota, hot = sb("iota", [P, NE]), sb("hot", [P, NT, NE])
    col = sb("col", [P, 4, NT])
    stats, mv = sb("mstats", [P, NT, 6]), sb("mmv", [P, NT, 2])
    eps_var, rstd = sb("mev", [P, NT]), sb("mrstd", [P, NT])

    w_in = [es.enter_context(nc.semaphore(f"expert_weights_in{i}")) for i in range(2)]

    def load_expert(eng, i, ex_):
        one = slice(ex_, ex_ + 1) if isinstance(ex_, int) else bass.ds(ex_, 1)
        eng.dma_start(w1[:, i, :, :], dram["L1_ffn_W1"][one].rearrange("o (k p) n -> p (o k) n", p=P)).then_inc(w_in[i], 16)
        eng.dma_start(w2[:, i, :, :], dram["L1_ffn_W2"][one].rearrange("o (k p) n -> p (o k) n", p=P)).then_inc(w_in[i], 16)

    with stage(nc, "mi", "in_", "unused") as (block, in_, _u):
        @block.sync
        def _(sp):
            sp.dma_start(xs[:, :, :].rearrange("p (b t) c -> p b t c", b=B), x5.rearrange("b p t c -> p b t c")).then_inc(in_, 16)
            sp.dma_start(wg[:, :, :], dram["L1_ffn_Wg"].rearrange("(k p) n -> p k n", p=P)).then_inc(in_, 16)
            sp.dma_start(bg[:, :], dram["L1_ffn_bg"].partition_broadcast(P)).then_inc(in_, 16)
            sp.dma_start(b2s[:, :], dram["L1_ffn_b2"]).then_inc(in_, 16)
            for x_ in range(NE):
                sp.dma_start(b1c[:, x_, :], dram["L1_ffn_b1"][x_].rearrange("(f p) -> p f", p=P)).then_inc(in_, 16)
            sp.wait_ge(in_, 16 * (4 + NE))

        @block.scalar
        def _(act):
            for i in range(2):
                load_expert(act, i, i)

        @block.gpsimd
        def _(pool):
            pool.iota(idx[:, 0, :], [[1, NE]], base=0, channel_multiplier=0)

    with stage(nc, "mn", "dc", "var_ready", "rstd_ready", "normed", "turned", "copied", "gated", "logged") as (
            block, dc, var_ready, rstd_ready, normed, turned, copied, gated, logged):
        on_vector, on_pool = norm_stats(nc, "mn", xs, stats, mv, rstd, eps_var, nhalf, NT, (dc, var_ready, rstd_ready))

        @block.gpsimd
        def _(pool):
            on_pool(pool)

        @block.vector
        def _(dve):
            then = chained(dve, dc)
            dve.tensor_copy(iota[:, :], idx[:, 0, :])
            on_vector(dve, then)
            for t in range(NT):
                dve.tensor_scalar(xn[:, t, :], xs[:, t, :], mv[:, t, 0:1], rstd[:, t:t + 1],
                                  ALU.subtract, ALU.mult).then_inc(normed, 1)
            for t in range(NT):
                dve.wait_ge(gated, t + 1)
                dve.tensor_tensor(lg[:, t, :], psum[:, 6, t * NE:(t + 1) * NE], bg[:, :], ALU.add)

        @block.tensor
        def _(pe):
            for b in range(B):
                if b >= 2:
                    pe.wait_ge(copied, b - 1)
                for t in range(QT):
                    tt = b * QT + t
                    pe.wait_ge(normed, tt + 1)
                    for k in range(KT):
                        last = pe.transpose(psum[:, 2 * (b % 2) + k, t * P:(t + 1) * P],
                                            xn[:, tt, k * P:(k + 1) * P], ident[:, :])
                last.then_inc(turned, 1)
            for tt in range(NT):
                pe.wait_ge(copied, tt // QT + 1)
                for k in range(KT):
                    last = pe.matmul(psum[:, 6, tt * NE:(tt + 1) * NE], xTall[:, k, tt * P:(tt + 1) * P], wg[:, k, :],
                                     start=(tt == 0 and k == 0), stop=(k == KT - 1), skip_group_check=True)
                if tt == NT - 1:
                    last.then_inc(gated, NT)

        @block.scalar
        def _(act):
            for b in range(B):
                act.wait_ge(turned, b + 1)
                act.copy(xTall[:, :, b * T:(b + 1) * T], psum[:, 2 * (b % 2):2 * (b % 2) + 2, :]).then_inc(copied, 1)

    with stage(nc, "mg", "dc", "ready", "exped", "mixed", "turned", "crow", "biased") as (
            block, dc, ready, exped, mixed, turned, crow, biased):
        @block.vector
        def _(dve):
            then = chained(dve, dc)
            wide = [P, NT, NE]
            mxr, sm_ = col[:, 0, :], col[:, 1, :]
            then(dve.tensor_reduce(mxr, lg[:, :, :], AX.X, ALU.max))
            dve.tensor_tensor(lg[:, :, :], lg[:, :, :], mxr.unsqueeze(2).to_broadcast(wide), ALU.subtract).then_inc(ready, 1)
            dve.wait_ge(exped, 1)
            then(dve.tensor_reduce(sm_, ex[:, :, :], AX.X, ALU.add))
            then(dve.reciprocal(sm_, sm_))
            then(dve.tensor_tensor(ex[:, :, :], ex[:, :, :], sm_.unsqueeze(2).to_broadcast(wide), ALU.mult))
            for t in range(NT):
                ins = dve.max(top[:, t, :], ex[:, t, :])
            then(ins)
            for t in range(NT):
                ins = dve.max_index(idx[:, t, :], top[:, t, :], ex[:, t, :])
            then(ins)
            then(dve.tensor_copy(idf[:, :, :], idx[:, :, :]))
            then(dve.tensor_tensor(mxr, top[:, :, 0], top[:, :, 1], ALU.add))
            then(dve.tensor_scalar(mxr, mxr, 1e-8, None, ALU.add))
            then(dve.reciprocal(mxr, mxr))
            for i in range(2):
                then(dve.tensor_tensor(col[:, 2 + i, :], top[:, :, i], mxr, ALU.mult))
                dst = comb if i == 0 else hot
                then(dve.tensor_tensor(dst[:, :, :], iota[:, :].unsqueeze(1).to_broadcast(wide),
                                       idf[:, :, i].unsqueeze(2).to_broadcast(wide), ALU.is_equal))
                then(dve.tensor_tensor(dst[:, :, :], dst[:, :, :], col[:, 2 + i, :].unsqueeze(2).to_broadcast(wide), ALU.mult))
            then(dve.tensor_tensor(comb[:, :, :], comb[:, :, :], hot[:, :, :], ALU.add))
            dve.sem_inc(mixed, 1)
            for t in range(NT):
                dve.wait_ge(biased, t + 1)
                dve.tensor_tensor(xs[:, t, :], psum[:, 4 + t % 4, 0:C], xs[:, t, :], ALU.add).then_inc(crow, 1)

        @block.scalar
        def _(act):
            act.wait_ge(ready, 1)
            act.activation(ex[:, :, :], lg[:, :, :], ACT.Exp).then_inc(exped, 1)
            for i in range(4):
                act.wait_ge(turned, i + 1)
                act.copy(combT[:, i * T:(i + 1) * T], psum[0:NE, i, :]).then_inc(exped, 1)

        @block.tensor
        def _(pe):
            pe.wait_ge(mixed, 1)
            for i in range(4):
                for t in range(QT):
                    last = pe.transpose(psum[0:NE, i, t * P:(t + 1) * P], comb[:, i * QT + t, :], ident[:, :])
                last.then_inc(turned, 1)
            for t in range(NT):
                pe.wait_ge(exped, 2 + t // QT)
                if t >= 4:
                    pe.wait_ge(crow, t - 3)
                pe.matmul(psum[:, 4 + t % 4, 0:C], combT[:, t * P:(t + 1) * P], b2s[:, :], start=True,
                          stop=True).then_inc(biased, 1)

    def expert_pair(e0, prefetch):
        with stage(nc, "ex" if prefetch else "el", "up", "acted", "down", "added", "dc") as (block, up, acted, down, added, dc):
            units = [(i, b) for i in range(2) for b in range(B)]

            @block.tensor
            def _(pe):
                def rise(u):
                    i, b = units[u]
                    if b == 0:
                        pe.wait_ge(w_in[i], 32)
                    for f in range(FT):
                        m = u * FT + f
                        if m >= 4:
                            pe.wait_ge(acted, m - 3)
                        for k in range(KT):
                            last = pe.matmul(psum[:, m % 4, :], w1[:, i, k, f * P:(f + 1) * P],
                                             xTall[:, k, b * T:(b + 1) * T], start=(k == 0), stop=(k == KT - 1))
                        last.then_inc(up, 1)

                def fall(u):
                    i, b = units[u]
                    pe.wait_ge(acted, FT * (u + 1))
                    for t in range(QT):
                        m = u * QT + t
                        if m >= 4:
                            pe.wait_ge(added, m - 3)
                        for f in range(FT):
                            last = pe.matmul(psum[:, 4 + m % 4, 0:C], hid[:, u % 2, f, t * P:(t + 1) * P],
                                             w2[:, i, f, :], start=(f == 0), stop=(f == FT - 1))
                        last.then_inc(down, 1)

                rise(0)
                for u in range(len(units)):
                    if u + 1 < len(units):
                        rise(u + 1)
                    fall(u)

            @block.scalar
            def _(act):
                for u, (i, b) in enumerate(units):
                    for f in range(FT):
                        m = u * FT + f
                        act.wait_ge(up, m + 1)
                        if u >= 2 and f == 0:
                            act.wait_ge(down, QT * (u - 1))
                        bias = b1c[:, bass.ds(e0 + i, 1), f:f + 1].rearrange("p a b -> p (a b)")
                        act.activation(hid[:, u % 2, f, :], psum[:, m % 4, :], ACT.Gelu_apprx_tanh,
                                       bias=bias).then_inc(acted, 1)

            @block.vector
            def _(dve):
                for u, (i, b) in enumerate(units):
                    for t in range(QT):
                        m, tt = u * QT + t, b * QT + t
                        dve.wait_ge(down, m + 1)
                        if i:
                            dve.wait_ge(added, b * QT + t + 1)
                        c_ = comb[:, tt, bass.ds(e0 + i, 1)]
                        dve.scalar_tensor_tensor(xs[:, tt, :], psum[:, 4 + m % 4, 0:C], c_, xs[:, tt, :],
                                                 ALU.mult, ALU.add).then_inc(added, 1)

            if prefetch:
                @block.sync
                def _(sp):
                    for i in range(2):
                        sp.wait_ge(down, B * QT * (i + 1))
                        sp.sem_clear(w_in[i])
                        load_expert(sp, i, e0 + 2 + i)

    with nc.Fori(0, NE // 2 - 1) as pair:
        expert_pair(pair * 2, True)
    expert_pair(NE - 2, False)

    with stage(nc, "mo", "stored", "unused") as (block, stored, _u):
        @block.sync
        def _(sp):
            ov = out.rearrange("b (t p) c -> p (b t) c", p=P)
            sp.dma_start(ov, xs[:, :, :]).then_inc(stored, 16)
            sp.wait_ge(stored, 16)


SCALARS = ("L1_attn_b_sur", "L1_attn_threshold")


def kernel(**inputs):
    import numpy as _np
    import concourse.bacc as _bacc
    from concourse.bass_utils import run_bass_kernel_spmd as _run

    nc = _bacc.Bacc("TRN2", target_bir_lowering=False, num_devices=1)
    arrays, dram = {}, {}
    for name, a in inputs.items():
        a = _np.ascontiguousarray(a)
        if name in SCALARS:
            a = a.reshape(1)
        arrays[f"in_{name}"] = a
        dram[name] = nc.dram_tensor(f"in_{name}", a.shape, mybir.dt.from_np(a.dtype), kind="ExternalInput").ap()
    out = nc.dram_tensor("out_0", (B, T, C), F32, kind="ExternalOutput").ap()
    build(nc, dram, out)
    r = _run(nc, [arrays], core_ids=[0])
    return r.results[0]["out_0"]
```

```python
from contextlib import ExitStack, contextmanager

import concourse.bass as bass
from concourse import mybir

F32 = mybir.dt.float32
BF16 = mybir.dt.bfloat16
U32 = mybir.dt.uint32
ALU = mybir.AluOpType
ACT = mybir.ActivationFunctionType
AX = mybir.AxisListType

P = 128
B, T, C = 4, 512, 256
TC, CC = 1024, 128
QT, KT, CT = T // P, C // P, TC // P
H, J = 16, 4
HG, W = H // J, 32
D16 = C // H
BANK = 512
EPS = 1e-5
BIG = 1e30
F = 4 * C
FT = F // P
NE = 8
GRID_MAX = 7.5
MAGIC = 12582912.0


def build(nc, dram, out):
    ctx = ExitStack()
    with ctx:
        ctx.enter_context(nc.allow_non_contiguous_dma(reason="bias vectors to columns, once"))
        psum = ctx.enter_context(nc.psum_tensor("psum", [P, 8, BANK], F32))
        x5 = nc.dram_tensor("x_after_layers", [B, P, QT, C], F32, kind="Internal").ap()
        ident = ctx.enter_context(nc.sbuf_tensor("ident", [P, P], F32))
        nhalf = ctx.enter_context(nc.sbuf_tensor("nhalf", [P, QT * QT], F32))
        with ExitStack() as layers:
            decoder_layers(nc, layers, dram, x5, psum, ident, nhalf)
        with ExitStack() as experts:
            mixture(nc, experts, dram, x5, out, psum, ident, nhalf)


class Shared:
    pass


@contextmanager
def stage(nc, tag, *names):
    with ExitStack() as s:
        sems = [s.enter_context(nc.semaphore(f"{tag}_{n}")) for n in names]
        with nc.Block() as block:
            yield (block, *sems)
        nums = sorted(x.num for x in sems)
        while nums:
            n = next((i for i, v in enumerate(nums) if v != nums[0] + i), len(nums))
            nc.all_engine_barrier(sems_to_clear=range(nums[0], nums[0] + n))
            nums = nums[n:]


def chained(eng, sem):
    count = [0]

    def then(ins):
        count[0] += 1
        ins.then_inc(sem, 1)
        eng.wait_ge(sem, count[0])
    return then


def norm_stats(nc, tag, src, stats, mv, rstd, eps_var, nhalf, n, sems):
    chain, var_ready, rstd_ready = sems

    def on_vector(dve, then):
        for t in range(n):
            last = dve.bn_stats(stats[:, t, :], src[:, t, :])
        then(last)
        for t in range(n):
            last = dve.bn_aggr(mv[:, t, :], stats[:, t, :])
        then(last)
        dve.tensor_scalar(eps_var[:, 0:n], mv[:, 0:n, 1], EPS, None, ALU.add).then_inc(var_ready, 1)
        dve.wait_ge(rstd_ready, 1)

    def on_pool(pool):
        pool.wait_ge(var_ready, 1)
        pool.tensor_tensor(rstd[:, 0:n], eps_var[:, 0:n], nhalf[:, 0:n], ALU.pow).then_inc(rstd_ready, 1)
    return on_vector, on_pool


def decoder_layers(nc, es, dram, x5, psum, ident, nhalf):
    def sb(name, shape, dt=F32):
        return es.enter_context(nc.sbuf_tensor(name, shape, dt))

    w_slot = sb("w_slot", [P, 6 * BANK])
    wA = w_slot[:, 0:KT * 3 * C].rearrange("p (k n) -> p k n", k=KT)
    w1q, w1k, w1v = (w_slot[:, i * 1024:(i + 1) * 1024].rearrange("p (k n) -> p k n", k=KT) for i in range(3))
    w2q = w1q
    w2k = w_slot[:, 1024:1536].rearrange("p (k n) -> p k n", k=1)
    w2v = w_slot[:, 1536:2048].rearrange("p (k n) -> p k n", k=1)
    bA = sb("bA", [P, 3 * C])
    wBq, wBk, wBcq = (sb(n, [P, KT, C]) for n in ("wBq", "wBk", "wBcq"))
    wBck = sb("wBck", [P, 1, C])
    wBv, wBcv = sb("wBv", [P, KT, C]), sb("wBcv", [P, 1, C])
    wBp = sb("wBp", [P, HG, C])
    colB = sb("colB", [P, 2, HG])
    wC = sb("wC", [P, KT, C])
    wD, bD, wDo = sb("wD", [P, KT, 3 * C]), sb("bD", [P, 3 * C]), sb("wDo", [P, HG, C])
    w_sur, scal = sb("w_sur", [P, C]), sb("scal", [P, 2])
    w_li1 = [sb(f"w_li1_{i}", [P, HG, C]) for i in (1, 2)]
    w_mlp = sb("w_mlp", [P, KT * F + FT * C])
    w_li2 = w_mlp[:, 0:KT * F].rearrange("p (k n) -> p k n", k=KT)
    w_li3 = w_mlp[:, KT * F:KT * F + FT * C].rearrange("p (f n) -> p f n", f=FT)
    q_stack = w_mlp[:, :].bitcast(BF16)
    rows = sb("rows", [P, 15, C])
    R = {n: rows[:, i, :] for i, n in enumerate(
        ("L0_xattn_bp", "L0_ffn_bias", "L1_attn_b_out", "L1_xattn_ln1_g", "L1_xattn_ln1_b",
         "L1_xattn_ln2_g", "L1_xattn_ln2_b", "L1_xattn_a1_li1_b", "L1_xattn_a1_li3_b",
         "L1_xattn_a2_li1_b", "L1_xattn_a2_li3_b",
         "L0_xattn_bq", "L0_xattn_bk", "L0_xattn_bcq", "L0_xattn_bck"))}
    cols = sb("cols", [P, 40])
    Ccol, at = {}, 0
    for a in ("a1", "a2"):
        for n, k in (("lnx_g", 2), ("lnx_b", 2), ("lny_g", 2 if a == "a1" else 1),
                     ("lny_b", 2 if a == "a1" else 1), ("ln3_g", 2), ("ln3_b", 2), ("li2_b", 8)):
            Ccol[f"L1_xattn_{a}_{n}"] = cols[:, at:at + k]
            at += k
    identb = sb("identb", [P, P], BF16)
    ones_f = sb("ones_f", [P, W])
    pads_of = sb("pads_of", [P, J])
    avg = sb("avg", [P, 16])
    hide_above, hide_below = sb("hide_above", [P, P], BF16), sb("hide_below", [P, P], BF16)

    x, xh, xa, xo = (sb(n, [P, QT, C]) for n in ("x", "xh", "xa", "xo"))
    xT = sb("xT", [P, KT, T])
    cT, cnT = sb("cT", [P, 1, TC]), sb("cnT", [P, 1, TC])
    yT = sb("yT", [P, HG, T])
    stack = sb("stack", [P, 16384], BF16)
    vbig = sb("vbig", [P, CT * H * W])
    prob = sb("prob", [P, 4, 2, T])
    parts2 = sb("parts2", [P, 6144], BF16)
    ob, scr = sb("ob", [P, T]), sb("scr", [P, 2 * T])
    sm, rs = scr[:, 0:T], scr[:, T:2 * T]
    stats, mv = sb("stats", [P, CT, 6]), sb("mv", [P, CT, 2])
    eps_var, rstd = sb("eps_var", [P, CT]), sb("rstd", [P, CT])
    small, inverse = sb("small", [P, 32]), sb("inverse", [P, QT * J])

    NM = HG * QT * J
    mx = ob[:, 0:2 * NM].rearrange("p (h g t j) -> p h g t j", h=2, g=HG, t=QT)
    mm, m1, m2 = (ob[:, (2 + i) * NM:(3 + i) * NM] for i in range(3))
    mb = ob[:, 5 * NM:5 * NM + 3 * NM // 2].bitcast(BF16).rearrange("p (i m) -> p i m", i=3)
    yT2 = yT[:, KT:2 * KT, :]
    work = stack[:, :].bitcast(F32)
    hT = work[:, 0:FT * T].rearrange("p (f n) -> p f n", f=FT)
    V = vbig[:, 0:QT * H * W].rearrange("p (k n) -> p k n", k=QT)
    Vc = vbig[:, :].rearrange("p (k n) -> p k n", k=CT)
    probb = prob[:, :, :, :].rearrange("p a b n -> p (a b n)").bitcast(BF16)
    parts = [probb[:, 0:6144], parts2[:, :]]
    mpad = probb[:, 0:HG * QT * J * W].rearrange("p (m w) -> p m w", w=W)
    pm = xh[:, :, :].rearrange("p a (b n) -> p a b n", b=2)

    loads = es.enter_context(nc.semaphore("params_loaded"))
    slot_loaded = es.enter_context(nc.semaphore("slot_loaded"))
    mlp_loaded = es.enter_context(nc.semaphore("mlp_loaded"))

    def load_qkv(eng, i):
        if i == 0:
            for m, n in enumerate("qkv"):
                eng.dma_start(wA[:, :, m * C:(m + 1) * C],
                              dram[f"L0_attn_W{n}"].rearrange("(k p) n -> p k n", p=P)).then_inc(slot_loaded, 16)
            return
        for w, n in ((w1q, "wq"), (w1k, "wk"), (w1v, "wv")) if i == 1 else ((w2q, "wq"), (w2k, "wk"), (w2v, "wv")):
            s = dram[f"L1_xattn_a{i}_{n}"].rearrange("h (k p) d -> k p h d", p=P)
            for k in range(w.shape[1]):
                eng.dma_start(w[:, k, :].rearrange("p (h d) -> p h d", d=W), s[k]).then_inc(slot_loaded, 16)

    def spread(v):
        return v.partition_broadcast(P)

    with stage(nc, "clear", "cleared", "shaped", "dc") as (block, cleared, shaped, dc):
        padded = [wBp, wDo]

        @block.vector
        def _(dve):
            for w in padded:
                dve.memset(w[:, :, :], 0.0)
            dve.memset(colB[:, :, :], 0.0)
            dve.memset(ones_f[:, :], 1.0)
            dve.memset(nhalf[:, :], -0.5)
            dve.memset(ident[:, :], 1.0).then_inc(cleared, 1)
            dve.memset(avg[:, :], float(H) / 128.0).then_inc(cleared, 1)
            dve.memset(prob[:, 0, 0, 0:P], BIG).then_inc(cleared, 1)
            dve.memset(prob[:, 0, 1, 0:P], -BIG).then_inc(cleared, 1)
            dve.wait_ge(shaped, 5)
            strips = ident[:, :].rearrange("p (j w) -> p j w", w=W)
            dve.tensor_copy(pads_of[:, :], strips[:, :, D16])
            dve.tensor_copy(identb[:, :], ident[:, :])
            dve.tensor_copy(hide_below[:, :], prob[:, 0, 0, 0:P])
            dve.tensor_copy(hide_above[:, :], prob[:, 0, 1, 0:P])

        @block.gpsimd
        def _(pool):
            pool.wait_ge(cleared, 4)
            pool.affine_select(ident[:, :], ident[:, :], [[1, P]], ALU.is_equal, 0.0, base=0,
                               channel_multiplier=-1).then_inc(shaped, 1)
            pool.affine_select(avg[:, :], avg[:, :], [[-8, 16]], ALU.is_ge, 0.0, base=0,
                               channel_multiplier=1).then_inc(shaped, 1)
            pool.wait_ge(shaped, 2)
            pool.affine_select(avg[:, :], avg[:, :], [[8, 16]], ALU.is_ge, 0.0, base=7,
                               channel_multiplier=-1).then_inc(shaped, 1)
            for i in range(2):
                pool.affine_select(prob[:, 0, i, 0:P], prob[:, 0, i, 0:P], [[1, P]], ALU.is_gt, 0.0,
                                   base=0, channel_multiplier=-1).then_inc(shaped, 1)

    with stage(nc, "load", "unused") as (block, _u):
        n_loads = [0]

        def put(eng, dst, src):
            eng.dma_start(dst, src).then_inc(loads, 16)
            n_loads[0] += 1

        def load_first(eng):
            load_qkv(eng, 0)

        def pad_rows(eng, dst, src):
            s = src.rearrange("(g j d) n -> j d g n", j=J, d=D16)
            for j in range(J):
                put(eng, dst[W * j:W * j + D16, :, :], s[j])

        @block.sync
        def _(sp):
            for i, n in enumerate("qkv"):
                put(sp, bA[:, i * C:(i + 1) * C], spread(dram[f"L0_attn_b{n}"]))
            for w, n in ((wBq, "Wq"), (wBk, "Wk"), (wBcq, "Wcq"), (wBck, "Wck")):
                put(sp, w[:, :, :], dram[f"L0_xattn_{n}"].rearrange("(k p) n -> p k n", p=P))
            put(sp, wBv[:, :, :], dram["L0_xattn_Wv"].rearrange("(k p) n -> p k n", p=P))
            pad_rows(sp, wBp, dram["L0_xattn_Wp"])
            put(sp, bD[:, :], spread(dram["L1_attn_b_qkv"]))
            put(sp, wD[:, :, :], dram["L1_attn_W_qkv"].rearrange("(k p) n -> p k n", p=P))
            put(sp, w_sur[:, :], spread(dram["L1_attn_w_sur"]))
            put(sp, scal[:, 0:1], spread(dram["L1_attn_b_sur"]))
            put(sp, scal[:, 1:2], spread(dram["L1_attn_threshold"]))
            for n, dst in R.items():
                put(sp, dst, spread(dram[n]))

        @block.scalar
        def _(act):
            load_first(act)
            put(act, wBcv[:, :, :], dram["L0_xattn_Wcv"].rearrange("(k p) n -> p k n", p=P))
            pad_rows(act, wDo, dram["L1_attn_W_out"])
            for i in (1, 2):
                put(act, w_li1[i - 1][:, :, :],
                    dram[f"L1_xattn_a{i}_li1_w"].rearrange("(g p) n -> p g n", p=P))

            for i, n in enumerate(("bv", "bcv")):
                s = dram[f"L0_xattn_{n}"].rearrange("(g j d) -> j d g", j=J, d=D16)
                for j in range(J):
                    put(act, colB[W * j:W * j + D16, i, :], s[j])
            for n, dst in Ccol.items():
                put(act, dst, dram[n].rearrange("(k p) -> p k", p=P))
            put(act, xa[:, 0:KT, :], dram["L0_ffn_weight"].rearrange("(k p) n -> p k n", p=P))
            act.wait_ge(loads, 16 * n_loads[0])

    def quantise(dve, then, src, n, a, b_, c_, amax, scale, rscale):
        nb = n * C // 32
        s3 = src.rearrange("p t (b e) -> p (t b) e", e=32)
        a3 = a.rearrange("p t (b e) -> p (t b) e", e=32)
        wide3 = [P, nb, 32]
        then(dve.tensor_reduce(amax, s3, AX.X, ALU.max, apply_absolute_value=True))
        then(dve.tensor_scalar(scale, amax, 1.0 / GRID_MAX, 1e-30, ALU.mult, ALU.max))
        then(dve.reciprocal(rscale, scale))
        then(dve.tensor_tensor(a3, s3, rscale.unsqueeze(2).to_broadcast(wide3), ALU.mult))
        then(dve.tensor_tensor(b_, a, a, ALU.mult))
        dve.tensor_scalar(c_, b_, 4.0, -4.0, ALU.is_ge, ALU.mult)
        then(dve.tensor_scalar(src, b_, 16.0, -2.0, ALU.is_ge, ALU.mult))
        then(dve.scalar_tensor_tensor(b_, c_, 8.0, src, ALU.add, ALU.add))
        then(dve.tensor_scalar(c_, c_, -1.0 / 32.0, 0.125, ALU.mult, ALU.add))
        then(dve.scalar_tensor_tensor(c_, src, -0.125, c_, ALU.mult, ALU.add))
        then(dve.tensor_tensor(a, a, b_, ALU.mult))
        then(dve.tensor_scalar(src, a, MAGIC, None, ALU.add))
        then(dve.tensor_scalar(src, src, MAGIC, None, ALU.subtract))
        then(dve.tensor_tensor(b_, src, a, ALU.subtract))
        then(dve.tensor_scalar(b_, b_, 0.5, None, ALU.is_ge))
        then(dve.tensor_tensor(src, src, b_, ALU.subtract))
        then(dve.tensor_tensor(src, src, c_, ALU.mult))
        then(dve.tensor_tensor(s3, s3, scale.unsqueeze(2).to_broadcast(wide3), ALU.mult))

    amax, scale, rscale = m1[:, 0:32], m2[:, 0:32], mm[:, 0:32]

    with stage(nc, "qw", "dc", "quant", "turned") as (block, dc, quant, turned):
        @block.vector
        def _(dve):
            then = chained(dve, dc)
            quantise(dve, then, xa[:, 0:KT, :], KT, xo[:, 0:KT, :], xh[:, 0:KT, :], x[:, 0:KT, :],
                     amax[:, 0:16], scale[:, 0:16], rscale[:, 0:16])
            dve.sem_inc(quant, 1)

        @block.tensor
        def _(pe):
            pe.wait_ge(quant, 1)
            for n in range(KT):
                for k in range(KT):
                    last = pe.transpose(psum[:, k, n * P:(n + 1) * P], xa[:, n, k * P:(k + 1) * P], ident[:, :])
            last.then_inc(turned, 1)

        @block.scalar
        def _(act):
            act.wait_ge(turned, 1)
            act.copy(wC[:, :, :], psum[:, 0:KT, 0:C])

    def norm(tag, src, dst=None, turns=(), gain=None, n=QT, width=C, also=None):
        kts = width // P
        names = ("dc", "ac", "var_ready", "rstd_ready", "normed", "turned", "raw_turned")
        with stage(nc, tag, *names) as (block, dc, ac, var_ready, rstd_ready, normed, turned, raw_turned):
            on_vector, on_pool = norm_stats(nc, tag, src, stats, mv, rstd, eps_var, nhalf, n,
                                            (dc, var_ready, rstd_ready))

            @block.gpsimd
            def _(pool):
                on_pool(pool)

            @block.vector
            def _(dve):
                then = chained(dve, dc)
                on_vector(dve, then)
                if also is not None:
                    dve.wait_ge(raw_turned, 1)
                for t in range(n):
                    ins = dve.tensor_scalar(dst[:, t, :], src[:, t, :], mv[:, t, 0:1], rstd[:, t:t + 1],
                                            ALU.subtract, ALU.mult)
                    if gain is None:
                        ins.then_inc(normed, 1)
                    else:
                        then(ins)
                        then(dve.tensor_tensor(dst[:, t, :], dst[:, t, :], gain[0], ALU.mult))
                        dve.tensor_tensor(dst[:, t, :], dst[:, t, :], gain[1], ALU.add).then_inc(normed, 1)

            def bank(t, k):
                i = t * kts + k if kts == 1 else k * n + t
                return psum[:, i // 4, (i % 4) * P:(i % 4 + 1) * P]

            def raw_bank(t):
                return psum[:, 4 + t // 4, (t % 4) * P:(t % 4 + 1) * P]

            if turns or also is not None:
                @block.tensor
                def _(pe):
                    if also is not None:
                        for t in range(n):
                            last = pe.transpose(raw_bank(t), src[:, t, :], ident[:, :])
                        last.then_inc(raw_turned, 1)
                    for t in range(n):
                        pe.wait_ge(normed, t + 1)
                        for k in range(kts):
                            last = pe.transpose(bank(t, k), dst[:, t, k * P:(k + 1) * P], ident[:, :])
                    last.then_inc(turned, 1)

                @block.scalar
                def _(act):
                    banks = n * kts // 4
                    if also is not None:
                        act.wait_ge(raw_turned, 1)
                        act.copy(also.rearrange("p k (a n) -> p (k a) n", n=BANK), psum[:, 4:4 + banks, :])
                    act.wait_ge(turned, 1)
                    per = banks // kts
                    for target, g, b_ in turns:
                        tv = target.rearrange("p k (a n) -> p k a n", n=BANK)
                        for k in range(kts):
                            src_ = psum[:, k * per:(k + 1) * per, :]
                            if g is None:
                                act.copy(tv[:, k], src_)
                            else:
                                act.activation(tv[:, k], src_, ACT.Identity, bias=b_[:, k:k + 1],
                                               scale=g[:, k:k + 1])

    def products(tag, jobs, before=None, start_wait=None, loading=None):
        on = {"act": [j for j in jobs if j[0] == "act"], "dve": [j for j in jobs if j[0] == "dve"]}
        place = {}
        for i, j in enumerate(jobs):
            place[i] = (j[0], sum(1 for k in jobs[:i + 1] if k[0] == j[0]))
        with stage(nc, tag, "summed", "act_free", "dve_free", "prepared", "pc") as (
                block, summed, act_free, dve_free, prepared, pc):
            free = {"act": act_free, "dve": dve_free}

            @block.tensor
            def _(pe):
                if start_wait is not None:
                    pe.wait_ge(*start_wait)
                for i, (_e, pairs, n, _f) in enumerate(jobs):
                    if i >= 8:
                        e, count = place[i - 8]
                        pe.wait_ge(free[e], count)
                    for k, (lhsT, rhs) in enumerate(pairs):
                        last = pe.matmul(psum[:, i % 8, 0:n], lhsT, rhs, start=(k == 0),
                                         stop=(k == len(pairs) - 1))
                    last.then_inc(summed, 1)

            def evacuate(eng, name):
                for i, (e, _p, n, f) in enumerate(jobs):
                    if e == name:
                        eng.wait_ge(summed, i + 1)
                        f(eng, psum[:, i % 8, 0:n]).then_inc(free[name], 1)

            @block.scalar
            def _(act):
                evacuate(act, "act")

            @block.vector
            def _(dve):
                if before is not None:
                    dve.wait_ge(prepared, 1)
                evacuate(dve, "dve")

            @block.gpsimd
            def _(pool):
                if before is not None:
                    before(pool, chained(pool, pc))
                    pool.sem_inc(prepared, 1)
            if loading is not None:
                @block.sync
                def _(sp):
                    loading(sp)

    ORDER = {("q", 16): "hmlhmh", ("k", 16): "hhhmml",
             ("q", 32): "hmhlmh", ("k", 32): "hhmhml"}
    ROWS = 96

    def view(first, heads, tiles, n):
        return stack[:, first:first + heads * tiles * n].rearrange("p (h a n) -> p h a n", h=heads, a=tiles)

    def operands(tag, ops, jobs, wait=None, pads=None):
        names = ("pad_ones", "pc", "projected", "biased", "high", "rest", "mid", "low", "parted",
                 "turned", "act_free", "dve_free", "summed", "act_out", "dve_out")
        n_ops = len(ops)
        fills = []
        last_fill = []
        for u, o in enumerate(ops):
            nh, nt, d = o["heads"], o["tiles"], o["d"]
            stg = parts[u % 2].rearrange("p (t h c) -> p t h c", t=nt, c=6 * d)[:, :, 0:nh, :] \
                if nt * nh * 6 * d == 6144 else \
                parts[u % 2][:, 0:nt * nh * 6 * d].rearrange("p (t h c) -> p t h c", t=nt, c=6 * d)
            o["stg"] = stg
            per = 8 // nt
            tiles = [(h, a) for h in range(nh) for a in range(d // 16)]
            for i in range(0, len(tiles), per):
                fills.append((u, stg, tiles[i:i + per], o))
            last_fill.append(len(fills))
        with stage(nc, tag, *names) as (block, pad_ones, pc, projected, biased, high, rest, mid, low, parted,
                                        turned, act_free, dve_free, summed, act_out, dve_out):
            def cols(o):
                return o["heads"] * o["d"]

            def bank(u):
                return psum[:, 2 * (u % 2):2 * (u % 2) + 2, :].rearrange("p a n -> p (a n)")

            def value(u):
                o = ops[u]
                if "value" in o:
                    return o["value"]
                return left(u) if o.get("bias") is not None else bank(u)[:, 0:o["tiles"] * cols(o)]

            def left(u):
                o = ops[u]
                if "value" in o:
                    return o["value"]
                buf = scr[:, :] if u % 2 == 0 else xo[:, :, :].rearrange("p t n -> p (t n)")
                return buf[:, 0:o["tiles"] * cols(o)]

            def slots(u, i, n=1):
                o = ops[u]
                d = o["d"]
                v = o["stg"].rearrange("p t h c -> p (t h) c")
                return v[:, :, i * d:(i + n) * d]

            def by_head(u, v):
                return v.rearrange("p (m d) -> p m d", d=ops[u]["d"])

            def at(u, part):
                o = ops[u]
                return [i for i, c in enumerate(ORDER[o["side"], o["d"]]) if c == part]

            def fill_target(f):
                u, stg, tiles, o = fills[f]
                nt, t0 = o["tiles"], o["first"]
                h, a = tiles[0]
                if o["d"] == 16:
                    return o["stack"][0:ROWS, h:h + len(tiles), 0, t0:t0 + nt * P]
                if len(tiles) == 1:
                    return o["stack"][0:ROWS, h, a, t0:t0 + nt * P]
                return o["stack"][0:ROWS, h, :, t0:t0 + nt * P]

            def fill_source(f):
                u, stg, tiles, o = fills[f]
                n = o["tiles"] * P
                v = psum[0:ROWS, 4 + f % 2, :].bitcast(BF16)[:, 0:len(tiles) * n]
                return v if len(tiles) == 1 else v.rearrange("p (a n) -> p a n", n=n)

            @block.tensor
            def _(pe):
                def project(u):
                    o = ops[u]
                    if "value" in o:
                        return
                    if u >= 2:
                        if ops[u - 2].get("bias") is None:
                            pe.wait_ge(rest, u - 1)
                        else:
                            pe.wait_ge(biased, u - 1)
                    w, c0, src = o["w"]
                    n = cols(o)
                    for t in range(o["tiles"]):
                        for k in range(w.shape[1]):
                            last = pe.matmul(bank(u)[:, t * n:(t + 1) * n],
                                             src[:, k, o["first"] + t * P:o["first"] + (t + 1) * P],
                                             w[:, k, c0:c0 + n], start=(k == 0), stop=(k == w.shape[1] - 1))
                    last.then_inc(projected, 1)

                if wait is not None:
                    pe.wait_ge(*wait)
                project(0)
                if n_ops > 1:
                    project(1)
                done = 0

                def some_jobs(upto):
                    nonlocal done
                    while done < min(upto, len(jobs)):
                        i = done
                        if i >= 2:
                            pe.wait_ge(act_out if i % 2 else dve_out, (i - 2) // 2 + 1)
                        _e, pairs, n, _f = jobs[i]
                        for k, (lhsT, rhs) in enumerate(pairs):
                            last = pe.matmul(psum[:, 6 + i % 2, 0:n], lhsT, rhs, start=(k == 0),
                                             stop=(k == len(pairs) - 1))
                        last.then_inc(summed, 1)
                        done += 1

                for u in range(n_ops):
                    some_jobs(-(-len(jobs) * (u + 1) // n_ops))
                    pe.wait_ge(parted, u + 1)
                    for f in range(last_fill[u - 1] if u else 0, last_fill[u]):
                        if f >= 2:
                            pe.wait_ge(act_free if f % 2 else dve_free, (f - 2) // 2 + 1)
                        _u, stg, tiles, o = fills[f]
                        nt, d = o["tiles"], o["d"]
                        out_ = psum[0:ROWS, 4 + f % 2, :].bitcast(BF16)
                        for i, (h, a) in enumerate(tiles):
                            for t in range(nt):
                                last = pe.transpose(out_[:, (i * nt + t) * P:(i * nt + t + 1) * P],
                                                    stg[:, t, h, a * ROWS:(a + 1) * ROWS], identb[:, :])
                        last.then_inc(turned, 1)
                    if u + 2 < n_ops:
                        project(u + 2)

            def evacuate_job(eng, i):
                eng.wait_ge(summed, i + 1)
                _e, _p, n, f = jobs[i]
                f(eng, psum[:, 6 + i % 2, 0:n]).then_inc(act_out if i % 2 else dve_out, 1)

            def evacuate_fill(eng, f):
                eng.wait_ge(turned, f + 1)
                if f % 2:
                    eng.copy(fill_target(f), fill_source(f)).then_inc(act_free, 1)
                else:
                    eng.tensor_copy(fill_target(f), fill_source(f)).then_inc(dve_free, 1)

            def share(u, odd):
                lo, hi = -(-len(jobs) * u // n_ops), -(-len(jobs) * (u + 1) // n_ops)
                return [i for i in range(lo, hi) if i % 2 == odd]

            def fills_of(u, odd):
                return [f for f in range(last_fill[u - 1] if u else 0, last_fill[u]) if f % 2 == odd]

            @block.scalar
            def _(act):
                def split(u):
                    o = ops[u]
                    if o.get("bias") is not None:
                        act.wait_ge(biased, u + 1)
                    elif "value" not in o:
                        act.wait_ge(projected, u + 1)
                    if u >= 2:
                        act.wait_ge(turned, last_fill[u - 2])
                    act.copy(slots(u, at(u, "h")[0]), by_head(u, value(u))).then_inc(high, 1)
                    act.wait_ge(rest, u + 1)
                    act.copy(slots(u, at(u, "m")[0]), by_head(u, left(u))).then_inc(mid, 1)

                split(0)
                for u in range(n_ops):
                    if u + 1 < n_ops:
                        split(u + 1)
                    for i in share(u, 1):
                        evacuate_job(act, i)
                    for f in fills_of(u, 1):
                        evacuate_fill(act, f)

            @block.vector
            def _(dve):
                def split(u):
                    o = ops[u]
                    if u >= 2:
                        dve.wait_ge(low, u - 1)
                    if o.get("bias") is not None:
                        dve.wait_ge(projected, u + 1)
                        n = cols(o)
                        v3 = bank(u)[:, 0:o["tiles"] * n].rearrange("p (t n) -> p t n", n=n)
                        dve.tensor_tensor(left(u).rearrange("p (t n) -> p t n", n=n), v3,
                                          o["bias"].unsqueeze(1).to_broadcast([P, o["tiles"], n]),
                                          ALU.add).then_inc(biased, 1)
                    else:
                        dve.sem_inc(biased, 1)
                    dve.wait_ge(high, u + 1)
                    dve.tensor_tensor(by_head(u, left(u)), by_head(u, value(u)), slots(u, at(u, "h")[0]),
                                      ALU.subtract).then_inc(rest, 1)
                    h = at(u, "h")
                    for i in h[1:]:
                        dve.tensor_copy(slots(u, i), slots(u, h[0]))
                    dve.wait_ge(mid, u + 1)
                    m = at(u, "m")
                    for i in m[1:]:
                        ins = dve.tensor_copy(slots(u, i), slots(u, m[0]))
                    ins.then_inc(pc, 1)
                    dve.wait_ge(pc, u + 1)
                    dve.wait_ge(low, u + 1)
                    dve.sem_inc(parted, 1)

                split(0)
                for u in range(n_ops):
                    if u + 1 < n_ops:
                        split(u + 1)
                    for i in share(u, 0):
                        evacuate_job(dve, i)
                    for f in fills_of(u, 0):
                        evacuate_fill(dve, f)

            @block.gpsimd
            def _(pool):
                if pads is not None:
                    pool.memset(pads.rearrange("p t (h w) -> p (t h) w", w=W)[:, :, D16:W], 1.0).then_inc(pad_ones, 1)
                    pool.wait_ge(pad_ones, 1)
                for o in ops:
                    if o["side"] == "k":
                        t0, n = o["first"], o["tiles"] * P
                        a = o["d"] // 16 - 1
                        pool.memset(o["stack"][ROWS:P, :, a, t0:t0 + n], 1.0).then_inc(pad_ones, 1)
                n_ones = (pads is not None) + sum(o["side"] == "k" for o in ops)
                pool.wait_ge(pad_ones, n_ones)
                for u in range(n_ops):
                    pool.wait_ge(mid, u + 1)
                    pool.tensor_tensor(slots(u, at(u, "l")[0]), by_head(u, left(u)), slots(u, at(u, "m")[0]),
                                       ALU.subtract).then_inc(low, 1)

    def values(dst, w, srcT, tiles):
        jobs = []
        kts = w.shape[1]
        for t in range(tiles):
            pairs = [(srcT[:, k, t * P:(t + 1) * P], w[:, k, :]) for k in range(kts)]

            def f(eng, bank, t=t):
                to = dst[:, t, :]
                if w.shape[2] == C:
                    to = to.rearrange("p (h w) -> p h w", w=W)[:, :, 0:D16]
                    bank = bank.rearrange("p (h w) -> p h w", w=D16)
                return eng.copy(to, bank) if eng is nc.scalar else eng.tensor_copy(to, bank)
            jobs.append(("act" if t % 2 else "dve", pairs, w.shape[2], f))
        return jobs

    def into_rows(dst, resid, lhs, w, n=C):
        jobs = []
        for t in range(QT):
            pairs = [(lhs[:, k, t * P:(t + 1) * P], w[:, k, :]) for k in range(w.shape[1])]

            def f(eng, bank, t=t):
                return eng.tensor_tensor(dst[:, t, :], bank, resid[:, t, :], ALU.add)
            jobs.append(("dve", pairs, n, f))
        return jobs

    def add_rows(dst, *parts):
        def before(pool, then):
            for part in parts:
                for t in range(QT):
                    p_ = part[:, t, :] if len(part.shape) == 3 else part
                    ins = pool.tensor_tensor(dst[:, t, :], dst[:, t, :], p_, ALU.add)
                then(ins)
        return before

    def row_maxima(tag, Q, K, n_keys, causal, op=ALU.max, dist=None):
        halves, hgs = n_keys // BANK, Q.shape[1] // J
        groups = [(g, t, h) for g in range(hgs) for t in range(QT) for h in range(halves)]
        hide = hide_above if op == ALU.max else hide_below
        nm, last_tile = hgs * QT * J, Q.shape[2] - 1
        with stage(nc, tag, "scored", "reduced", "dc", "padz", "split", "turned", "tiny", "tiny_back") as (
                block, scored, reduced, dc, padz, split, turned, tiny, tiny_back):
            @block.tensor
            def _(pe):
                for i, (g, t, h) in enumerate(groups):
                    n = (t + 1) * P if causal else BANK
                    base = (i % 2) * 4
                    if i >= 2:
                        pe.wait_ge(reduced, i - 1)
                    if causal:
                        for j in range(J):
                            pe.matmul(psum[:, base + j, t * P:(t + 1) * P], identb[:, :], hide[:, :],
                                      start=True, stop=False, skip_group_check=True)
                    for j in range(J):
                        hd = g * J + j
                        last = pe.matmul(psum[:, base + j, 0:n], Q[0:ROWS, hd, 0, t * P:(t + 1) * P],
                                         K[0:ROWS, hd, 0, h * BANK:h * BANK + n], start=not causal,
                                         stop=True, skip_group_check=True)
                    last.then_inc(scored, 1)
                pe.wait_ge(split, 1)
                for f in range(hgs * J // 2):
                    for i in range(2):
                        g, j = (2 * f + i) // J, (2 * f + i) % J
                        for t in range(QT):
                            last = pe.transpose(psum[ROWS:P, f, :].bitcast(BF16)[:, (i * QT + t) * P:(i * QT + t + 1) * P],
                                                mpad[:, (g * QT + t) * J + j, :], identb[:, :])
                    last.then_inc(turned, 1)

            @block.gpsimd
            def _(pool):
                pool.memset(mpad[:, 0:nm, :], 0.0).then_inc(padz, 1)

            def turn(eng, odd):
                for f in range(hgs * J // 2):
                    if f % 2 == odd:
                        eng.wait_ge(turned, f + 1)
                        src = psum[ROWS:P, f, :].bitcast(BF16).rearrange("p (a n) -> p a n", a=2)
                        dst = Q[ROWS:P, 2 * f:2 * f + 2, last_tile, :]
                        if odd:
                            eng.copy(dst, src)
                        else:
                            eng.tensor_copy(dst, src)

            @block.vector
            def _(dve):
                then = chained(dve, dc)
                for i, (g, t, h) in enumerate(groups):
                    n = (t + 1) * P if causal else BANK
                    base = (i % 2) * 4
                    dve.wait_ge(scored, i + 1)
                    dve.tensor_reduce(mx[:, h, g, t, :], psum[:, base:base + 4, 0:n], AX.X, op).then_inc(reduced, 1)
                dve.wait_ge(reduced, len(groups))
                m = mx[:, 0, 0:hgs, :, :].rearrange("p g t j -> p (g t j)")
                if halves == 2:
                    then(dve.tensor_tensor(mm[:, 0:nm], m, mx[:, 1, 0:hgs, :, :].rearrange("p g t j -> p (g t j)"), ALU.max))
                    m = mm[:, 0:nm]
                if dist is not None:
                    dist(dve, then, m, tiny, tiny_back)
                    m = mm[:, 0:nm]
                sign = -1.0 if dist is None else 1.0
                then(dve.tensor_copy(mb[:, 0, 0:nm], m))
                then(dve.tensor_tensor(m1[:, 0:nm], m, mb[:, 0, 0:nm], ALU.subtract))
                then(dve.tensor_copy(mb[:, 1, 0:nm], m1[:, 0:nm]))
                then(dve.tensor_tensor(m2[:, 0:nm], m1[:, 0:nm], mb[:, 1, 0:nm], ALU.subtract))
                then(dve.tensor_copy(mb[:, 2, 0:nm], m2[:, 0:nm]))
                dve.wait_ge(padz, 1)
                for i in range(3):
                    ins = dve.tensor_scalar(mpad[:, 0:nm, i], mb[:, i, 0:nm], sign, None, ALU.mult)
                ins.then_inc(split, 1)
                turn(dve, 0)

            @block.scalar
            def _(act):
                if dist is not None:
                    act.preload_act_table_set("natural_log_exp_and_others")
                    act.wait_ge(tiny, 1)
                    act.activation(m2[:, :], m2[:, :], ACT.Ln).then_inc(tiny_back, 1)
                    act.wait_ge(tiny_back, 1)
                    act.activation(m2[:, :], m2[:, :], ACT.Exp, scale=0.5).then_inc(tiny_back, 1)
                    act.wait_ge(tiny, 2)
                    act.activation(m1[:, :], m1[:, :], ACT.Ln, bias=1.0).then_inc(tiny_back, 1)
                turn(act, 1)

    def attention(tag, Q, K, vals, n_keys, scale, g0=0, causal=False, anti=False, add=None, loading=None):
        kts, halves = n_keys // P, n_keys // BANK
        hgs, tiles = Q.shape[1] // J, Q.shape[2]
        order = list(range(kts))[::-1] if anti else list(range(kts))
        steps = [(g, k) for g in range(hgs) for k in order]
        padded = tiles == 1
        acc = parts2[:, 0:4096].bitcast(F32).rearrange("p (s a n) -> p s a n", s=2, a=2)
        units = [(t, j, h) for t in range(QT) for j in range(J) for h in range(halves)]
        NU, nm = len(units), QT * J
        pad = scr[:, 0:nm * W // 2].bitcast(BF16).rearrange("p (m w) -> p m w", w=W)
        found = scr[:, nm * W // 2:nm * W // 2 + 2 * nm]
        left1, left2 = (scr[:, nm * (W // 2 + 2 + i):nm * (W // 2 + 3 + i)] for i in range(2))
        three = scr[:, nm * (W // 2 + 4):nm * (W // 2 + 4) + 3 * nm // 2].bitcast(BF16).rearrange(
            "p (i m) -> p i m", i=3)

        def share(s):
            return range(NU * s // (kts - 1), NU * (s + 1) // (kts - 1))

        def unit_bank(g, u):
            return psum[:, 4 + u % 2 if g else u % 6, :]

        def first_query(k):
            return k * P if causal else 0

        with stage(nc, tag, "scored", "exped", "masked", "weighed", "dc", "added", "pool_added", "lifted",
                   "gathered", "inverted", "spread_in", "divided", "measured", "reduced", "padz", "split", "turned", "rows_in") as (
                block, scored, exped, masked, weighed, dc, added, pool_added, lifted,
                gathered, inverted, spread_in, divided, measured, reduced, padz, split, turned, rows_in):
            if loading is not None:
                @block.sync
                def _(sp):
                    loading(sp)

            @block.tensor
            def _(pe):
                def measure(g, u):
                    t, j, h = units[u]
                    n, i = (t + 1) * P if causal else BANK, g * NU + u
                    ring = 2 if g else 6
                    if u >= ring:
                        pe.wait_ge(reduced, i - ring + 1)
                    bank = unit_bank(g, u)
                    if causal:
                        pe.matmul(bank[:, t * P:(t + 1) * P], identb[:, :], hide_above[:, :],
                                  start=True, stop=False, skip_group_check=True)
                    pe.matmul(bank[:, 0:n], Q[0:ROWS, g * J + j, 0, t * P:(t + 1) * P],
                              K[0:ROWS, g * J + j, 0, h * BANK:h * BANK + n], start=not causal,
                              stop=True, skip_group_check=True).then_inc(measured, 1)

                def turn_maxima(g):
                    pe.wait_ge(split, g + 1)
                    for j in range(J):
                        for t in range(QT):
                            last = pe.transpose(psum[ROWS:P, 4 + j // 2, :].bitcast(BF16)[
                                :, ((j % 2) * QT + t) * P:((j % 2) * QT + t + 1) * P], pad[:, t * J + j, :], identb[:, :])
                    last.then_inc(turned, 1)

                def score(n, between=()):
                    g, k = steps[n]
                    q0 = first_query(k)
                    if n % kts == 0:
                        pe.wait_ge(rows_in, g + 1)
                    for p in range(2):
                        for u in between[p:p + 1]:
                            measure(g + 1, u)
                        i = 2 * n + p
                        if i >= 2:
                            pe.wait_ge(exped, i - 1)
                        for jj in range(2):
                            hd = g * J + 2 * p + jj
                            for a in range(tiles):
                                r = P if a == tiles - 1 else ROWS
                                last = pe.matmul(psum[:, 2 * p + jj, q0:T], K[0:r, hd, a, k * P:(k + 1) * P],
                                                 Q[0:r, hd, a, q0:T], start=(a == 0), stop=(a == tiles - 1))
                        last.then_inc(scored, 1)

                def weigh(n):
                    g, k = steps[n]
                    q0 = first_query(k)
                    first, final = k == order[0], k == order[-1]
                    pe.wait_ge(exped, 2 * n + 2)
                    if causal or anti:
                        pe.wait_ge(masked, 2 * n + 2)
                    if first and g >= 2:
                        pe.wait_ge(divided, g - 1)
                    for j in range(J):
                        c = (g0 + g) * P + W * j
                        lhsT = vals[:, k, c:c + W]
                        slot = (2 * n + j // 2) % 4
                        o = psum[W * j:W * j + W, 6 + g % 2, :]
                        if anti:
                            if k:
                                pe.matmul(o[:, 0:k * P], lhsT, prob[:, slot, j % 2, 0:k * P],
                                          start=first, stop=False, skip_group_check=True)
                            last = pe.matmul(o[:, k * P:(k + 1) * P], lhsT, pm[:, slot, j % 2, :],
                                             start=False, stop=final, skip_group_check=True)
                        else:
                            last = pe.matmul(o[:, q0:T], lhsT, prob[:, slot, j % 2, q0:T],
                                             start=first, stop=final, skip_group_check=True)
                    last.then_inc(weighed, 1)

                def gather(g):
                    pe.wait_ge(lifted, g + 1)
                    if padded:
                        gather_sums(pe, g, gathered)
                        return
                    for j in range(J):
                        last = pe.matmul(psum[W * j:W * j + W, 6 + g % 2, :], ones_f[:, :],
                                         acc[:, j // 2, j % 2, :], start=True, stop=True)
                    last.then_inc(gathered, 1)

                for u in range(NU):
                    measure(0, u)
                turn_maxima(0)
                score(0)
                for n in range(len(steps)):
                    g, s = divmod(n, kts)
                    mine = share(s) if g + 1 < hgs and s < kts - 1 else range(0)
                    if s < kts - 1:
                        score(n + 1, mine)
                    if s == 0 and g:
                        gather(g - 1)
                    after = -(-len(mine[2:]) // 2)
                    for u in mine[2:2 + after]:
                        measure(g + 1, u)
                    if s == kts - 1 and g + 1 < hgs:
                        turn_maxima(g + 1)
                    weigh(n)
                    for u in mine[2 + after:]:
                        measure(g + 1, u)
                    if s == 0 and g and padded:
                        spread_inverses(pe, g - 1, inverted, spread_in)
                    if s == kts - 1 and g + 1 < hgs:
                        score(n + 1)
                gather(hgs - 1)
                if padded:
                    spread_inverses(pe, hgs - 1, inverted, spread_in)

            @block.scalar
            def _(act):
                for n, (g, k) in enumerate(steps):
                    q0 = first_query(k)
                    for p in range(2):
                        i = 2 * n + p
                        act.wait_ge(scored, i + 1)
                        if n >= 2:
                            act.wait_ge(weighed, n - 1)
                            if not padded:
                                act.wait_ge(pool_added if p else added, n - 1)
                        act.activation(prob[:, i % 4, :, q0:T], psum[:, 2 * p:2 * p + 2, q0:T], ACT.Exp,
                                       scale=scale).then_inc(exped, 1)

            def accumulate(eng, n, p, sem):
                if n % kts == 0:
                    if n:
                        eng.wait_ge(gathered, n // kts)
                    eng.tensor_copy(acc[:, p], prob[:, (2 * n + p) % 4]).then_inc(sem, 1)
                else:
                    eng.wait_ge(sem, n)
                    eng.tensor_tensor(acc[:, p], acc[:, p], prob[:, (2 * n + p) % 4], ALU.add).then_inc(sem, 1)

            @block.gpsimd
            def _(pool):
                pool.memset(pad[:, :, :], 0.0).then_inc(padz, 1)
                for n, (g, k) in enumerate(steps):
                    if causal or anti:
                        for p in range(2):
                            i = 2 * n + p
                            pool.wait_ge(exped, i + 1)
                            if anti and n >= 2:
                                pool.wait_ge(weighed, n - 1)
                            d = prob[:, i % 4, :, k * P:(k + 1) * P]
                            if causal:
                                pool.affine_select(d, d, [[0, 2], [1, P]], ALU.is_ge, 0.0, base=0,
                                                   channel_multiplier=-1).then_inc(masked, 1)
                            else:
                                pool.affine_select(pm[:, i % 4, :, :], d, [[0, 2], [-1, P]], ALU.is_gt, 0.0,
                                                   base=0, channel_multiplier=1).then_inc(masked, 1)
                    if not padded:
                        pool.wait_ge(exped, 2 * n + 2)
                        accumulate(pool, n, 1, pool_added)

            @block.vector
            def _(dve):
                then = chained(dve, dc)

                def reduce(g, u):
                    t, j, h = units[u]
                    n, i = (t + 1) * P if causal else BANK, g * NU + u
                    dve.wait_ge(measured, i + 1)
                    c = h * nm + t * J + j
                    dve.tensor_reduce(found[:, c:c + 1], unit_bank(g, u)[:, 0:n], AX.X, ALU.max).then_inc(reduced, 1)

                def split_maxima(g):
                    dve.wait_ge(reduced, (g + 1) * NU)
                    m = found[:, 0:nm]
                    if halves == 2:
                        then(dve.tensor_tensor(m, m, found[:, nm:2 * nm], ALU.max))
                    then(dve.tensor_copy(three[:, 0, :], m))
                    then(dve.tensor_tensor(left1, m, three[:, 0, :], ALU.subtract))
                    then(dve.tensor_copy(three[:, 1, :], left1))
                    then(dve.tensor_tensor(left2, left1, three[:, 1, :], ALU.subtract))
                    then(dve.tensor_copy(three[:, 2, :], left2))
                    if g == 0:
                        dve.wait_ge(padz, 1)
                    dve.tensor_scalar(pad[:, :, 0:3], three[:, :, :].rearrange("p i m -> p m i"), -1.0, None,
                                      ALU.mult).then_inc(split, 1)

                def finish(g):
                    if padded:
                        divide(dve, then, g, spread_in, divided, g0, add)
                        return
                    dve.wait_ge(gathered, g + 1)
                    then(dve.reciprocal(rs[:, :], psum[:, 6 + g % 2, :]))
                    dve.tensor_tensor(yT[:, g0 + g, :], ob[:, :], rs[:, :], ALU.mult).then_inc(divided, 1)
                    dve.wait_ge(divided, g + 1)

                def take_rows(g):
                    dve.wait_ge(turned, g + 1)
                    for i in range(2):
                        ins = dve.tensor_copy(Q[ROWS:P, g * J + 2 * i:g * J + 2 * i + 2, tiles - 1, :],
                                              psum[ROWS:P, 4 + i, :].bitcast(BF16).rearrange("p (a n) -> p a n", a=2))
                    ins.then_inc(rows_in, 1)

                for u in range(NU):
                    reduce(0, u)
                split_maxima(0)
                take_rows(0)
                for n in range(len(steps)):
                    g, s = divmod(n, kts)
                    mine = share(s) if g + 1 < hgs and s < kts - 1 else range(0)
                    for u in mine[:2]:
                        reduce(g + 1, u)
                    if s == 0 and g and padded:
                        invert(dve, g - 1, gathered, inverted)
                    for u in mine[2:]:
                        reduce(g + 1, u)
                    if s == 0 and g:
                        finish(g - 1)
                    if g + 1 < hgs:
                        if s == kts - 2:
                            split_maxima(g + 1)
                        if s == kts - 1:
                            take_rows(g + 1)
                    if not padded:
                        dve.wait_ge(exped, 2 * n + 1)
                        accumulate(dve, n, 0, added)
                    if s == kts - 1:
                        dve.wait_ge(weighed, n + 1)
                        if not padded:
                            dve.wait_ge(added, n + 1)
                            dve.wait_ge(pool_added, n + 1)
                        dve.tensor_copy(ob[:, :], psum[:, 6 + g % 2, :]).then_inc(lifted, 1)
                if padded:
                    invert(dve, hgs - 1, gathered, inverted)
                finish(hgs - 1)

    def gather_sums(pe, g, gathered):
        for t in range(QT):
            last = pe.matmul(psum[:, 6 + g % 2, t * J:(t + 1) * J], ob[:, t * P:(t + 1) * P], pads_of[:, :],
                             start=True, stop=True, skip_group_check=True)
        last.then_inc(gathered, 1)

    def invert(dve, g, gathered, inverted):
        dve.wait_ge(gathered, g + 1)
        dve.reciprocal(inverse[:, :], psum[:, 6 + g % 2, 0:QT * J]).then_inc(inverted, 1)
        dve.wait_ge(inverted, 2 * g + 1)
        dve.tensor_copy(rs.rearrange("p (m w) -> p m w", w=W),
                        inverse[:, :].unsqueeze(2).to_broadcast([P, QT * J, W])).then_inc(inverted, 1)

    def spread_inverses(pe, g, inverted, spread_in):
        pe.wait_ge(inverted, 2 * g + 2)
        for t in range(QT):
            last = pe.matmul(psum[:, 6 + g % 2, t * P:(t + 1) * P], rs[:, t * P:(t + 1) * P], ident[:, :],
                             start=True, stop=True, skip_group_check=True)
        last.then_inc(spread_in, 1)

    def divide(dve, then, g, spread_in, divided, g0=0, add=None):
        bank = psum[:, 6 + g % 2, :]
        dve.wait_ge(spread_in, g + 1)
        if add is None:
            dve.tensor_tensor(yT[:, g0 + g, :], ob[:, :], bank, ALU.mult).then_inc(divided, 1)
        else:
            then(dve.tensor_tensor(ob[:, :], ob[:, :], bank, ALU.mult))
            dve.scalar_tensor_tensor(yT[:, g0 + g, :], ob[:, :], add[:, g0 + g:g0 + g + 1],
                                     yT[:, g0 + g, :], ALU.add, ALU.add).then_inc(divided, 1)
        dve.wait_ge(divided, g + 1)

    e = Shared()
    e.Ccol, e.R, e.ROWS, e.V, e.Vc, e.add_rows, e.amax = \
        Ccol, R, ROWS, V, Vc, add_rows, amax
    e.attention, e.avg, e.bA, e.bD, e.cT, e.cnT, e.colB = \
        attention, avg, bA, bD, cT, cnT, colB
    e.dram, e.hT, e.ident, e.into_rows, e.load_qkv, e.m1, e.m2 = \
        dram, hT, ident, into_rows, load_qkv, m1, m2
    e.mlp_loaded, e.mm, e.nc, e.norm, e.ob, e.gather_sums, e.invert, e.spread_inverses, e.divide, e.operands = \
        mlp_loaded, mm, nc, norm, ob, gather_sums, invert, spread_inverses, divide, operands
    e.parts2, e.prob, e.products, e.psum,  e.quantise, e.row_maxima = \
        parts2, prob, products, psum, quantise, row_maxima
    e.q_stack, e.rs, e.rscale, e.scal, e.scale, e.slot_loaded, e.sm, e.small = \
        q_stack, rs, rscale, scal, scale, slot_loaded, sm, small
    e.values, e.vbig, e.view, e.w1k, e.w1q, e.w1v, e.w2k = \
        values, vbig, view, w1k, w1q, w1v, w2k
    e.w2q, e.w2v, e.wA, e.wBck, e.wBcq, e.wBcv, e.wBk = \
        w2q, w2v, wA, wBck, wBcq, wBcv, wBk
    e.wBp, e.wBq, e.wBv, e.wC, e.wD, e.wDo, e.w_li1 = \
        wBp, wBq, wBv, wC, wD, wDo, w_li1
    e.w_li2, e.w_li3, e.w_sur, e.work, e.x, e.x5, e.xT = \
        w_li2, w_li3, w_sur, work, x, x5, xT
    e.xa, e.xh, e.xo, e.yT, e.yT2 = \
        xa, xh, xo, yT, yT2
    with nc.Fori(0, B) as b:
        batch(e, b)
    with stage(nc, "after", "unused") as (block, _u):
        @block.sync
        def _(sp):
            sp.wait_ge(slot_loaded, 48)


def batch(e, b):
    nc, dram, psum, R, Ccol, ident = e.nc, e.dram, e.psum, e.R, e.Ccol, e.ident
    x, xh, xa, xo, xT, yT2, yT = e.x, e.xh, e.xa, e.xo, e.xT, e.yT2, e.yT
    one = bass.ds(b, 1)
    context = e.prob[:, 0, :, :].rearrange("p a (t n) -> p (a t) n", n=CC)
    cn = e.prob[:, 1, :, :].rearrange("p a (t n) -> p (a t) n", n=CC)

    with stage(nc, "in", "rows_in") as (block, rows_in):
        @block.sync
        def _(sp):
            sp.dma_start(x[:, :, :], dram["x"][one].rearrange("o (t p) c -> p (o t) c", p=P)).then_inc(rows_in, 16)
            sp.dma_start(context[:, :, :], dram["ctx_512"][one].rearrange("o (t p) c -> p (o t) c", p=P)).then_inc(rows_in, 16)
            sp.wait_ge(rows_in, 32)

    a2 = "L1_xattn_a2_"
    e.norm("nctx", context, cn, turns=[(e.cnT, Ccol[a2 + "lny_g"], Ccol[a2 + "lny_b"])], n=CT, width=CC,
           also=e.cT)

    landmark_attention(e)
    standard_attention(e)
    fp6_linear(e)
    hyperbolic_attention(e)

    e.norm("n5", x, xh)
    e.norm("n6", xh, xa, gain=(R["L1_xattn_ln1_g"], R["L1_xattn_ln1_b"]))
    a1 = "L1_xattn_a1_"
    e.norm("n7", xa, xh, turns=[(xT, Ccol[a1 + "lnx_g"], Ccol[a1 + "lnx_b"]),
                                (yT2, Ccol[a1 + "lny_g"], Ccol[a1 + "lny_b"])])
    for c in range(2):
        Q, K = e.view(0, 8, 2, T), e.view(8192, 8, 2, T)
        e.operands(f"e1p{c}", [
            {"side": "q", "d": W, "heads": 8, "tiles": QT, "w": (e.w1q, 256 * c, xT), "stack": Q, "first": 0},
            {"side": "k", "d": W, "heads": 8, "tiles": QT, "w": (e.w1k, 256 * c, yT2), "stack": K, "first": 0}],
            e.values(e.V, e.w1v, yT2, QT) if c == 0 else [], wait=(e.slot_loaded, 96) if c == 0 else None)
        if c == 0:
            clear(nc, e.slot_loaded)
        e.attention(f"e1a{c}", Q, K, e.V, T, W ** -0.5, g0=2 * c, anti=True,
                 loading=(lambda sp: e.load_qkv(sp, 2)) if c == 1 else None)
    mlp_unit(e, 1, xa)
    e.norm("n9", xa, xa, gain=(R["L1_xattn_ln2_g"], R["L1_xattn_ln2_b"]))
    e.norm("n10", xa, xh, turns=[(xT, Ccol[a2 + "lnx_g"], Ccol[a2 + "lnx_b"])])
    for c in range(2):
        Q = e.q_stack.rearrange("p (h a n) -> p h a n", h=8, a=2)
        K = e.view(0, 8, 2, TC)
        e.operands(f"e2p{c}", [
            {"side": "q", "d": W, "heads": 8, "tiles": QT, "w": (e.w2q, C * c, xT), "stack": Q, "first": 0}] + [
            {"side": "k", "d": W, "heads": 8, "tiles": QT, "w": (e.w2k, C * c, e.cnT), "stack": K, "first": f}
            for f in (0, T)],
            e.values(e.Vc, e.w2v, e.cnT, CT) if c == 0 else [], wait=(e.slot_loaded, 64) if c == 0 else None)
        if c == 0:
            clear(nc, e.slot_loaded)
        e.attention(f"e2a{c}", Q, K, e.Vc, TC, W ** -0.5, g0=2 * c,
                    loading=(lambda sp: e.load_qkv(sp, 0)) if c == 1 else None)
    mlp_unit(e, 2, x)

    with stage(nc, "out", "stored") as (block, stored):
        @block.sync
        def _(sp):
            sp.dma_start(e.x5[one].rearrange("o p t c -> p (o t) c"), x[:, :, :]).then_inc(stored, 16)
            sp.wait_ge(stored, 16)


def clear(nc, sem):
    nc.all_engine_barrier(sems_to_clear=range(sem.num, sem.num + 1))


def load_mlp(e, eng, i):
    eng.dma_start(e.w_li2[:, :, :], e.dram[f"L1_xattn_a{i}_li2_w"].rearrange("(k p) n -> p k n", p=P)).then_inc(e.mlp_loaded, 16)
    eng.dma_start(e.w_li3[:, :, :], e.dram[f"L1_xattn_a{i}_li3_w"].rearrange("(k p) n -> p k n", p=P)).then_inc(e.mlp_loaded, 16)


def mlp_unit(e, i, target):
    nc, Ccol, R = e.nc, e.Ccol, e.R
    a = f"L1_xattn_a{i}_"
    w_li1, xo, xa, xT = e.w_li1[i - 1], e.xo, e.xa, e.xT

    def copy_first(pool, then):
        for t in range(QT):
            ins = pool.tensor_tensor(xo[:, t, :], xa[:, t, :], R[a + "li1_b"], ALU.add)
        then(ins)
    e.products(f"u{i}o", e.into_rows(xo, xo, e.yT, w_li1), before=copy_first,
               loading=(lambda sp: load_mlp(e, sp, 2)) if i == 2 else None)
    e.norm(f"u{i}n", xo, e.xh, turns=[(xT, Ccol[a + "ln3_g"], Ccol[a + "ln3_b"])])
    jobs = []
    for f in range(FT):
        pairs = [(e.w_li2[:, k, f * P:(f + 1) * P], xT[:, k, :]) for k in range(KT)]

        def gelu(eng, bank, f=f):
            return eng.activation(e.hT[:, f, :], bank, ACT.Gelu, bias=Ccol[a + "li2_b"][:, f:f + 1])
        jobs.append(("act", pairs, T, gelu))
    e.products(f"u{i}h", jobs, start_wait=(e.mlp_loaded, 32))
    clear(nc, e.mlp_loaded)
    parts = [xa, R[a + "li3_b"]] + ([e.x] if target is e.x else [])
    e.products(f"u{i}y", e.into_rows(target, xo, e.hT, e.w_li3), before=e.add_rows(xo, *parts))


def landmark_attention(e):
    nc, psum, x, ident = e.nc, e.psum, e.x, e.ident
    L = 64
    qkv = e.vbig[:, 0:QT * 3 * C].rearrange("p (t n) -> p t n", t=QT)
    k3 = e.yT[:, 0:2, :].rearrange("p a (t n) -> p (a t) n", n=C)
    qkT = e.work[:, 0:4 * T].rearrange("p (a n) -> p a n", a=4)
    qAT, kAT = qkT[:, 0:KT, :], qkT[:, KT:2 * KT, :]
    klT = e.work[:, 2048:2048 + KT * L].rearrange("p (k n) -> p k n", k=KT)
    k2T = e.work[:, 2304:2304 + QT * L].rearrange("p (t n) -> p t n", t=QT)
    mid = e.work[0:L, 2560:2560 + C]
    k1T = e.work[0:L, 3072:3072 + T]
    mxq, sums = e.small[:, 0:8], e.small[:, 8:16]

    e.norm("n1", x, e.xh, turns=[(e.xT, None, None)])
    jobs = []
    for t in range(QT):
        for n0, n in ((0, 2 * C), (2 * C, C)):
            pairs = [(e.xT[:, k, t * P:(t + 1) * P], e.wA[:, k, n0:n0 + n]) for k in range(KT)]

            def f(eng, bank, t=t, n0=n0, n=n):
                return eng.tensor_tensor(qkv[:, t, n0:n0 + n], bank, e.bA[:, n0:n0 + n], ALU.add)
            jobs.append(("dve", pairs, n, f))

    e.products("Ap", jobs, start_wait=(e.slot_loaded, 48))
    clear(nc, e.slot_loaded)

    with stage(nc, "Asm", "maxed", "exped", "dc", "soft", "turned", "copied", "lm", "lm_in", "k2",
               "k2_in", "k1_in", "md", "md_in", "fin") as (
            block, maxed, exped, dc, soft, turned, copied, lm, lm_in, k2, k2_in, k1_in, md, md_in, fin):
        def half(t, i):
            return qkv[:, t, i * C:(i + 1) * C]

        @block.sync
        def _(sp):
            e.load_qkv(sp, 1)

        @block.vector
        def _(dve):
            then = chained(dve, dc)
            for t in range(QT):
                ins = dve.tensor_reduce(mxq[:, 2 * t:2 * t + 2],
                                        qkv[:, t, 0:2 * C].rearrange("p (i n) -> p i n", i=2), AX.X, ALU.max,
                                        negate=True)
            ins.then_inc(maxed, 1)
            dve.wait_ge(exped, 8)
            then(dve.reciprocal(sums, sums))
            for t in range(QT):
                for i in range(2):
                    ins = dve.tensor_scalar(half(t, i), half(t, i), sums[:, 2 * t + i:2 * t + i + 1], None, ALU.mult)
                ins.then_inc(soft, 1)
            dve.wait_ge(soft, QT)
            for t in range(QT):
                ins = dve.tensor_tensor(k3[:, t, :], half(t, 1), half(t, 2), ALU.mult)
            then(ins)
            dve.wait_ge(lm, 1)
            dve.tensor_copy(klT, psum[:, 4, 0:KT * L].rearrange("p (k n) -> p k n", k=KT)).then_inc(lm_in, 1)
            dve.wait_ge(k2, 1)
            dve.tensor_copy(k2T, psum[:, 5, 0:QT * L].rearrange("p (t n) -> p t n", t=QT)).then_inc(k2_in, 1)
            dve.wait_ge(md, 1)
            dve.tensor_copy(mid, psum[0:L, 7, 0:C]).then_inc(md_in, 1)
            for t in range(QT):
                dve.wait_ge(fin, t + 1)
                dve.tensor_tensor(x[:, t, :], psum[:, t, 0:C], x[:, t, :], ALU.add)

        @block.scalar
        def _(act):
            act.wait_ge(maxed, 1)
            for t in range(QT):
                for i in range(2):
                    c = 2 * t + i
                    act.activation(half(t, i), half(t, i), ACT.Exp, bias=mxq[:, c:c + 1],
                                   accum_out=sums[:, c:c + 1]).then_inc(exped, 1)
            act.wait_ge(turned, 1)
            act.copy(qkT, psum[:, 0:4, :]).then_inc(copied, 1)
            act.wait_ge(k2, 1)
            act.copy(k1T, psum[0:L, 6, 0:T]).then_inc(k1_in, 1)

        @block.tensor
        def _(pe):
            for t in range(QT):
                pe.wait_ge(soft, t + 1)
                for i in range(2):
                    for k in range(KT):
                        last = pe.transpose(psum[:, i * KT + k, t * P:(t + 1) * P],
                                            qkv[:, t, i * C + k * P:i * C + (k + 1) * P], ident[:, :])
            last.then_inc(turned, 1)
            for t in range(QT):
                for k in range(KT):
                    last = pe.matmul(psum[:, 4, k * L + 16 * t:k * L + 16 * t + 16],
                                     qkv[:, t, C + k * P:C + (k + 1) * P], e.avg[:, :],
                                     start=(t == 0 and k == 0), stop=True, skip_group_check=True)
            last.then_inc(lm, 1)
            pe.wait_ge(lm_in, 1)
            pe.wait_ge(copied, 1)
            for k in range(KT):
                pe.matmul(psum[0:L, 6, :], klT[:, k, :], qAT[:, k, :], start=(k == 0), stop=(k == KT - 1))
            for t in range(QT):
                for k in range(KT):
                    last = pe.matmul(psum[:, 5, t * L:(t + 1) * L], kAT[:, k, t * P:(t + 1) * P], klT[:, k, :],
                                     start=(t == 0 and k == 0), stop=(k == KT - 1), skip_group_check=True)
            last.then_inc(k2, 1)
            pe.wait_ge(k2_in, 1)
            for t in range(QT):
                last = pe.matmul(psum[0:L, 7, 0:C], k2T[:, t, :], k3[:, t, :], start=(t == 0), stop=(t == QT - 1))
            last.then_inc(md, 1)
            pe.wait_ge(md_in, 1)
            pe.wait_ge(k1_in, 1)
            for t in range(QT):
                pe.matmul(psum[:, t, 0:C], k1T[:, t * P:(t + 1) * P], mid, start=True, stop=True).then_inc(fin, 1)


def standard_attention(e):
    x, xT, V, Vc, colB, R = e.x, e.xT, e.V, e.Vc, e.colB, e.R
    e.norm("n2", x, e.xh, turns=[(xT, None, None)])
    Q, K = e.view(0, H, 1, T), e.view(8192, H, 1, T)
    e.operands("Bp", [
        {"side": "q", "d": D16, "heads": H, "tiles": QT, "w": (e.wBq, 0, xT), "bias": R["L0_xattn_bq"],
         "stack": Q, "first": 0},
        {"side": "k", "d": D16, "heads": H, "tiles": QT, "w": (e.wBk, 0, xT), "bias": R["L0_xattn_bk"],
         "stack": K, "first": 0}], e.values(V, e.wBv, xT, QT), pads=V)
    e.attention("Ba", Q, K, V, T, D16 ** -0.5, causal=True)
    with stage(e.nc, "Bb", "unused") as (block, _u):
        @block.vector
        def _(dve):
            dve.tensor_tensor(e.small[:, 0:HG], colB[:, 0, :], colB[:, 1, :], ALU.add)
    Q = e.q_stack.rearrange("p (h a n) -> p h a n", h=H, a=1)
    K = e.view(0, H, 1, TC)
    e.operands("Bc", [
        {"side": "q", "d": D16, "heads": H, "tiles": QT, "w": (e.wBcq, 0, xT), "bias": R["L0_xattn_bcq"],
         "stack": Q, "first": 0}] + [
        {"side": "k", "d": D16, "heads": H, "tiles": QT, "w": (e.wBck, 0, e.cT), "bias": R["L0_xattn_bck"],
         "stack": K, "first": f} for f in (0, T)], e.values(Vc, e.wBcv, e.cT, CT), pads=Vc)
    e.attention("Bca", Q, K, Vc, TC, D16 ** -0.5, add=e.small[:, 0:HG])
    e.products("Bo", e.into_rows(x, x, e.yT, e.wBp), before=e.add_rows(x, e.R["L0_xattn_bp"]),
               loading=lambda sp: load_mlp(e, sp, 1))


def fp6_linear(e):
    nc, psum, x, xh = e.nc, e.psum, e.x, e.xh
    e.norm("n3", x, xh)
    sc = [e.vbig[:, i * QT * C:(i + 1) * QT * C].rearrange("p (t n) -> p t n", t=QT) for i in range(3)]
    with stage(nc, "Cq", "dc", "quant", "turned") as (block, dc, quant, turned):
        @block.vector
        def _(dve):
            then = chained(dve, dc)
            e.quantise(dve, then, xh[:, :, :], QT, *sc, e.amax, e.scale, e.rscale)
            dve.sem_inc(quant, 1)

        @block.tensor
        def _(pe):
            pe.wait_ge(quant, 1)
            for t in range(QT):
                for k in range(KT):
                    last = pe.transpose(psum[:, k, t * P:(t + 1) * P], xh[:, t, k * P:(k + 1) * P], e.ident[:, :])
            last.then_inc(turned, 1)

        @block.scalar
        def _(act):
            act.wait_ge(turned, 1)
            act.copy(e.xT[:, :, :], psum[:, 0:KT, :])
    e.products("Co", e.into_rows(x, x, e.xT, e.wC), before=e.add_rows(x, e.R["L0_ffn_bias"]))


def hyperbolic_attention(e):
    nc, psum, x, xh, ident = e.nc, e.psum, e.x, e.xh, e.ident
    V = e.V
    e.norm("n4", x, xh, turns=[(e.xT, None, None)])
    qkp = [e.cT[:, 0, :].rearrange("p (t n) -> p t n", t=QT), e.xo[:, :, :]]
    raw = e.prob[:, :, :, :].rearrange("p a b n -> p (a b n)")[:, 0:QT * 3 * C].rearrange("p (t n) -> p t n", t=QT)
    imp, spike = e.small[:, 0:4], e.small[:, 4:8]
    jobs = []
    for t in range(QT):
        for n0, n in ((0, 2 * C), (2 * C, C)):
            pairs = [(e.xT[:, k, t * P:(t + 1) * P], e.wD[:, k, n0:n0 + n]) for k in range(KT)]

            def f(eng, bank, t=t, n0=n0, n=n):
                return eng.tensor_tensor(raw[:, t, n0:n0 + n], bank, e.bD[:, n0:n0 + n], ALU.add)
            jobs.append(("dve", pairs, n, f))

    def fill_pads(pool, then):
        then(pool.memset(V[:, :, :], 1.0))
    e.products("Dp", jobs, before=fill_pads)

    rawv = raw.rearrange("p t (i h d) -> p t i h d", i=3, d=D16)
    NV = QT * 2 * H
    VW = QT * H * W
    nmin, root, small_c, small_s, big_c, big_s = (e.vbig[:, VW + i * NV:VW + (i + 1) * NV] for i in range(6))

    with stage(nc, "De", "dc", "ac", "wready", "rooted", "exped", "vals_in", "spiked", "spike_e") as (
            block, dc, ac, wready, rooted, exped, vals_in, spiked, spike_e):
        ones_tmp = e.rs[:, 0:NV]
        em = e.sm[:, 0:NV]
        ep = e.sm[:, NV:2 * NV]
        pick = e.sm[:, 2 * NV:3 * NV]

        @block.vector
        def _(dve):
            then = chained(dve, dc)
            for t in range(QT):
                then(dve.tensor_tensor_reduce(out=e.ob[:, 0:C], in0=xh[:, t, :], in1=e.w_sur[:, :], scale=1.0,
                                              scalar=0.0, op0=ALU.mult, op1=ALU.add, accum_out=imp[:, t:t + 1]))
            dve.tensor_scalar(imp, imp, e.scal[:, 0:1], None, ALU.add).then_inc(spiked, 1)
            for t in range(QT):
                dve.tensor_copy(V[:, t, :].rearrange("p (h w) -> p h w", w=W)[:, :, 0:D16], rawv[:, t, 2])
            sq = e.ob[:, 0:512]
            for t in range(QT):
                then(dve.tensor_tensor(sq, raw[:, t, 0:2 * C], raw[:, t, 0:2 * C], ALU.mult))
                sv = sq.rearrange("p (v d) -> p v d", d=D16)
                seg = nmin[:, t * 2 * H:(t + 1) * 2 * H]
                then(dve.tensor_reduce(seg, sv[:, :, 1:D16], AX.X, ALU.add))
                then(dve.tensor_tensor(seg, seg, sv[:, :, 0], ALU.subtract))
            then(dve.tensor_scalar(nmin, nmin, 1e-8, None, ALU.max))
            dve.sem_inc(wready, 1)
            then(dve.tensor_scalar(ones_tmp, nmin, 1.0, None, ALU.min))
            for dst, terms in ((small_c, (90.0, 56.0, 30.0, 12.0, 2.0)), (small_s, (110.0, 72.0, 42.0, 20.0, 6.0))):
                then(dve.tensor_scalar(dst, ones_tmp, 1.0 / terms[0], 1.0, ALU.mult, ALU.add))
                for c in terms[1:]:
                    then(dve.tensor_tensor(dst, dst, ones_tmp, ALU.mult))
                    then(dve.tensor_scalar(dst, dst, 1.0 / c, 1.0, ALU.mult, ALU.add))
            dve.wait_ge(exped, 2)
            then(dve.tensor_tensor(big_c, ep, em, ALU.add))
            then(dve.tensor_scalar(big_c, big_c, 0.5, None, ALU.mult))
            then(dve.tensor_tensor(big_s, ep, em, ALU.subtract))
            then(dve.reciprocal(em, root))
            then(dve.scalar_tensor_tensor(big_s, big_s, 0.5, em, ALU.mult, ALU.mult))
            then(dve.tensor_scalar(pick, nmin, 1.0, None, ALU.is_lt))
            for big, low in ((big_c, small_c), (big_s, small_s)):
                then(dve.copy_predicated(big, pick.bitcast(U32), low))
            for t in range(QT):
                for i in range(2):
                    seg = slice((2 * t + i) * H, (2 * t + i + 1) * H)
                    dst = qkp[i][:, t, :].rearrange("p (h w) -> p h w", w=D16)
                    dve.tensor_copy(dst[:, :, 0], big_c[:, seg])
                    sp_ = big_s[:, seg].unsqueeze(2).to_broadcast([P, H, D16 - 1])
                    if i == 0:
                        dve.tensor_tensor(dst[:, :, 1:D16], rawv[:, t, 0, :, 1:D16], sp_, ALU.mult)
                    else:
                        dve.scalar_tensor_tensor(dst[:, :, 1:D16], rawv[:, t, 1, :, 1:D16], -1.0, sp_,
                                                 ALU.mult, ALU.mult)
            dve.wait_ge(spike_e, 1)
            then(dve.tensor_scalar(spike, spike, 1.0, None, ALU.add))
            then(dve.reciprocal(spike, spike))
            dve.tensor_scalar(spike, spike, e.scal[:, 1:2], None, ALU.is_gt)

        @block.scalar
        def _(act):
            act.wait_ge(spiked, 1)
            act.activation(spike, imp, ACT.Exp, scale=-1.0).then_inc(spike_e, 1)
            act.wait_ge(wready, 1)
            act.activation(root, nmin, ACT.Sqrt).then_inc(rooted, 1)
            act.wait_ge(rooted, 1)
            act.activation(ep, root, ACT.Exp).then_inc(exped, 1)
            act.activation(em, root, ACT.Exp, scale=-1.0).then_inc(exped, 1)

    Q, K = e.view(0, H, 1, T), e.view(8192, H, 1, T)
    e.operands("Dt", [
        {"side": "q", "d": D16, "heads": H, "tiles": QT, "value": e.cT[:, 0, :], "stack": Q, "first": 0},
        {"side": "k", "d": D16, "heads": H, "tiles": QT, "value": e.xo[:, :, :].rearrange("p t n -> p (t n)"),
         "stack": K, "first": 0}], [])

    def least_distance(dve, then, m, tiny, tiny_back):
        mm, m1, m2 = e.mm[:, :], e.m1[:, :], e.m2[:, :]
        then(dve.tensor_scalar(m1, m, 1.0 + 1e-7, -1.0, ALU.max, ALU.add))
        dve.scalar_tensor_tensor(m2, m1, 2.0, m1, ALU.add, ALU.mult).then_inc(tiny, 1)
        dve.wait_ge(tiny_back, 2)
        dve.tensor_tensor(m1, m1, m2, ALU.add).then_inc(tiny, 1)
        dve.wait_ge(tiny_back, 3)
        then(dve.tensor_tensor(mm, m1, m1, ALU.mult))
    e.row_maxima("Dm", Q, K, T, True, op=ALU.min, dist=least_distance)

    steps = [(g, p, k) for g in range(HG) for p in range(2) for k in range(QT)]
    NS = len(steps)
    SCALE = -1.0 / D16 ** 0.5
    prob = e.prob
    tbuf = [r[:, i * 2 * T:(i + 1) * 2 * T].rearrange("p (a n) -> p a n", a=2)
            for r in (e.vbig[:, VW:2 * VW], e.parts2[:, :].bitcast(F32)) for i in range(2)]

    with stage(nc, "Da", "scored", "lows", "over", "wready", "rooted", "summed", "logged", "squared",
               "less", "exped", "masked", "weighed", "dc", "lifted", "gathered", "inverted", "spread_in",
               "divided") as (
            block, scored, lows, over, wready, rooted, summed, logged, squared, less, exped, masked,
            weighed, dc, lifted, gathered, inverted, spread_in, divided):
        @block.tensor
        def _(pe):
            def score(n):
                g, p, k = steps[n]
                q0 = k * P
                if n >= 2:
                    pe.wait_ge(over, n - 1)
                for jj in range(2):
                    hd = g * J + 2 * p + jj
                    last = pe.matmul(psum[:, 2 * (n % 2) + jj, q0:T], K[0:e.ROWS, hd, 0, q0:q0 + P],
                                     Q[0:e.ROWS, hd, 0, q0:T], start=True, stop=True)
                last.then_inc(scored, 1)

            def spread_lows(n):
                g, p, k = steps[n]
                if n:
                    pe.wait_ge(less, n)
                for jj in range(2):
                    hd = g * J + 2 * p + jj
                    last = pe.matmul(psum[:, 4 + jj, :], K[e.ROWS:P, hd, 0, 0:P], Q[e.ROWS:P, hd, 0, :],
                                     start=True, stop=True)
                last.then_inc(lows, 1)

            def weigh(n):
                g, p, k = steps[n]
                q0 = k * P
                pe.wait_ge(masked, n + 1)
                if g >= 2 and p == 0 and k == 0:
                    pe.wait_ge(divided, g - 1)
                for jj in range(2):
                    j = 2 * p + jj
                    last = pe.matmul(psum[W * j:W * j + W, 6 + g % 2, q0:T],
                                     V[:, k, g * P + W * j:g * P + W * j + W], prob[:, n % 4, jj, q0:T],
                                     start=(k == 0), stop=(k == QT - 1), skip_group_check=True)
                last.then_inc(weighed, 1)
                if n % (2 * QT) == 1 and g:
                    gather(g - 1)
                if n % (2 * QT) == 3 and g:
                    e.spread_inverses(pe, g - 1, inverted, spread_in)

            def gather(g):
                pe.wait_ge(lifted, g + 1)
                e.gather_sums(pe, g, gathered)

            for n in range(NS + 2):
                if n < NS:
                    score(n)
                if n >= 2:
                    m = n - 2
                    if steps[m][2] == 0:
                        spread_lows(m)
                    if m >= 1:
                        weigh(m - 1)
            weigh(NS - 1)
            gather(HG - 1)
            e.spread_inverses(pe, HG - 1, inverted, spread_in)

        @block.vector
        def _(dve):
            then = chained(dve, dc)

            def lift(g):
                dve.wait_ge(weighed, 2 * QT * (g + 1))
                dve.tensor_copy(e.ob[:, :], psum[:, 6 + g % 2, :]).then_inc(lifted, 1)

            def finish(g):
                e.divide(dve, then, g, spread_in, divided)

            def above_one(n):
                q0 = steps[n][2] * P
                dve.wait_ge(scored, n + 1)
                if n >= 4:
                    dve.wait_ge(exped, n - 3)
                    dve.wait_ge(weighed, n - 3)
                t_ = tbuf[n % 4][:, :, q0:T]
                dve.tensor_scalar(t_, psum[:, 2 * (n % 2):2 * (n % 2) + 2, q0:T], 1.0 + 1e-7, -1.0,
                                  ALU.max, ALU.add).then_inc(over, 1)
                dve.wait_ge(over, n + 1)
                dve.scalar_tensor_tensor(prob[:, n % 4, :, q0:T], t_, 2.0, t_, ALU.add, ALU.mult).then_inc(wready, 1)

            def add_root(n):
                q0 = steps[n][2] * P
                dve.wait_ge(rooted, 2 * (n + 1))
                t_ = tbuf[n % 4][:, :, q0:T]
                dve.tensor_tensor(t_, t_, prob[:, n % 4, :, q0:T], ALU.add).then_inc(summed, 1)

            def subtract_low(n):
                q0 = steps[n][2] * P
                dve.wait_ge(squared, n + 1)
                dve.wait_ge(lows, n // QT + 1)
                t_ = tbuf[n % 4][:, :, q0:T]
                dve.tensor_tensor(t_, t_, psum[:, 4:6, q0:T], ALU.subtract).then_inc(less, 1)

            done = inverse_at = 0
            for n in range(NS + 4):
                if n < NS:
                    above_one(n)
                if 1 <= n <= NS:
                    add_root(n - 1)
                if 2 <= n <= NS + 1:
                    subtract_low(n - 2)
                if n >= 4 + 2 * QT - 1 and (n - 4 - (2 * QT - 1)) % (2 * QT) == 0:
                    lift(done)
                    done += 1
                if n >= 6 + 2 * QT - 1 and (n - 6 - (2 * QT - 1)) % (2 * QT) == 0:
                    e.invert(dve, inverse_at, gathered, inverted)
                    inverse_at += 1
                if n >= 8 + 2 * QT - 1 and (n - 8 - (2 * QT - 1)) % (2 * QT) == 0:
                    finish(inverse_at - 1)
            e.invert(dve, HG - 1, gathered, inverted)
            finish(HG - 1)

        @block.scalar
        def _(act):
            act.preload_act_table_set("natural_log_exp_and_others")

            def root(n):
                q0 = steps[n][2] * P
                w_ = prob[:, n % 4, :, q0:T]
                act.wait_ge(wready, n + 1)
                act.activation(w_, w_, ACT.Ln).then_inc(rooted, 1)
                act.wait_ge(rooted, 2 * n + 1)
                act.activation(w_, w_, ACT.Exp, scale=0.5).then_inc(rooted, 1)

            def log(n):
                q0 = steps[n][2] * P
                t_ = tbuf[n % 4][:, :, q0:T]
                act.wait_ge(summed, n + 1)
                act.activation(t_, t_, ACT.Ln, bias=1.0).then_inc(logged, 1)

            def exponentiate(n):
                q0 = steps[n][2] * P
                act.wait_ge(less, n + 1)
                act.activation(prob[:, n % 4, :, q0:T], tbuf[n % 4][:, :, q0:T], ACT.Exp,
                               scale=SCALE).then_inc(exped, 1)

            for n in range(NS + 2):
                if n < NS:
                    root(n)
                if 1 <= n <= NS:
                    log(n - 1)
                if n >= 2:
                    exponentiate(n - 2)

        @block.gpsimd
        def _(pool):
            def square(n):
                q0 = steps[n][2] * P
                t_ = tbuf[n % 4][:, :, q0:T]
                pool.wait_ge(logged, n + 1)
                pool.tensor_tensor(t_, t_, t_, ALU.mult).then_inc(squared, 1)

            def cut(n):
                q0 = steps[n][2] * P
                d = prob[:, n % 4, :, q0:q0 + P]
                pool.wait_ge(exped, n + 1)
                pool.affine_select(d, d, [[0, 2], [1, P]], ALU.is_ge, 0.0, base=0,
                                   channel_multiplier=-1).then_inc(masked, 1)

            for n in range(NS + 1):
                if n < NS:
                    square(n)
                if n >= 1:
                    cut(n - 1)

    jobs = []
    for t in range(QT):
        pairs = [(e.yT[:, g, t * P:(t + 1) * P], e.wDo[:, g, :]) for g in range(HG)]

        def f(eng, bank, t=t):
            return eng.scalar_tensor_tensor(x[:, t, :], bank, spike[:, t:t + 1], x[:, t, :], ALU.mult, ALU.add)
        jobs.append(("dve", pairs, C, f))
    e.products("Do", jobs, before=e.add_rows(x, e.R["L1_attn_b_out"]))


def mixture(nc, es, dram, x5, out, psum, ident, nhalf):
    def sb(name, shape, dt=F32):
        return es.enter_context(nc.sbuf_tensor(name, shape, dt))

    NT = B * QT
    xs, xn = sb("xs", [P, NT, C]), sb("xn", [P, NT, C])
    xTall = sb("xTall", [P, KT, NT * P])
    hid = sb("hid", [P, 2, FT, T])
    w1, w2 = sb("ew1", [P, 2, KT, F]), sb("ew2", [P, 2, FT, C])
    b1c = sb("b1c", [P, NE, FT])
    b2s = sb("b2s", [NE, C])
    wg, bg = sb("wg", [P, KT, NE]), sb("bg", [P, NE])
    comb = sb("comb", [P, NT, NE])
    combT = sb("combT", [NE, NT * P])
    lg, ex, top = sb("lg", [P, NT, NE]), sb("ex", [P, NT, NE]), sb("top", [P, NT, NE])
    idx, idf = sb("idx", [P, NT, NE], U32), sb("idf", [P, NT, NE])
    iota, hot = sb("iota", [P, NE]), sb("hot", [P, NT, NE])
    col = sb("col", [P, 4, NT])
    stats, mv = sb("mstats", [P, NT, 6]), sb("mmv", [P, NT, 2])
    eps_var, rstd = sb("mev", [P, NT]), sb("mrstd", [P, NT])

    w_in = [es.enter_context(nc.semaphore(f"expert_weights_in{i}")) for i in range(2)]

    def load_expert(eng, i, ex_):
        one = slice(ex_, ex_ + 1) if isinstance(ex_, int) else bass.ds(ex_, 1)
        eng.dma_start(w1[:, i, :, :], dram["L1_ffn_W1"][one].rearrange("o (k p) n -> p (o k) n", p=P)).then_inc(w_in[i], 16)
        eng.dma_start(w2[:, i, :, :], dram["L1_ffn_W2"][one].rearrange("o (k p) n -> p (o k) n", p=P)).then_inc(w_in[i], 16)

    with stage(nc, "mi", "in_", "unused") as (block, in_, _u):
        @block.sync
        def _(sp):
            sp.dma_start(xs[:, :, :].rearrange("p (b t) c -> p b t c", b=B), x5.rearrange("b p t c -> p b t c")).then_inc(in_, 16)
            sp.dma_start(wg[:, :, :], dram["L1_ffn_Wg"].rearrange("(k p) n -> p k n", p=P)).then_inc(in_, 16)
            sp.dma_start(bg[:, :], dram["L1_ffn_bg"].partition_broadcast(P)).then_inc(in_, 16)
            sp.dma_start(b2s[:, :], dram["L1_ffn_b2"]).then_inc(in_, 16)
            for x_ in range(NE):
                sp.dma_start(b1c[:, x_, :], dram["L1_ffn_b1"][x_].rearrange("(f p) -> p f", p=P)).then_inc(in_, 16)
            sp.wait_ge(in_, 16 * (4 + NE))

        @block.scalar
        def _(act):
            for i in range(2):
                load_expert(act, i, i)

        @block.gpsimd
        def _(pool):
            pool.iota(idx[:, 0, :], [[1, NE]], base=0, channel_multiplier=0)

    with stage(nc, "mn", "dc", "var_ready", "rstd_ready", "normed", "turned", "copied", "gated", "logged") as (
            block, dc, var_ready, rstd_ready, normed, turned, copied, gated, logged):
        on_vector, on_pool = norm_stats(nc, "mn", xs, stats, mv, rstd, eps_var, nhalf, NT, (dc, var_ready, rstd_ready))

        @block.gpsimd
        def _(pool):
            on_pool(pool)

        @block.vector
        def _(dve):
            then = chained(dve, dc)
            dve.tensor_copy(iota[:, :], idx[:, 0, :])
            on_vector(dve, then)
            for t in range(NT):
                dve.tensor_scalar(xn[:, t, :], xs[:, t, :], mv[:, t, 0:1], rstd[:, t:t + 1],
                                  ALU.subtract, ALU.mult).then_inc(normed, 1)
            for t in range(NT):
                dve.wait_ge(gated, t + 1)
                dve.tensor_tensor(lg[:, t, :], psum[:, 6, t * NE:(t + 1) * NE], bg[:, :], ALU.add)

        @block.tensor
        def _(pe):
            for b in range(B):
                if b >= 2:
                    pe.wait_ge(copied, b - 1)
                for t in range(QT):
                    tt = b * QT + t
                    pe.wait_ge(normed, tt + 1)
                    for k in range(KT):
                        last = pe.transpose(psum[:, 2 * (b % 2) + k, t * P:(t + 1) * P],
                                            xn[:, tt, k * P:(k + 1) * P], ident[:, :])
                last.then_inc(turned, 1)
            for tt in range(NT):
                pe.wait_ge(copied, tt // QT + 1)
                for k in range(KT):
                    last = pe.matmul(psum[:, 6, tt * NE:(tt + 1) * NE], xTall[:, k, tt * P:(tt + 1) * P], wg[:, k, :],
                                     start=(tt == 0 and k == 0), stop=(k == KT - 1), skip_group_check=True)
                if tt == NT - 1:
                    last.then_inc(gated, NT)

        @block.scalar
        def _(act):
            for b in range(B):
                act.wait_ge(turned, b + 1)
                act.copy(xTall[:, :, b * T:(b + 1) * T], psum[:, 2 * (b % 2):2 * (b % 2) + 2, :]).then_inc(copied, 1)

    with stage(nc, "mg", "dc", "ready", "exped", "mixed", "turned", "crow", "biased") as (
            block, dc, ready, exped, mixed, turned, crow, biased):
        @block.vector
        def _(dve):
            then = chained(dve, dc)
            wide = [P, NT, NE]
            mxr, sm_ = col[:, 0, :], col[:, 1, :]
            then(dve.tensor_reduce(mxr, lg[:, :, :], AX.X, ALU.max))
            dve.tensor_tensor(lg[:, :, :], lg[:, :, :], mxr.unsqueeze(2).to_broadcast(wide), ALU.subtract).then_inc(ready, 1)
            dve.wait_ge(exped, 1)
            then(dve.tensor_reduce(sm_, ex[:, :, :], AX.X, ALU.add))
            then(dve.reciprocal(sm_, sm_))
            then(dve.tensor_tensor(ex[:, :, :], ex[:, :, :], sm_.unsqueeze(2).to_broadcast(wide), ALU.mult))
            for t in range(NT):
                ins = dve.max(top[:, t, :], ex[:, t, :])
            then(ins)
            for t in range(NT):
                ins = dve.max_index(idx[:, t, :], top[:, t, :], ex[:, t, :])
            then(ins)
            then(dve.tensor_copy(idf[:, :, :], idx[:, :, :]))
            then(dve.tensor_tensor(mxr, top[:, :, 0], top[:, :, 1], ALU.add))
            then(dve.tensor_scalar(mxr, mxr, 1e-8, None, ALU.add))
            then(dve.reciprocal(mxr, mxr))
            for i in range(2):
                then(dve.tensor_tensor(col[:, 2 + i, :], top[:, :, i], mxr, ALU.mult))
                dst = comb if i == 0 else hot
                then(dve.tensor_tensor(dst[:, :, :], iota[:, :].unsqueeze(1).to_broadcast(wide),
                                       idf[:, :, i].unsqueeze(2).to_broadcast(wide), ALU.is_equal))
                then(dve.tensor_tensor(dst[:, :, :], dst[:, :, :], col[:, 2 + i, :].unsqueeze(2).to_broadcast(wide), ALU.mult))
            then(dve.tensor_tensor(comb[:, :, :], comb[:, :, :], hot[:, :, :], ALU.add))
            dve.sem_inc(mixed, 1)
            for t in range(NT):
                dve.wait_ge(biased, t + 1)
                dve.tensor_tensor(xs[:, t, :], psum[:, 4 + t % 4, 0:C], xs[:, t, :], ALU.add).then_inc(crow, 1)

        @block.scalar
        def _(act):
            act.wait_ge(ready, 1)
            act.activation(ex[:, :, :], lg[:, :, :], ACT.Exp).then_inc(exped, 1)
            for i in range(4):
                act.wait_ge(turned, i + 1)
                act.copy(combT[:, i * T:(i + 1) * T], psum[0:NE, i, :]).then_inc(exped, 1)

        @block.tensor
        def _(pe):
            pe.wait_ge(mixed, 1)
            for i in range(4):
                for t in range(QT):
                    last = pe.transpose(psum[0:NE, i, t * P:(t + 1) * P], comb[:, i * QT + t, :], ident[:, :])
                last.then_inc(turned, 1)
            for t in range(NT):
                pe.wait_ge(exped, 2 + t // QT)
                if t >= 4:
                    pe.wait_ge(crow, t - 3)
                pe.matmul(psum[:, 4 + t % 4, 0:C], combT[:, t * P:(t + 1) * P], b2s[:, :], start=True,
                          stop=True).then_inc(biased, 1)

    def expert_pair(e0, prefetch):
        with stage(nc, "ex" if prefetch else "el", "up", "acted", "down", "added", "dc") as (block, up, acted, down, added, dc):
            units = [(i, b) for i in range(2) for b in range(B)]

            @block.tensor
            def _(pe):
                def rise(u):
                    i, b = units[u]
                    if b == 0:
                        pe.wait_ge(w_in[i], 32)
                    for f in range(FT):
                        m = u * FT + f
                        if m >= 4:
                            pe.wait_ge(acted, m - 3)
                        for k in range(KT):
                            last = pe.matmul(psum[:, m % 4, :], w1[:, i, k, f * P:(f + 1) * P],
                                             xTall[:, k, b * T:(b + 1) * T], start=(k == 0), stop=(k == KT - 1))
                        last.then_inc(up, 1)

                def fall(u):
                    i, b = units[u]
                    pe.wait_ge(acted, FT * (u + 1))
                    for t in range(QT):
                        m = u * QT + t
                        if m >= 4:
                            pe.wait_ge(added, m - 3)
                        for f in range(FT):
                            last = pe.matmul(psum[:, 4 + m % 4, 0:C], hid[:, u % 2, f, t * P:(t + 1) * P],
                                             w2[:, i, f, :], start=(f == 0), stop=(f == FT - 1))
                        last.then_inc(down, 1)

                rise(0)
                for u in range(len(units)):
                    if u + 1 < len(units):
                        rise(u + 1)
                    fall(u)

            @block.scalar
            def _(act):
                for u, (i, b) in enumerate(units):
                    for f in range(FT):
                        m = u * FT + f
                        act.wait_ge(up, m + 1)
                        if u >= 2 and f == 0:
                            act.wait_ge(down, QT * (u - 1))
                        bias = b1c[:, bass.ds(e0 + i, 1), f:f + 1].rearrange("p a b -> p (a b)")
                        act.activation(hid[:, u % 2, f, :], psum[:, m % 4, :], ACT.Gelu_apprx_tanh,
                                       bias=bias).then_inc(acted, 1)

            @block.vector
            def _(dve):
                for u, (i, b) in enumerate(units):
                    for t in range(QT):
                        m, tt = u * QT + t, b * QT + t
                        dve.wait_ge(down, m + 1)
                        if i:
                            dve.wait_ge(added, b * QT + t + 1)
                        c_ = comb[:, tt, bass.ds(e0 + i, 1)]
                        dve.scalar_tensor_tensor(xs[:, tt, :], psum[:, 4 + m % 4, 0:C], c_, xs[:, tt, :],
                                                 ALU.mult, ALU.add).then_inc(added, 1)

            if prefetch:
                @block.sync
                def _(sp):
                    for i in range(2):
                        sp.wait_ge(down, B * QT * (i + 1))
                        sp.sem_clear(w_in[i])
                        load_expert(sp, i, e0 + 2 + i)

    with nc.Fori(0, NE // 2 - 1) as pair:
        expert_pair(pair * 2, True)
    expert_pair(NE - 2, False)

    with stage(nc, "mo", "stored", "unused") as (block, stored, _u):
        @block.sync
        def _(sp):
            ov = out.rearrange("b (t p) c -> p (b t) c", p=P)
            sp.dma_start(ov, xs[:, :, :]).then_inc(stored, 16)
            sp.wait_ge(stored, 16)


SCALARS = ("L1_attn_b_sur", "L1_attn_threshold")


def kernel(**inputs):
    import numpy as _np
    import concourse.bacc as _bacc
    from concourse.bass_utils import run_bass_kernel_spmd as _run

    nc = _bacc.Bacc("TRN2", target_bir_lowering=False, num_devices=1)
    arrays, dram = {}, {}
    for name, a in inputs.items():
        a = _np.ascontiguousarray(a)
        if name in SCALARS:
            a = a.reshape(1)
        arrays[f"in_{name}"] = a
        dram[name] = nc.dram_tensor(f"in_{name}", a.shape, mybir.dt.from_np(a.dtype), kind="ExternalInput").ap()
    out = nc.dram_tensor("out_0", (B, T, C), F32, kind="ExternalOutput").ap()
    build(nc, dram, out)
    r = _run(nc, [arrays], core_ids=[0])
    return r.results[0]["out_0"]
```
